# Optimizing a Trainium2 kernel written in Bass

```python
import numpy as np
import jax
import jax.numpy as jnp

def _softmax(x, axis=-1):
    return jax.nn.softmax(x, axis=axis)

def _gelu(x):
    return jax.nn.gelu(x, approximate=True)

def _silu(x):
    return jax.nn.silu(x)

def _sigmoid(x):
    return jax.nn.sigmoid(x)

def _layernorm(x, axis=-1, eps=1e-05):
    m = jnp.mean(x, axis=axis, keepdims=True)
    v = jnp.var(x, axis=axis, keepdims=True)
    return (x - m) / jnp.sqrt(v + eps)

def _scatter_add(tgt, idx, src, axis=0):
    return tgt.at[idx].add(src)

def _segment_sum(src, seg, n):
    return jax.ops.segment_sum(src, seg, n)
kernel_name = 'mk_gps_d1_gnn_r8_b77f11'

def setup_inputs(seed: int=0):
    np.random.seed(seed)
    _w = jnp.asarray

    def _rec_inputs():
        import jax
        import jax.numpy as jnp
        _gk = jax.random.key(seed)
        x = -0.0001126 + 1 * jax.random.normal(jax.random.fold_in(_gk, 1), (1250, 768), jnp.float32)
        _s = jax.random.randint(jax.random.fold_in(_gk, 2), (20000,), 0, 1250, jnp.int32)
        _d = jax.random.randint(jax.random.fold_in(_gk, 3), (20000,), 0, 1250, jnp.int32)
        _loop = jnp.arange(1250, dtype=jnp.int32)
        src = jnp.concatenate([_s, _d, _loop])
        dst = jnp.concatenate([_d, _s, _loop])
        _o = jnp.argsort(dst, stable=True)
        src = src[_o]
        dst = dst[_o]
        return (x, src, dst)
    x, src, dst = _rec_inputs()

    def _L0_gnn_setup():
        import jax, jax.numpy as jnp
        import numpy as np
        N_NODES = 1250
        N_EDGES = 20000
        NEG_SLOPE = 0.2

        def _gat_layer(x, src, dst, W, a_src, a_dst, bias, concat):
            N = x.shape[0]
            H, C = a_src.shape
            h = (x @ W).reshape(N, H, C)
            al_s = jnp.einsum('nhc,hc->nh', h, a_src)
            al_d = jnp.einsum('nhc,hc->nh', h, a_dst)
            e = jax.nn.leaky_relu(al_s[src] + al_d[dst], NEG_SLOPE)
            m = jax.ops.segment_max(e, dst, num_segments=N)
            ex = jnp.exp(e - m[dst])
            denom = jax.ops.segment_sum(ex, dst, num_segments=N)
            alpha = ex / (denom[dst] + 1e-16)
            msg = h[src] * alpha[:, :, None]
            out = jax.ops.segment_sum(msg, dst, num_segments=N)
            out = out.reshape(N, H * C) if concat else out.mean(axis=1)
            return out + bias
        key = jax.random.key(seed)
        ks = jax.random.split(key, 10)
        in_dim, hid, out_dim, heads = (768, 512, 768, 4)
        x = jax.random.normal(ks[0], (N_NODES, in_dim), dtype=jnp.float32)
        edge_index = jax.random.randint(ks[1], (2, N_EDGES), 0, N_NODES, dtype=jnp.int64)
        g = lambda k, shape, fan: jax.random.normal(k, shape, jnp.float32) / np.sqrt(fan)
        return {'x': x, 'edge_index': edge_index, 'W1': g(ks[2], (in_dim, heads * hid), in_dim), 'att_src1': g(ks[3], (heads, hid), hid), 'att_dst1': g(ks[4], (heads, hid), hid), 'b1': jnp.zeros((heads * hid,), jnp.float32), 'W2': g(ks[5], (heads * hid, out_dim), heads * hid), 'att_src2': g(ks[6], (1, out_dim), out_dim), 'att_dst2': g(ks[7], (1, out_dim), out_dim), 'b2': jnp.zeros((out_dim,), jnp.float32)}
    _L0_gnn_all = _L0_gnn_setup()
    _L0_gnn_in = {k: v for k, v in _L0_gnn_all.items() if k in ('W1', 'att_src1', 'att_dst1', 'b1', 'W2', 'att_src2', 'att_dst2', 'b2')}
    del _L0_gnn_all

    def _L0_mix_setup():
        import jax, jax.numpy as jnp
        import numpy as np
        EMBED_DIM = 768
        NUM_HEADS = 8
        HEAD_DIM = EMBED_DIM // NUM_HEADS
        NUM_RF = 256
        B, N = (8, 512)
        key = jax.random.key(seed)
        ks = jax.random.split(key, 6)
        x = jax.random.normal(ks[0], (B, N, EMBED_DIM), dtype=jnp.float32)
        s_qkv = 1.0 / np.sqrt(EMBED_DIM)
        qkv_w = jax.random.uniform(ks[1], (3 * EMBED_DIM, EMBED_DIM), minval=-s_qkv, maxval=s_qkv)
        qkv_b = jax.random.uniform(ks[2], (3 * EMBED_DIM,), minval=-s_qkv, maxval=s_qkv)
        proj_w = jax.random.uniform(ks[3], (EMBED_DIM, EMBED_DIM), minval=-s_qkv, maxval=s_qkv)
        proj_b = jax.random.uniform(ks[4], (EMBED_DIM,), minval=-s_qkv, maxval=s_qkv)
        rf = jax.random.normal(ks[5], (NUM_RF, HEAD_DIM), dtype=jnp.float32)
        rf = rf / jnp.linalg.norm(rf, axis=1, keepdims=True)
        return {'x': x, 'qkv_w': qkv_w, 'qkv_b': qkv_b, 'proj_w': proj_w, 'proj_b': proj_b, 'rf': rf}
    _L0_mix_all = _L0_mix_setup()
    _L0_mix_in = {k: v for k, v in _L0_mix_all.items() if k in ('qkv_w', 'qkv_b', 'proj_w', 'proj_b', 'rf')}
    del _L0_mix_all

    def _L0_ffn_setup():
        import jax, jax.numpy as jnp
        import numpy as np
        G, E = (4, 8)
        KG, KE = (2, 2)
        D, M = (768, 384)
        SCALE = 0.02

        def _combine_weights(xf, Wg, bg, Wge, bge):
            N = xf.shape[0]
            glog = xf @ Wg + bg
            gtop, gidx = jax.lax.top_k(glog, KG)
            ggate = jax.nn.softmax(gtop, axis=-1)
            elog_all = jnp.einsum('nd,gde->nge', xf, Wge) + bge
            elog = jnp.take_along_axis(elog_all, gidx[:, :, None], axis=1)
            etop, eidx = jax.lax.top_k(elog, KE)
            egate = jax.nn.softmax(etop, axis=-1)
            w = ggate[:, :, None] * egate
            flat = gidx[:, :, None] * E + eidx
            comb = jnp.zeros((N, G * E), xf.dtype).at[jnp.arange(N)[:, None, None], flat].add(w)
            return comb
        key = jax.random.key(seed)
        ks = jax.random.split(key, 8)
        x = jax.random.normal(ks[0], (1, 512, D), jnp.float32)
        Wg = jax.random.normal(ks[1], (D, G), jnp.float32) * SCALE
        bg = jnp.zeros((G,), jnp.float32)
        Wge = jax.random.normal(ks[2], (G, D, E), jnp.float32) * SCALE
        bge = jnp.zeros((G, E), jnp.float32)
        W1 = jax.random.normal(ks[3], (G * E, D, M), jnp.float32) * SCALE
        b1 = jnp.zeros((G * E, M), jnp.float32)
        W2 = jax.random.normal(ks[4], (G * E, M, D), jnp.float32) * SCALE
        b2 = jnp.zeros((G * E, D), jnp.float32)
        return {'x': x, 'Wg': Wg, 'bg': bg, 'Wge': Wge, 'bge': bge, 'W1': W1, 'b1': b1, 'W2': W2, 'b2': b2}
    _L0_ffn_all = _L0_ffn_setup()
    _L0_ffn_in = {k: v for k, v in _L0_ffn_all.items() if k in ('Wg', 'bg', 'Wge', 'bge', 'W1', 'b1', 'W2', 'b2')}
    del _L0_ffn_all
    return {'x': x, 'src': src, 'dst': dst, 'L0_gnn_W1': _L0_gnn_in['W1'], 'L0_gnn_att_src1': _L0_gnn_in['att_src1'], 'L0_gnn_att_dst1': _L0_gnn_in['att_dst1'], 'L0_gnn_b1': _L0_gnn_in['b1'], 'L0_gnn_W2': _L0_gnn_in['W2'], 'L0_gnn_att_src2': _L0_gnn_in['att_src2'], 'L0_gnn_att_dst2': _L0_gnn_in['att_dst2'], 'L0_gnn_b2': _L0_gnn_in['b2'], 'L0_mix_qkv_w': _L0_mix_in['qkv_w'], 'L0_mix_qkv_b': _L0_mix_in['qkv_b'], 'L0_mix_proj_w': _L0_mix_in['proj_w'], 'L0_mix_proj_b': _L0_mix_in['proj_b'], 'L0_mix_rf': _L0_mix_in['rf'], 'L0_ffn_Wg': _L0_ffn_in['Wg'], 'L0_ffn_bg': _L0_ffn_in['bg'], 'L0_ffn_Wge': _L0_ffn_in['Wge'], 'L0_ffn_bge': _L0_ffn_in['bge'], 'L0_ffn_W1': _L0_ffn_in['W1'], 'L0_ffn_b1': _L0_ffn_in['b1'], 'L0_ffn_W2': _L0_ffn_in['W2'], 'L0_ffn_b2': _L0_ffn_in['b2']}

def reference(x, src, dst, L0_gnn_W1, L0_gnn_att_src1, L0_gnn_att_dst1, L0_gnn_b1, L0_gnn_W2, L0_gnn_att_src2, L0_gnn_att_dst2, L0_gnn_b2, L0_mix_qkv_w, L0_mix_qkv_b, L0_mix_proj_w, L0_mix_proj_b, L0_mix_rf, L0_ffn_Wg, L0_ffn_bg, L0_ffn_Wge, L0_ffn_bge, L0_ffn_W1, L0_ffn_b1, L0_ffn_W2, L0_ffn_b2):
    import jax
    import jax.numpy as jnp

    def _L0_gnn_ref(x, edge_index, W1, att_src1, att_dst1, b1, W2, att_src2, att_dst2, b2):
        import jax, jax.numpy as jnp
        import numpy as np
        N_NODES = 1250
        N_EDGES = 20000
        NEG_SLOPE = 0.2

        def _gat_layer(x, src, dst, W, a_src, a_dst, bias, concat):
            N = x.shape[0]
            H, C = a_src.shape
            h = (x @ W).reshape(N, H, C)
            al_s = jnp.einsum('nhc,hc->nh', h, a_src)
            al_d = jnp.einsum('nhc,hc->nh', h, a_dst)
            e = jax.nn.leaky_relu(al_s[src] + al_d[dst], NEG_SLOPE)
            m = jax.ops.segment_max(e, dst, num_segments=N)
            ex = jnp.exp(e - m[dst])
            denom = jax.ops.segment_sum(ex, dst, num_segments=N)
            alpha = ex / (denom[dst] + 1e-16)
            msg = h[src] * alpha[:, :, None]
            out = jax.ops.segment_sum(msg, dst, num_segments=N)
            out = out.reshape(N, H * C) if concat else out.mean(axis=1)
            return out + bias
        N = x.shape[0]
        loops = jnp.arange(N, dtype=edge_index.dtype)
        src = jnp.concatenate([edge_index[0], loops])
        dst = jnp.concatenate([edge_index[1], loops])
        h = jax.nn.elu(_gat_layer(x, src, dst, W1, att_src1, att_dst1, b1, concat=True))
        out = _gat_layer(h, src, dst, W2, att_src2, att_dst2, b2, concat=False)
        return out

    def _L0_mix_ref(x, qkv_w, qkv_b, proj_w, proj_b, rf):
        import jax, jax.numpy as jnp
        import numpy as np
        EMBED_DIM = 768
        NUM_HEADS = 8
        HEAD_DIM = EMBED_DIM // NUM_HEADS
        NUM_RF = 256
        B, N = (8, 512)
        Bn, Nn, C = x.shape
        H, D = (NUM_HEADS, HEAD_DIM)
        qkv = x @ qkv_w.T + qkv_b
        qkv = qkv.reshape(Bn, Nn, 3, H, D).transpose(2, 0, 3, 1, 4)
        q, k, v = (qkv[0], qkv[1], qkv[2])
        scale = D ** (-0.5)
        q = q * scale
        k = k * scale
        q_norm = jnp.sum(q * q, axis=-1, keepdims=True) * 0.5
        k_norm = jnp.sum(k * k, axis=-1, keepdims=True) * 0.5
        phi_q = jnp.exp(jnp.einsum('bhnd,md->bhnm', q, rf) - q_norm)
        phi_k = jnp.exp(jnp.einsum('bhnd,md->bhnm', k, rf) - k_norm)
        kv = jnp.einsum('bhnm,bhnd->bhmd', phi_k, v)
        numerator = jnp.einsum('bhnm,bhmd->bhnd', phi_q, kv)
        k_sum = jnp.sum(phi_k, axis=2)
        denominator = jnp.einsum('bhnm,bhm->bhn', phi_q, k_sum)[..., None]
        attn = numerator / jnp.maximum(denominator, 1e-06)
        out = attn.transpose(0, 2, 1, 3).reshape(Bn, Nn, C)
        return out @ proj_w.T + proj_b

    def _L0_ffn_ref(x, Wg, bg, Wge, bge, W1, b1, W2, b2):
        import jax, jax.numpy as jnp
        import numpy as np
        G, E = (4, 8)
        KG, KE = (2, 2)
        D, M = (768, 384)
        SCALE = 0.02

        def _combine_weights(xf, Wg, bg, Wge, bge):
            N = xf.shape[0]
            glog = xf @ Wg + bg
            gtop, gidx = jax.lax.top_k(glog, KG)
            ggate = jax.nn.softmax(gtop, axis=-1)
            elog_all = jnp.einsum('nd,gde->nge', xf, Wge) + bge
            elog = jnp.take_along_axis(elog_all, gidx[:, :, None], axis=1)
            etop, eidx = jax.lax.top_k(elog, KE)
            egate = jax.nn.softmax(etop, axis=-1)
            w = ggate[:, :, None] * egate
            flat = gidx[:, :, None] * E + eidx
            comb = jnp.zeros((N, G * E), xf.dtype).at[jnp.arange(N)[:, None, None], flat].add(w)
            return comb
        shp = x.shape
        xf = x.reshape(-1, D)
        comb = _combine_weights(xf, Wg, bg, Wge, bge)
        h = jax.nn.gelu(jnp.einsum('nd,edm->nem', xf, W1) + b1, approximate=False)
        y = jnp.einsum('nem,emd->ned', h, W2) + b2
        out = jnp.einsum('ne,ned->nd', comb, y)
        return out.reshape(shp)
    edge_index = jnp.stack([src, dst])
    xn = _layernorm(x, axis=-1)
    x = x + _L0_gnn_ref(xn, edge_index, L0_gnn_W1, L0_gnn_att_src1, L0_gnn_att_dst1, L0_gnn_b1, L0_gnn_W2, L0_gnn_att_src2, L0_gnn_att_dst2, L0_gnn_b2) + _L0_mix_ref(xn[None], L0_mix_qkv_w, L0_mix_qkv_b, L0_mix_proj_w, L0_mix_proj_b, L0_mix_rf)[0]
    x = x + _L0_ffn_ref(_layernorm(x, axis=-1)[None], L0_ffn_Wg, L0_ffn_bg, L0_ffn_Wge, L0_ffn_bge, L0_ffn_W1, L0_ffn_b1, L0_ffn_W2, L0_ffn_b2)[0]
    return x

_drawn_inputs = setup_inputs


def setup_inputs(seed=0):
    import zlib

    import numpy as np

    out = dict(_drawn_inputs(seed))
    spreads = {'L0_gnn_b1': (0.0, 0.1),
     'L0_gnn_b2': (0.0, 0.1),
     'L0_ffn_bg': (0.0, 0.773),
     'L0_ffn_bge': (0.0, 0.1),
     'L0_ffn_b1': (0.0, 0.647),
     'L0_ffn_b2': (0.0, 0.1)}
    factors = {'L0_gnn_att_dst1': 5.315,
     'L0_gnn_att_src2': 5.084,
     'L0_gnn_att_dst2': 24.023,
     'L0_mix_qkv_w': 4.369,
     'L0_mix_qkv_b': 3.76,
     'L0_mix_proj_w': 3.14,
     'L0_mix_rf': 8.0}
    for name, (base, spread) in spreads.items():
        noise = np.random.default_rng([zlib.crc32(name.encode()), seed]).standard_normal(out[name].shape)
        drawn = base * np.exp(spread * noise) if base else spread * noise
        out[name] = jnp.asarray(drawn.astype(out[name].dtype))
    for name, factor in factors.items():
        out[name] = (out[name] * factor).astype(out[name].dtype)
    return out
```

```python
from contextlib import ExitStack

import concourse.bass as bass
from concourse import mybir

F32 = mybir.dt.float32
F16 = mybir.dt.float16
BF16 = mybir.dt.bfloat16
I32 = mybir.dt.int32
U32 = mybir.dt.uint32
ALU = mybir.AluOpType
ACT = mybir.ActivationFunctionType
AX = mybir.AxisListType

N = 1250
NT = 10
P = N // NT
D = 768
KD = D // 128
H1 = 4
C1 = 512
F1 = H1 * C1
KF = F1 // 128
CH = 3
CHW = [416, 416, 418]
CHO = [0, 416, 832]
EDGES = 41250
ER = 128
EROWS = 324
EG = 3
EGP = EROWS // EG
WIN = 32
NW = 40
SPLIT = 4
SLO = 314
CTW = SPLIT * SLO
PADNODE = NW * WIN - 1
BIG = 1.0e30
MH = 8
MD = D // MH
RF = 256
NE = 32
NG = 4
EPG = NE // NG
FM = 384
KM = FM // 128
SLOT = 128
MAXT = (4 * N + NE * (SLOT - 1)) // SLOT + NE // 4
SLOPE = 0.2
EPS = 1e-5


class Chain:

    def __init__(self, eng, sem):
        self.eng, self.sem, self.base, self.i, self.per, self.j = eng, sem, 0, 0, 0, 0

    def start(self, i, per):
        self.i, self.per, self.j = i, per, 0

    def end(self, count):
        assert self.j == self.per, (self.j, self.per)
        self.base += count * self.per
        self.i, self.per, self.j = 0, 0, 0

    def __call__(self, ins):
        self.j += 1
        ins.then_inc(self.sem, 1)
        self.eng.wait_ge(self.sem, self.i * self.per + (self.base + self.j))

    def flat_end(self):
        self.base += self.j
        self.j = 0


class Ctx:

    def __init__(self, nc):
        self.nc, self.sems = nc, []

    def sem(self, name):
        self.sems.append(self.nc.alloc_semaphore(name=name))
        return self.sems[-1]

    def clear(self):
        self.nc.clear_and_free_semaphores(self.sems)
        self.sems = []
        with self.nc.Block():
            pass


def sb(nc, st, name, shape, dt=F32):
    return st.enter_context(nc.sbuf_tensor(name, shape, dt))


def pb(nc, st, name, shape, dt=F32):
    return st.enter_context(nc.psum_tensor(name, shape, dt))


def refine_rstd(step, dve, rstd, std, veps, tmp):
    step(dve.reciprocal(rstd, std))
    step(dve.tensor_tensor(tmp, rstd, rstd, ALU.mult))
    step(dve.tensor_tensor(tmp, tmp, veps, ALU.mult))
    step(dve.tensor_scalar(tmp, tmp, -0.5, 1.5, ALU.mult, ALU.add))
    step(dve.tensor_tensor(rstd, rstd, tmp, ALU.mult))


def norm_phase(nc, cx, x, ident, xnT):
    x_loaded, stats_done, sqrt_done, xn_ready, transposed, used_dve, used_act, id_done = (
        cx.sem(f"norm_{s}") for s in
        ("x_loaded", "stats_done", "sqrt_done", "xn_ready", "transposed", "used_dve", "used_act", "id_done"))
    dve_step = cx.sem("norm_dve_step")
    with ExitStack() as st:
        xa = sb(nc, st, "xa", [P, NT, D])
        stats = sb(nc, st, "stats", [P, NT, 2, 6])
        mv = sb(nc, st, "mv", [P, NT, 2])
        std = sb(nc, st, "std", [P, NT])
        veps = sb(nc, st, "veps", [P, NT])
        tmp = sb(nc, st, "tmp", [P, NT])
        rstd = sb(nc, st, "rstd", [P, NT])
        xn = [sb(nc, st, f"xn{b}", [P, D]) for b in range(2)]
        tp = [[pb(nc, st, f"tp{b}{h}", [128, 3, P]) for h in range(2)] for b in range(2)]
        block = st.enter_context(nc.Block())

        @block.sync
        def _(sp):
            sp.dma_start(xa[:], x.rearrange("(t p) d -> p t d", p=P)).then_inc(x_loaded, 16)

        @block.gpsimd
        def _(pool):
            pool.memset(ident[:], 0.0).then_inc(id_done, 1)
            pool.wait_ge(id_done, 1)
            pool.affine_select(out=ident[:], in_=ident[:], compare_op=ALU.not_equal, fill=1.0, base=0,
                               pattern=[[-1, 128]], channel_multiplier=1).then_inc(id_done, 1)

        @block.vector
        def _(dve):
            step = Chain(dve, dve_step)
            dve.wait_ge(x_loaded, 16)
            for t in range(NT):
                for h in range(2):
                    last = dve.bn_stats(stats[:, t, h, :], xa[:, t, h * 384:(h + 1) * 384])
            step(last)
            for t in range(NT):
                last = dve.bn_aggr(mv[:, t, :], stats[:, t, :, :])
            step(last)
            dve.tensor_scalar(veps[:], mv[:, :, 1], EPS, None, ALU.add).then_inc(stats_done, 1)
            dve.wait_ge(sqrt_done, 1)
            refine_rstd(step, dve, rstd[:], std[:], veps[:], tmp[:])
            step.flat_end()
            with dve.Fori(0, NT // 2) as i:
                for b in range(2):
                    dve.wait_ge(transposed, i * 2 + (b + 1))
                    dve.tensor_scalar(xn[b][:], xa[:, bass.ds(i * 2 + b, 1), :],
                                      mv[:, bass.ds(i * 2 + b, 1), 0], rstd[:, bass.ds(i * 2 + b, 1)],
                                      ALU.subtract, ALU.mult).then_inc(xn_ready, 1)
                    dve.wait_ge(transposed, i * 2 + (b + 3))
                    dve.tensor_copy(xnT[:, 0:3, bass.ds(i * (2 * P) + b * P, P)], tp[b][0][:]).then_inc(used_dve, 1)

        @block.scalar
        def _(act):
            act.wait_ge(stats_done, 1)
            act.activation(std[:], veps[:], ACT.Sqrt).then_inc(sqrt_done, 1)
            with act.Fori(0, NT // 2) as i:
                for b in range(2):
                    act.wait_ge(transposed, i * 2 + (b + 3))
                    act.activation(xnT[:, 3:6, bass.ds(i * (2 * P) + b * P, P)], tp[b][1][:],
                                   ACT.Copy).then_inc(used_act, 1)

        @block.tensor
        def _(pe):
            pe.sem_inc(transposed, 2)
            pe.sem_inc(used_dve, 2)
            pe.sem_inc(used_act, 2)
            pe.wait_ge(id_done, 2)
            with pe.Fori(0, NT // 2) as i:
                for b in range(2):
                    pe.wait_ge(xn_ready, i * 2 + (b + 1))
                    pe.wait_ge(used_dve, i * 2 + (b + 1))
                    pe.wait_ge(used_act, i * 2 + (b + 1))
                    for k in range(KD):
                        last = pe.transpose(tp[b][k // 3][:, k % 3, :], xn[b][:, k * 128:(k + 1) * 128],
                                            ident[0:P, 0:P])
                    last.then_inc(transposed, 1)


def numerator(nc, cx, tag, half, rfT, qT, kv, attn):
    HH, A, HT = MH // 2, MD + 1, NT // 2
    feat, exped, num, num_used = (cx.sem(tag + s) for s in ("feat", "exped", "num", "num_used"))
    dve_step = cx.sem(tag + "num_step")
    with ExitStack() as st:
        phiq = [sb(nc, st, tag + f"phiq{b}", [128, 2, N]) for b in range(2)]
        den = sb(nc, st, tag + "den", [P, 2, HT])
        F = [pb(nc, st, tag + f"F{j}", [128, 512]) for j in range(6)]
        R = [pb(nc, st, tag + f"R{j}", [P, HT, A]) for j in range(2)]
        block = st.enter_context(nc.Block())

        @block.tensor
        def _(pe):
            pe.sem_inc(num, 4)
            with pe.Fori(0, HH // 2) as i:
                for b in range(2):
                    for j in range(6):
                        m, c = j // CH, j % CH
                        pe.wait_ge(exped, i * 12 + (6 * b + j + 1))
                        pe.matmul(F[j][:, 0:CHW[c]], rfT[:, m * 128:(m + 1) * 128],
                                  qT[:, bass.ds(i * 2 + b, 1), CHO[c]:CHO[c] + CHW[c]],
                                  start=True, stop=True).then_inc(feat, 1)
                for b in range(2):
                    pe.wait_ge(exped, i * 12 + (6 * b + 12))
                    for j in range(2):
                        pe.wait_ge(num_used, i * 4 + (2 * b + j + 1))
                        for t in range(HT):
                            tt = j * HT + t
                            for m in range(2):
                                last = pe.matmul(R[j][:, t, :], phiq[b][:, m, tt * P:(tt + 1) * P],
                                                 kv[:, bass.ds(i * 2 + b, 1), m, :], start=(m == 0), stop=(m == 1),
                                                 skip_group_check=True)
                        last.then_inc(num, 1)

        @block.scalar
        def _(act):
            act.sem_inc(exped, 6)
            with act.Fori(0, HH // 2) as i:
                for b in range(2):
                    act.wait_ge(num, i * 4 + (2 * b + 2))
                    for j in range(6):
                        m, c = j // CH, j % CH
                        act.wait_ge(feat, i * 12 + (6 * b + j + 1))
                        act.activation(phiq[b][:, m, CHO[c]:CHO[c] + CHW[c]], F[j][:, 0:CHW[c]],
                                       ACT.Exp).then_inc(exped, 1)

        @block.vector
        def _(dve):
            step = Chain(dve, dve_step)
            dve.sem_inc(num_used, 2)
            with dve.Fori(0, HH // 2) as i:
                step.start(i, 8)
                for b in range(2):
                    for j in range(2):
                        dve.wait_ge(num, i * 4 + (2 * b + j + 5))
                        dve.wait_ge(num_used, i * 4 + (2 * b + j + 1))
                        step(dve.tensor_scalar(den[:, j, :], R[j][:, :, MD], 1e-6, None, ALU.max))
                        step(dve.reciprocal(den[:, j, :], den[:, j, :]))
                        dve.tensor_tensor(attn[:, j * HT:(j + 1) * HT, bass.ds((i * 2 + b) * MD + half * HH * MD, MD)],
                                          R[j][:, :, 0:MD], den[:, j, :].unsqueeze(2).to_broadcast([P, HT, MD]),
                                          ALU.mult).then_inc(num_used, 1)
            step.end(HH // 2)


def proj_phase(nc, cx, attn, projT, proj_b, gnn_b2, x, x1_dram, ident):
    (loaded, x_loaded, staged, turned, copied_a, copied_d, projected, summed, stored, stores) = (
        cx.sem("proj_" + s) for s in ("loaded", "x_loaded", "staged", "turned", "copied_a", "copied_d", "projected",
                                      "summed", "stored", "stores"))
    dve_step = cx.sem("proj_step")
    with ExitStack() as st:
        w = sb(nc, st, "proj_w", [128, KD, D])
        bias = sb(nc, st, "proj_bias", [P, 2, D])
        xr = sb(nc, st, "proj_x", [P, NT, D])
        at = sb(nc, st, "proj_at", [P, D])
        aT = sb(nc, st, "proj_aT", [128, KD, P])
        TP = [pb(nc, st, f"proj_T{j}", [128, 3, P]) for j in range(2)]
        Y = [pb(nc, st, f"proj_Y{j}", [P, 384]) for j in range(2)]
        block = st.enter_context(nc.Block())

        @block.sync
        def _(sp):
            sp.dma_start(w[:], projT.rearrange("(k p) n -> p k n", p=128)).then_inc(loaded, 16)
            sp.dma_start(bias[:, 0, :], proj_b.partition_broadcast(P)).then_inc(loaded, 16)
            sp.dma_start(bias[:, 1, :], gnn_b2.partition_broadcast(P)).then_inc(loaded, 16)
            sp.dma_start(xr[:], x.rearrange("(t p) d -> p t d", p=P)).then_inc(x_loaded, 16)
            sp.wait_ge(summed, 2 * NT)
            sp.dma_start(x1_dram.rearrange("(t p) d -> p t d", p=P), xr[:]).then_inc(stores, 16)
            sp.wait_ge(stores, 16)

        @block.gpsimd
        def _(pool):
            with pool.Fori(0, NT) as t:
                pool.wait_ge(turned, t + 1)
                pool.tensor_copy(at[:], attn[:, bass.ds(t, 1), :]).then_inc(staged, 1)

        @block.tensor
        def _(pe):
            pe.sem_inc(turned, 1)
            pe.sem_inc(projected, 1)

            def turn(t):
                pe.wait_ge(staged, t + 1)
                pe.wait_ge(copied_a, t + 1)
                pe.wait_ge(copied_d, t + 1)
                for k in range(KD):
                    last = pe.transpose(TP[k // 3][:, k % 3, :], at[:, k * 128:(k + 1) * 128], ident[0:P, 0:P])
                last.then_inc(turned, 1)

            def project(t):
                pe.wait_ge(copied_a, t + 2)
                pe.wait_ge(copied_d, t + 2)
                for j in range(2):
                    pe.wait_ge(stored, 2 * t + (j + 1))
                    for k in range(KD):
                        last = pe.matmul(Y[j][:], aT[:, k, :], w[:, k, j * 384:(j + 1) * 384],
                                         start=(k == 0), stop=(k == KD - 1))
                    last.then_inc(projected, 1)

            pe.wait_ge(loaded, 48)
            with pe.Fori(0, NT) as t:
                turn(t)
                project(t)

        @block.scalar
        def _(act):
            act.sem_inc(copied_a, 1)
            with act.Fori(0, NT) as t:
                act.wait_ge(turned, t + 2)
                act.wait_ge(projected, 2 * t + 1)
                act.activation(aT[:, 0:3, :], TP[0][:], ACT.Copy).then_inc(copied_a, 1)

        @block.vector
        def _(dve):
            step = Chain(dve, dve_step)
            dve.sem_inc(copied_d, 1)
            dve.sem_inc(stored, 2)
            dve.wait_ge(loaded, 48)
            dve.wait_ge(x_loaded, 16)
            step(dve.tensor_tensor(bias[:, 0, :], bias[:, 0, :], bias[:, 1, :], ALU.add))
            step(dve.tensor_tensor(xr[:], xr[:], bias[:, 0:1, :].to_broadcast([P, NT, D]), ALU.add))
            with dve.Fori(0, NT) as t:
                dve.wait_ge(turned, t + 2)
                dve.wait_ge(projected, 2 * t + 1)
                dve.tensor_copy(aT[:, 3:6, :], TP[1][:]).then_inc(copied_d, 1)
                for j in range(2):
                    dve.wait_ge(projected, 2 * t + (j + 2))
                    col = xr[:, bass.ds(t, 1), j * 384:(j + 1) * 384]
                    dve.tensor_tensor(col, Y[j][:].unsqueeze(1), col, ALU.add).then_inc(stored, 1)
            dve.drain().then_inc(summed, 2 * NT)


def mix_half_phase(nc, cx, half, wqkvT, qkv_b, rfT_dram, xnT, ident, ones, attn):
    HH = MH // 2
    HW = HH * MD
    A = MD + 1
    SCALE = MD ** -0.5
    tag = f"mix{half}_"
    (w_loaded, staged, q_done, k_done, v_done, q_evac, k_evac, v_evac, qsq, ksq, q_ready, k_ready, q_turned,
     k_turned, qT_done, kT_done, phi_a, phi_b, exp_a, exp_b, kv_step, kv_copied, consts) = (
        cx.sem(tag + s) for s in
        ("w_loaded", "staged", "q_done", "k_done", "v_done", "q_evac", "k_evac", "v_evac", "qsq", "ksq", "q_ready",
         "k_ready", "q_turned", "k_turned", "qT_done", "kT_done", "phi_a", "phi_b", "exp_a", "exp_b", "kv_step",
         "kv_copied", "consts"))
    dve_step = cx.sem(tag + "dve_step")
    pool_step = cx.sem(tag + "pool_step")
    with ExitStack() as st:
        rfT = sb(nc, st, tag + "rfT", [A, RF])
        qT = sb(nc, st, tag + "qT", [A, HH, N])
        kv = sb(nc, st, tag + "kv", [128, HH, 2, A])
        with ExitStack() as st1:
            w = sb(nc, st1, tag + "w", [128, KD, 3, HW])
            brow = sb(nc, st1, tag + "brow", [P, 3, HW])
            xs = sb(nc, st1, tag + "xs", [128, KD, P])
            qs = sb(nc, st1, tag + "qs", [P, 2, HH, A])
            sq = sb(nc, st1, tag + "sq", [P, 2, HH, MD])
            nrm = sb(nc, st1, tag + "nrm", [P, 2, HH])
            vs = sb(nc, st1, tag + "vs", [P, HH, A])
            kT = sb(nc, st1, tag + "kT", [A, HH, P])
            phik = sb(nc, st1, tag + "phik", [P, HH, RF])
            zero = sb(nc, st1, tag + "zero", [P, 128])
            G = [pb(nc, st1, tag + f"G{j}", [P, HW]) for j in range(3)]
            TQ = pb(nc, st1, tag + "TQ", [A, HH, P])
            PH = [pb(nc, st1, tag + f"PH{j}", [P, 2, RF]) for j in range(2)]
            KV = [pb(nc, st1, tag + f"KV{j}", [128, 2, 2, A]) for j in range(2)]
            block = st1.enter_context(nc.Block())

            @block.sync
            def _(sp):
                for c in range(3):
                    src = wqkvT[:, c * D + half * HW:c * D + (half + 1) * HW].rearrange("(k p) n -> p k n", p=128)
                    sp.dma_start(w[:, :, c, :], src).then_inc(w_loaded, 16)
                    sp.dma_start(brow[:, c, :], qkv_b[c * D + half * HW:c * D + (half + 1) * HW]
                                 .partition_broadcast(P)).then_inc(w_loaded, 16)
                sp.dma_start(rfT[0:MD, :], rfT_dram).then_inc(w_loaded, 16)

            @block.gpsimd
            def _(pool):
                pool.memset(zero[:], 0.0).then_inc(consts, 1)
                pool.memset(vs[:], 1.0).then_inc(consts, 1)
                pool.tensor_copy(xs[:], xnT[:, :, 0:P]).then_inc(staged, 1)
                with pool.Fori(1, NT) as t:
                    pool.wait_ge(v_done, t)
                    pool.tensor_copy(xs[:], xnT[:, :, bass.ds(t * P, P)]).then_inc(staged, 1)

            @block.vector
            def _(dve):
                step = Chain(dve, dve_step)
                dve.sem_inc(q_ready, 1)
                dve.sem_inc(k_ready, 1)
                dve.wait_ge(w_loaded, 16 * 7)
                step(dve.memset(rfT[MD:A, :], 1.0))
                step(dve.tensor_scalar(brow[:, 0:2, :], brow[:, 0:2, :], SCALE, None, ALU.mult))
                step.flat_end()
                dve.wait_ge(consts, 2)
                with dve.Fori(0, NT) as t:
                    step.start(t, 2)
                    for c, (done, turned, evac, squared, ready) in enumerate(
                            ((q_done, q_turned, q_evac, qsq, q_ready), (k_done, k_turned, k_evac, ksq, k_ready))):
                        dve.wait_ge(done, t + 1)
                        dve.wait_ge(turned, t + 1)
                        dve.scalar_tensor_tensor(qs[:, c, :, 0:MD], G[c][:].rearrange("p (h d) -> p h d", d=MD), SCALE,
                                                 brow[:, c, :].rearrange("p (h d) -> p h d", d=MD),
                                                 ALU.mult, ALU.add).then_inc(evac, 1)
                        dve.wait_ge(squared, t + 1)
                        step(dve.tensor_reduce(nrm[:, c, :], sq[:, c, :, :], AX.X, ALU.add))
                        dve.tensor_scalar(qs[:, c, :, MD:A], nrm[:, c, :].unsqueeze(2), -0.5, None,
                                          ALU.mult).then_inc(ready, 1)
                    dve.wait_ge(v_done, t + 1)
                    dve.wait_ge(kv_step, t + 1)
                    dve.tensor_tensor(vs[:, :, 0:MD], G[2][:].rearrange("p (h d) -> p h d", d=MD),
                                      brow[:, 2, :].rearrange("p (h d) -> p h d", d=MD), ALU.add).then_inc(v_evac, 1)
                step.end(NT)
                dve.wait_ge(kv_step, NT + 1)
                for j in range(2):
                    dve.tensor_copy(kv[:, 2 * j:2 * j + 2, :, :], KV[j][:]).then_inc(kv_copied, 1)

            @block.scalar
            def _(act):
                for freed in (kT_done, exp_a, exp_b):
                    act.sem_inc(freed, 1)
                with act.Fori(0, NT) as t:
                    for c, (evac, squared, ready) in enumerate(((q_evac, qsq, q_ready), (k_evac, ksq, k_ready))):
                        act.wait_ge(evac, t + 1)
                        act.wait_ge(ready, t + 1)
                        act.activation(sq[:, c, :, :], qs[:, c, :, 0:MD], ACT.Square).then_inc(squared, 1)
                        if c == 0:
                            act.wait_ge(q_turned, t + 2)
                            act.activation(qT[:, :, bass.ds(t * P, P)], TQ[:], ACT.Copy).then_inc(qT_done, 1)
                    act.wait_ge(k_turned, t + 2)
                    act.wait_ge(phi_b, t + 1)
                    act.activation(kT[:], TQ[:], ACT.Copy).then_inc(kT_done, 1)
                    act.wait_ge(kv_step, t + 1)
                    act.wait_ge(phi_a, t + 1)
                    act.activation(phik[:, 0:2, :], PH[0][:], ACT.Exp).then_inc(exp_a, 1)
                    act.wait_ge(phi_b, t + 2)
                    act.activation(phik[:, 2:4, :], PH[1][:], ACT.Exp).then_inc(exp_b, 1)

            @block.tensor
            def _(pe):
                pe.sem_inc(q_turned, 1)
                pe.sem_inc(k_turned, 1)
                pe.sem_inc(kv_step, 1)
                pe.sem_inc(phi_b, 1)

                def gemm(c, t, done, evac):
                    if c == 0:
                        pe.wait_ge(staged, t + 1)
                    if evac is not None:
                        pe.wait_ge(evac, t)
                    for k in range(KD):
                        last = pe.matmul(G[c][:], xs[:, k, :], w[:, k, c, :], start=(k == 0), stop=(k == KD - 1))
                    last.then_inc(done, 1)

                def turn(c, t):
                    pe.wait_ge(k_ready if c else q_ready, t + 2)
                    if c == 0:
                        pe.wait_ge(kT_done, t + 1)
                    else:
                        pe.wait_ge(qT_done, t + 1)
                    for h in range(HH):
                        last = pe.transpose(TQ[:, h, :], qs[:, c, h, :], ident[0:P, 0:P])
                    last.then_inc(k_turned if c else q_turned, 1)

                def features(t):
                    pe.wait_ge(kT_done, t + 2)
                    for j, (done, used) in enumerate(((phi_a, exp_a), (phi_b, exp_b))):
                        pe.wait_ge(used, t + 1)
                        for h in range(2):
                            last = pe.matmul(PH[j][:, h, :], kT[:, 2 * j + h, :], rfT[:], start=True, stop=True,
                                             skip_group_check=True)
                        last.then_inc(done, 1)

                def keys_values(t, stop):
                    pe.wait_ge(exp_b, t + 2)
                    pe.wait_ge(exp_a, t + 2)
                    pe.wait_ge(v_evac, t + 1)
                    for h in range(HH):
                        for m in range(2):
                            last = pe.matmul(KV[h // 2][:, h % 2, m, :], phik[:, h, m * 128:(m + 1) * 128],
                                             vs[:, h, :], start=False, stop=stop, skip_group_check=True)
                    last.then_inc(kv_step, 1)

                pe.wait_ge(consts, 2)
                pe.wait_ge(w_loaded, 16 * 7)
                for j in range(2):
                    pe.matmul(KV[j][:].rearrange("p h m a -> p (h m a)"), zero[:],
                              vs[:].rearrange("p h a -> p (h a)"), start=True, stop=False, skip_group_check=True)
                gemm(0, 0, q_done, None)
                gemm(1, 0, k_done, None)
                gemm(2, 0, v_done, None)
                with pe.Fori(0, NT - 1) as t:
                    turn(0, t)
                    gemm(0, t + 1, q_done, q_evac)
                    turn(1, t)
                    gemm(1, t + 1, k_done, k_evac)
                    features(t)
                    gemm(2, t + 1, v_done, v_evac)
                    keys_values(t, False)
                turn(0, NT - 1)
                turn(1, NT - 1)
                features(NT - 1)
                keys_values(NT - 1, True)
        numerator(nc, cx, tag, half, rfT, qT, kv, attn)


def logits_phase(nc, cx, W1, a_src, a_dst, xnT, ident, w, al, alT_dram):
    loaded, wa_step, rows_done, rows_copied, turned, stored, al_copied = (
        cx.sem("logit_" + s) for s in ("loaded", "wa_step", "rows_done", "rows_copied", "turned", "stored", "al_copied"))
    J = 2 * H1
    with ExitStack() as st:
        ab = sb(nc, st, "logit_a", [128, 2, F1])
        junk = sb(nc, st, "logit_junk", [128, 2, C1])
        wa = sb(nc, st, "logit_wa", [128, KD, J])
        alT = sb(nc, st, "logit_alT", [J, N])
        R = [pb(nc, st, f"logit_R{c}", [J, 512]) for c in range(CH)]
        T = pb(nc, st, "logit_T", [P, NT, J])
        block = st.enter_context(nc.Block())

        @block.sync
        def _(sp):
            sp.dma_start(ab[:, 0, :], a_src.rearrange("h c -> (h c)").partition_broadcast(128)).then_inc(loaded, 16)
            sp.dma_start(ab[:, 1, :], a_dst.rearrange("h c -> (h c)").partition_broadcast(128)).then_inc(loaded, 16)
            sp.dma_start(w[:], W1.rearrange("(k p) n -> p k n", p=128)).then_inc(loaded, 16)
            sp.wait_ge(rows_copied, CH)
            sp.dma_start(alT_dram, alT[:]).then_inc(stored, 16)
            sp.wait_ge(stored, 16)

        @block.vector
        def _(dve):
            dve.wait_ge(loaded, 48)
            n = 0
            for k in range(KD):
                for s in range(2):
                    for h in range(H1):
                        if n >= 2:
                            dve.wait_ge(wa_step, n - 1)
                        dve.tensor_tensor_reduce(out=junk[:, n % 2, :], in0=w[:, k, h * C1:(h + 1) * C1],
                                                 in1=ab[:, s, h * C1:(h + 1) * C1], scale=1.0, scalar=0.0,
                                                 op0=ALU.mult, op1=ALU.add,
                                                 accum_out=wa[:, k, s * H1 + h:s * H1 + h + 1]).then_inc(wa_step, 1)
                        n += 1
            for c in range(CH):
                dve.wait_ge(rows_done, c + 1)
                dve.tensor_copy(alT[:, CHO[c]:CHO[c] + CHW[c]], R[c][:, 0:CHW[c]]).then_inc(rows_copied, 1)
            dve.wait_ge(turned, 1)
            dve.tensor_copy(al[:], T[:]).then_inc(al_copied, 1)

        @block.tensor
        def _(pe):
            pe.wait_ge(wa_step, KD * J)
            for c in range(CH):
                for k in range(KD):
                    last = pe.matmul(R[c][:, 0:CHW[c]], wa[:, k, :], xnT[:, k, CHO[c]:CHO[c] + CHW[c]],
                                     start=(k == 0), stop=(k == KD - 1))
                last.then_inc(rows_done, 1)
            pe.wait_ge(rows_copied, CH)
            for t in range(NT):
                last = pe.transpose(T[:, t, :], alT[:, t * P:(t + 1) * P], ident[0:J, 0:J])
            last.then_inc(turned, 1)


def edge_table_phase(nc, cx, src, dst, ident, keyT, sloT, spans):
    blank, loaded, iotas, key_ready, turned, span_ready, span_max, copied = (
        cx.sem("edge_" + s) for s in
        ("blank", "loaded", "iotas", "key_ready", "turned", "span_ready", "span_max", "copied"))
    dve_step = cx.sem("edge_step")
    FULL = EDGES // ER
    REST = EDGES - FULL * ER
    LAST = FULL - 2 * EGP
    with ExitStack() as st:
        di = sb(nc, st, "edge_di", [EGP, EG, ER], I32)
        si = sb(nc, st, "edge_si", [EGP, EG, ER], I32)
        df = sb(nc, st, "edge_df", [EGP, EG, ER])
        sf = sb(nc, st, "edge_sf", [EGP, EG, ER])
        hi = sb(nc, st, "edge_hi", [EGP, EG, ER])
        key = sb(nc, st, "edge_key", [EGP, EG, ER])
        slo = sb(nc, st, "edge_slo", [EGP, EG, ER])
        rng = sb(nc, st, "edge_rng", [EGP, 2, EG])
        row = sb(nc, st, "edge_row", [EGP, EG])
        row1 = sb(nc, st, "edge_row1", [EGP, 2, EG])
        win = sb(nc, st, "edge_win", [EGP, NW])
        c1 = sb(nc, st, "edge_c1", [EGP, NW])
        best = sb(nc, st, "edge_best", [EGP, 2, NW])
        allb = sb(nc, st, "edge_allb", [EGP, 2, NW])
        spi = sb(nc, st, "edge_spi", [EGP, 2, NW], I32)
        T = [pb(nc, st, f"edge_T{j}", [128, EROWS]) for j in range(2)]
        block = st.enter_context(nc.Block())

        @block.sync
        def _(sp):
            sp.wait_ge(blank, 2)
            for v, t in ((dst, di), (src, si)):
                for g in range(2):
                    sp.dma_start(t[:, g, :], v[g * EGP * ER:(g + 1) * EGP * ER].rearrange("(p e) -> p e", e=ER)
                                 ).then_inc(loaded, 16)
                sp.dma_start(t[0:LAST, 2, :], v[2 * EGP * ER:FULL * ER].rearrange("(p e) -> p e", e=ER)
                             ).then_inc(loaded, 16)
                sp.dma_start(t[LAST:LAST + 1, 2, 0:REST], v[FULL * ER:EDGES].unsqueeze(0)).then_inc(loaded, 16)

        @block.gpsimd
        def _(pool):
            pool.memset(di[:], PADNODE).then_inc(blank, 1)
            pool.memset(si[:], 0).then_inc(blank, 1)
            pool.iota(row[:], [[EGP, EG]], base=0, channel_multiplier=1,
                      allow_small_or_imprecise_dtypes=True).then_inc(iotas, 1)
            pool.iota(win[:], [[WIN, NW]], base=0, channel_multiplier=0,
                      allow_small_or_imprecise_dtypes=True).then_inc(iotas, 1)
            pool.wait_ge(span_ready, 1)
            pool.partition_all_reduce(allb[:], best[:], EGP, bass.bass_isa.ReduceOp.max).then_inc(span_max, 1)

        @block.vector
        def _(dve):
            step = Chain(dve, dve_step)
            dve.wait_ge(loaded, 8 * 16)
            step(dve.tensor_copy(df[:], di[:]))
            step(dve.tensor_copy(sf[:], si[:]))
            step(dve.tensor_scalar(hi[:], sf[:], float(SLO), None, ALU.is_ge))
            for part in range(2, SPLIT):
                step(dve.scalar_tensor_tensor(hi[:], sf[:], float(part * SLO), hi[:], ALU.is_ge, ALU.add))
            step(dve.scalar_tensor_tensor(slo[:], hi[:], -float(SLO), sf[:], ALU.mult, ALU.add))
            dve.scalar_tensor_tensor(key[:], df[:], float(SPLIT), hi[:], ALU.mult, ALU.add).then_inc(key_ready, 1)
            step(dve.tensor_reduce(rng[:, 0, :], df[:], AX.X, ALU.min))
            step(dve.tensor_reduce(rng[:, 1, :], df[:], AX.X, ALU.max))
            dve.wait_ge(iotas, 2)
            step(dve.tensor_scalar(row1[:, 0, :], row[:], -1.0, 1000.0, ALU.mult, ALU.add))
            step(dve.tensor_scalar(row1[:, 1, :], row[:], 1.0, None, ALU.add))
            step(dve.memset(best[:], 0.0))
            for g in range(EG):
                step(dve.tensor_scalar(c1[:], win[:], float(WIN - 1), rng[:, 0, g:g + 1], ALU.add, ALU.is_ge))
                step(dve.scalar_tensor_tensor(c1[:], win[:], rng[:, 1, g:g + 1], c1[:], ALU.is_le, ALU.mult))
                for e in range(2):
                    ins = dve.scalar_tensor_tensor(best[:, e, :], c1[:], row1[:, e, g:g + 1], best[:, e, :],
                                                   ALU.mult, ALU.max)
                    if (g, e) == (EG - 1, 1):
                        ins.then_inc(span_ready, 1)
                    else:
                        step(ins)
            dve.wait_ge(span_max, 1)
            step(dve.tensor_scalar(allb[:, 0, :], allb[:, 0, :], -1.0, 1000.0, ALU.mult, ALU.add))
            step(dve.tensor_scalar(allb[:, 0, :], allb[:, 0, :], float(EROWS - 2), None, ALU.min))
            step(dve.tensor_scalar(allb[:, 1, :], allb[:, 1, :], 1.0, None, ALU.add))
            step(dve.scalar_tensor_tensor(allb[:, 1, :], allb[:, 0, :], 2.0, allb[:, 1, :], ALU.add, ALU.max))
            step(dve.tensor_copy(spi[:], allb[:]))
            step(dve.tensor_scalar(spans[:], spi[0:1, :, :].rearrange("p e w -> p (e w)"), 1, None,
                                   ALU.logical_shift_right))
            for j, dest in enumerate((keyT, sloT)):
                dve.wait_ge(turned, j + 1)
                dve.tensor_copy(dest[:], T[j][:]).then_inc(copied, 1)

        @block.tensor
        def _(pe):
            pe.wait_ge(key_ready, 1)
            for j, s in enumerate((key, slo)):
                for g in range(EG):
                    last = pe.transpose(T[j][:, g * EGP:(g + 1) * EGP], s[:, g, :], ident[0:EGP, 0:EGP])
                last.then_inc(turned, 1)


def count_phase(nc, cx, keyT, sloT, spans, ct_dram, xnT, w, h):
    assert NW == H1 * NT
    RING = 8
    consts, hot, used, counted, evac, gemm, h_evac = (
        cx.sem("count_" + s) for s in ("consts", "hot", "used", "counted", "evac", "gemm", "h_evac"))
    stores = [cx.sem(f"count_stored{b}") for b in range(2)]
    with ExitStack() as st:
        ikey = sb(nc, st, "count_ikey", [128, 128], F16)
        islo = sb(nc, st, "count_islo", [128, SLO], F16)
        off = sb(nc, st, "count_off", [128, NW])
        zero = sb(nc, st, "count_zero", [128, 128], BF16)
        A = sb(nc, st, "count_A", [128, RING * 2, 128], BF16)
        B = sb(nc, st, "count_B", [128, RING * 2, SLO], BF16)
        out = [sb(nc, st, f"count_out{b}", [128, SLO]) for b in range(2)]
        S = [pb(nc, st, f"count_S{b}", [128, SLO]) for b in range(2)]
        G = [pb(nc, st, f"count_G{b}", [P, C1]) for b in range(2)]
        block = st.enter_context(nc.Block())

        def windows(eng, name, body, before=None, after=None):
            with eng.register(name + "_turn") as turn, eng.register(name + "_slot") as slot:
                eng.reg_mov(turn, 1)
                eng.reg_mov(slot, 0)
                with eng.Fori(0, H1) as hd:
                    for t in range(NT):
                        lo = eng.value_load(spans[0:1, bass.ds(hd * NT + t, 1)], min_val=0, max_val=EROWS // 2 - 1)
                        hi = eng.value_load(spans[0:1, bass.ds(hd * NT + (NW + t), 1)], min_val=1,
                                            max_val=EROWS // 2)
                        if before is not None:
                            before(hd, t)
                        with eng.Fori(lo, hi) as r:
                            body(r, eng.snap(turn), eng.snap(slot, min_val=0, max_val=RING - 1), hd, t)
                            eng.reg_add(turn, turn, 1)
                            eng.reg_add(slot, slot, 1)
                            eng.reg_mod(slot, slot, RING)
                        if after is not None:
                            after(hd, t)

        @block.gpsimd
        def _(pool):
            kw = dict(allow_small_or_imprecise_dtypes=True)
            pool.iota(ikey[:], [[1, 128]], base=0, channel_multiplier=0, **kw).then_inc(consts, 1)
            pool.iota(islo[:], [[1, SLO]], base=0, channel_multiplier=0, **kw).then_inc(consts, 1)
            pool.iota(off[:], [[-WIN * SPLIT, NW]], base=0, channel_multiplier=0, **kw).then_inc(consts, 1)
            pool.memset(zero[:], 0.0).then_inc(consts, 1)
            pool.memset(h[:, :, :, C1:C1 + 1], 1.0)

        @block.vector
        def _(dve):
            dve.wait_ge(consts, 4)

            def body(r, n, s, hd, t):
                dve.wait_ge(used, n)
                for b in range(2):
                    dve.tensor_scalar(A[:, bass.ds(s * 2 + b, 1), :], ikey[:].unsqueeze(1),
                                      keyT[:, bass.ds(r * 2 + b, 1)], off[:, bass.ds(hd * NT + t, 1)],
                                      ALU.subtract, ALU.is_equal)
                    last = dve.tensor_scalar(B[:, bass.ds(s * 2 + b, 1), :], islo[:].unsqueeze(1),
                                             sloT[:, bass.ds(r * 2 + b, 1)], None, ALU.is_equal)
                last.then_inc(hot, 1)

            windows(dve, "count_dve", body)

        @block.tensor
        def _(pe):
            pe.wait_ge(consts, 4)
            pe.sem_inc(used, RING)

            def before(hd, t):
                pe.wait_ge(h_evac, hd * NT + (t + 1))
                for k in range(KD):
                    last = pe.matmul(G[t % 2][:], xnT[:, k, t * P:(t + 1) * P], w[:, k, bass.ds(hd * C1, C1)],
                                     start=(k == 0), stop=(k == KD - 1))
                last.then_inc(gemm, 1)
                pe.wait_ge(evac, hd * NT + (t + 1))
                pe.matmul(S[t % 2][:], zero[:], islo[:], start=True, stop=False, skip_group_check=True)

            def body(r, n, s, hd, t):
                pe.wait_ge(hot, n)
                for b in range(2):
                    last = pe.matmul(S[t % 2][:], A[:, bass.ds(s * 2 + b, 1), :].rearrange("p o k -> p (o k)"),
                                     B[:, bass.ds(s * 2 + b, 1), :].rearrange("p o k -> p (o k)"),
                                     start=False, stop=False, skip_group_check=True)
                last.then_inc(used, 1)

            def after(hd, t):
                pe.matmul(S[t % 2][:], zero[:], islo[:], start=False, stop=True, skip_group_check=True
                          ).then_inc(counted, 1)

            windows(pe, "count_pe", body, before, after)

        @block.scalar
        def _(act):
            act.sem_inc(evac, 2)
            act.sem_inc(h_evac, 2)
            with act.Fori(0, H1) as hd:
                for t in range(NT):
                    act.wait_ge(gemm, hd * NT + (t + 1))
                    act.activation(h[:, t, bass.ds(hd, 1), 0:C1], G[t % 2][:].unsqueeze(1), ACT.Copy
                                   ).then_inc(h_evac, 1)
                    act.wait_ge(counted, hd * NT + (t + 1))
                    act.wait_ge(stores[t % 2], hd * (16 * NT // 2) + 16 * (t // 2))
                    act.activation(out[t % 2][:], S[t % 2][:], ACT.Copy).then_inc(evac, 1)

        @block.sync
        def _(sp):
            with sp.Fori(0, NW // 2) as w2:
                for q in range(2):
                    sp.wait_ge(evac, w2 * 2 + (q + 3))
                    sp.dma_start(ct_dram[bass.ds(w2 * 256 + q * 128, 128), :], out[q][:]).then_inc(stores[q], 16)
            for q in range(2):
                sp.wait_ge(stores[q], 16 * (NW // 2))


def mask_phase(nc, cx, ct_dram, c_dram, mask_dram, alT_dram, ident, al, mT_dram):
    HT = NT // 2
    rows_loaded, masked, turned, ev_d, ev_a, m_ready, m_turned, m_copied, m_stored = (
        cx.sem("mask_" + s) for s in ("rows_loaded", "masked", "turned", "ev_d", "ev_a", "m_ready",
                                      "m_turned", "m_copied", "m_stored"))
    loads = [cx.sem(f"mask_loaded{b}") for b in range(2)]
    mask_stores = [cx.sem(f"mask_mstored{b}") for b in range(2)]
    c_stores = [cx.sem(f"mask_cstored{b}") for b in range(2)]
    dve_step = cx.sem("mask_step")
    with ExitStack() as st:
        ct = [sb(nc, st, f"mask_ct{b}", [P, N]) for b in range(2)]
        mk = [sb(nc, st, f"mask_mk{b}", [P, N]) for b in range(2)]
        co = [sb(nc, st, f"mask_co{b}", [P, NT, P]) for b in range(2)]
        rows = sb(nc, st, "mask_rows", [P, H1, N])
        junk = sb(nc, st, "mask_junk", [P, N])
        big = sb(nc, st, "mask_big", [P, NT, H1])
        m = sb(nc, st, "mask_m", [P, NT, H1])
        mT = sb(nc, st, "mask_mT", [H1, N])
        T = [[pb(nc, st, f"mask_T{b}{j}", [P, 4, P]) for j in range(3)] for b in range(2)]
        width = [4, 4, 2]
        block = st.enter_context(nc.Block())

        @block.sync
        def _(sp):
            for h in range(H1):
                sp.dma_start(rows[:, h, :], alT_dram[h, :].partition_broadcast(P)).then_inc(rows_loaded, 16)
            with sp.Fori(0, HT) as i:
                for b in range(2):
                    sp.wait_ge(turned, i * 2 + (b + 1))
                    sp.wait_ge(masked, i * 2 + (b + 1))
                    sp.dma_start(ct[b][:], ct_dram.rearrange("(d a) s -> d (a s)", a=SPLIT)
                                 [bass.ds(i * (2 * P) + b * P, P), 0:N]).then_inc(loads[b], 16)
            sp.wait_ge(m_copied, 3)
            sp.dma_start(mT_dram, mT[:]).then_inc(m_stored, 16)
            sp.wait_ge(m_stored, 16)

        @block.gpsimd
        def _(pool):
            for t in range(NT):
                b = t % 2
                pool.wait_ge(masked, t + 3)
                pool.dma_start(mask_dram[t, :, :], mk[b][:]).then_inc(mask_stores[b], 16)
                pool.wait_ge(ev_d, t + 3)
                pool.wait_ge(ev_a, t + 3)
                pool.dma_start(c_dram[t, :, :], co[b][:].rearrange("p t d -> p (t d)")).then_inc(c_stores[b], 16)
            for b in range(2):
                pool.wait_ge(mask_stores[b], 16 * HT)
                pool.wait_ge(c_stores[b], 16 * HT)

        @block.vector
        def _(dve):
            step = Chain(dve, dve_step)
            dve.sem_inc(masked, 2)
            dve.sem_inc(ev_d, 2)
            dve.wait_ge(rows_loaded, 64)
            for t in range(NT):
                b = t % 2
                dve.wait_ge(loads[b], 16 * (t // 2 + 1))
                diag = ct[b][:, t * P:(t + 1) * P]
                step(dve.tensor_tensor(diag, diag, ident[0:P, 0:P], ALU.add))
                dve.wait_ge(mask_stores[b], 16 * (t // 2))
                dve.tensor_scalar(mk[b][:], ct[b][:], 0.0, -BIG, ALU.is_equal, ALU.mult).then_inc(masked, 1)
                dve.wait_ge(masked, t + 3)
                for h in range(H1):
                    step(dve.tensor_tensor_reduce(out=junk[:], in0=mk[b][:], in1=rows[:, h, :], scale=1.0,
                                                  scalar=-3.0e38, op0=ALU.add, op1=ALU.max,
                                                  accum_out=big[:, t, h:h + 1]))
                dve.wait_ge(turned, t + 3)
                dve.wait_ge(c_stores[b], 16 * (t // 2))
                dve.tensor_copy(co[b][:, 0:4, :], T[b][0][:]).then_inc(ev_d, 1)
            step(dve.tensor_tensor(big[:], big[:], al[:, :, H1:2 * H1], ALU.add))
            dve.scalar_tensor_tensor(m[:], big[:], SLOPE, big[:], ALU.mult, ALU.max).then_inc(m_ready, 1)
            for j in range(3):
                dve.wait_ge(m_turned, j + 1)
                dve.tensor_copy(mT[:, 4 * j * P:(4 * j + width[j]) * P],
                                T[0][j][0:H1, 0:width[j], :].rearrange("p t d -> p (t d)")).then_inc(m_copied, 1)

        @block.scalar
        def _(act):
            act.sem_inc(ev_a, 2)
            with act.Fori(0, HT) as i:
                for b in range(2):
                    act.wait_ge(turned, i * 2 + (b + 3))
                    act.wait_ge(c_stores[b], i * 16)
                    act.activation(co[b][:, 4:8, :], T[b][1][:], ACT.Copy)
                    act.activation(co[b][:, 8:10, :], T[b][2][:, 0:2, :], ACT.Copy).then_inc(ev_a, 1)

        @block.tensor
        def _(pe):
            pe.sem_inc(turned, 2)
            with pe.Fori(0, HT) as i:
                for b in range(2):
                    pe.wait_ge(masked, i * 2 + (b + 3))
                    pe.wait_ge(ev_a, i * 2 + (b + 1))
                    pe.wait_ge(ev_d, i * 2 + (b + 1))
                    for t in range(NT):
                        last = pe.transpose(T[b][t // 4][:, t % 4, :], ct[b][:, t * P:(t + 1) * P], ident[0:P, 0:P])
                    last.then_inc(turned, 1)
            pe.wait_ge(m_ready, 1)
            pe.wait_ge(ev_a, NT + 2)
            pe.wait_ge(ev_d, NT + 2)
            for j in range(3):
                for t in range(width[j]):
                    last = pe.transpose(T[0][j][0:H1, t, :], m[:, 4 * j + t, :], ident[0:P, 0:P])
                last.then_inc(m_turned, 1)


def gat1_phase(nc, cx, b1, h, al, alT_dram, mT_dram, c_dram, h1T_dram, ident):
    (rows_loaded, e_ready, exp_done, w_ready, agg, mn_ready, exp_mn, elu_ready, turned,
     t_evac, dve_step) = (
        cx.sem("gat1_" + s) for s in
        ("rows_loaded", "e_ready", "exp_done", "w_ready", "agg", "mn_ready", "exp_mn",
         "elu_ready", "turned", "t_evac", "dve_step"))
    c_loaded = [cx.sem(f"gat1_c_loaded{b}") for b in range(2)]
    stored = [cx.sem(f"gat1_stored{b}") for b in range(2)]
    b_loaded = cx.sem("gat1_b_loaded")
    HC = C1 // 2
    with ExitStack() as st:
        brow = sb(nc, st, "gat1_brow", [P, F1])
        rows = sb(nc, st, "gat1_rows", [P, 2, N])
        u = sb(nc, st, "gat1_u", [P, NT, P])
        e = [sb(nc, st, f"gat1_e{b}", [P, NT, P]) for b in range(2)]
        wt = [sb(nc, st, f"gat1_wt{b}", [P, NT, P]) for b in range(2)]
        cnt = [sb(nc, st, f"gat1_cnt{b}", [P, NT, P]) for b in range(2)]
        rden = [sb(nc, st, f"gat1_rden{b}", [P, 1]) for b in range(2)]
        o = [sb(nc, st, f"gat1_o{b}", [P, C1]) for b in range(2)]
        mn = [sb(nc, st, f"gat1_mn{b}", [P, C1]) for b in range(2)]
        oT = [sb(nc, st, f"gat1_oT{b}", [128, 4, P]) for b in range(2)]
        Z = [[pb(nc, st, f"gat1_Z{b}{j}", [P, HC + j]) for j in range(2)] for b in range(2)]
        T = [pb(nc, st, f"gat1_T{b}", [128, 4, P]) for b in range(2)]
        block = st.enter_context(nc.Block())

        @block.sync
        def _(sp):
            sp.dma_start(brow[:], b1.partition_broadcast(P)).then_inc(b_loaded, 16)
            with sp.Fori(0, H1) as hd:
                sp.wait_ge(e_ready, hd * NT)
                sp.dma_start(rows[:, 0, :], alT_dram[bass.ds(hd + H1, 1), :].partition_broadcast(P)
                             ).then_inc(rows_loaded, 16)
                sp.dma_start(rows[:, 1, :], mT_dram[bass.ds(hd, 1), :].partition_broadcast(P)
                             ).then_inc(rows_loaded, 16)
                for t in range(NT):
                    sp.wait_ge(w_ready, hd * NT + (t + 1))
                    sp.dma_start(cnt[t % 2][:], c_dram[t, :, :].rearrange("p (t d) -> p t d", d=P)
                                 ).then_inc(c_loaded[t % 2], 16)

        @block.vector
        def _(dve):
            step = Chain(dve, dve_step)
            for freed in (w_ready, mn_ready):
                dve.sem_inc(freed, 2)
            dve.wait_ge(b_loaded, 16)

            def scores(hd, t):
                b = t % 2
                dve.wait_ge(e_ready, hd * NT + t)
                step(dve.tensor_tensor(u[:], al[:, :, bass.ds(hd, 1)].to_broadcast([P, NT, P]),
                                       rows[:, 0:1, t * P:(t + 1) * P].to_broadcast([P, NT, P]), ALU.add))
                step(dve.scalar_tensor_tensor(u[:], u[:], SLOPE, u[:], ALU.mult, ALU.max))
                dve.wait_ge(w_ready, hd * NT + (t + 1))
                dve.tensor_tensor(e[b][:], u[:], rows[:, 1:2, t * P:(t + 1) * P].to_broadcast([P, NT, P]),
                                  ALU.subtract).then_inc(e_ready, 1)

            def weights(hd, t):
                b = t % 2
                dve.wait_ge(exp_done, hd * NT + (t + 1))
                dve.wait_ge(c_loaded[b], hd * (16 * NT // 2) + 16 * (t // 2 + 1))
                dve.wait_ge(agg, hd * NT + (t + 1))
                dve.tensor_tensor(wt[b][:], e[b][:], cnt[b][:], ALU.mult).then_inc(w_ready, 1)

            def normalise(hd, t):
                b = t % 2
                dve.wait_ge(agg, hd * NT + (t + 3))
                dve.wait_ge(turned, hd * NT + (t + 1))
                step(dve.tensor_scalar(rden[b][:], Z[b][1][:, HC:HC + 1], 1e-16, None, ALU.add))
                step(dve.reciprocal(rden[b][:], rden[b][:]))
                dve.scalar_tensor_tensor(o[b][:, 0:HC], Z[b][0][:], rden[b][:],
                                         brow[:, bass.ds(hd * C1, HC)], ALU.mult, ALU.add)
                step(dve.scalar_tensor_tensor(o[b][:, HC:C1], Z[b][1][:, 0:HC], rden[b][:],
                                              brow[:, bass.ds(hd * C1 + HC, HC)], ALU.mult, ALU.add))
                dve.wait_ge(elu_ready, hd * NT + t)
                dve.tensor_scalar(mn[b][:], o[b][:], 0.0, None, ALU.min).then_inc(mn_ready, 1)

            def elu(hd, t):
                b = t % 2
                dve.wait_ge(exp_mn, hd * NT + (t + 1))
                dve.scalar_tensor_tensor(o[b][:], mn[b][:], -1.0, o[b][:], ALU.add, ALU.max).then_inc(elu_ready, 1)

            with dve.Fori(0, H1) as hd:
                step.start(hd, 2 * NT + 3 * NT)
                dve.wait_ge(rows_loaded, hd * 32 + 32)
                scores(hd, 0)
                weights(hd, 0)
                for t in range(NT + 1):
                    if t + 1 < NT:
                        scores(hd, t + 1)
                    if t >= 1:
                        normalise(hd, t - 1)
                    if t + 1 < NT:
                        weights(hd, t + 1)
                    if t >= 1:
                        elu(hd, t - 1)
                step.end(H1)

        @block.scalar
        def _(act):
            act.sem_inc(t_evac, 2)
            with act.Fori(0, H1) as hd:
                def exp_scores(t):
                    act.wait_ge(e_ready, hd * NT + (t + 1))
                    act.activation(e[t % 2][:], e[t % 2][:], ACT.Exp).then_inc(exp_done, 1)

                exp_scores(0)
                for t in range(NT + 1):
                    if t + 1 < NT:
                        exp_scores(t + 1)
                    if t >= 1:
                        b = (t - 1) % 2
                        act.wait_ge(mn_ready, hd * NT + (t + 2))
                        act.activation(mn[b][:], mn[b][:], ACT.Exp).then_inc(exp_mn, 1)
                        act.wait_ge(turned, hd * NT + (t + 2))
                        act.wait_ge(stored[b], hd * (16 * NT // 2) + 16 * ((t - 1) // 2))
                        act.activation(oT[b][:], T[b][:], ACT.Copy).then_inc(t_evac, 1)
                        act.wait_ge(t_evac, hd * NT + (t + 2))
                        act.dma_start(h1T_dram[t - 1, :, :].rearrange("p (f d) -> p f d", d=P)
                                      [:, bass.ds(hd * 4, 4), :], oT[b][:]).then_inc(stored[b], 16)
            for b in range(2):
                act.wait_ge(stored[b], 16 * H1 * NT // 2)

        @block.tensor
        def _(pe):
            pe.sem_inc(agg, 2)
            pe.sem_inc(turned, 2)
            with pe.Fori(0, H1) as hd:
                for t in range(NT + 1):
                    if t < NT:
                        b = t % 2
                        pe.wait_ge(w_ready, hd * NT + (t + 3))
                        pe.wait_ge(mn_ready, hd * NT + (t + 1))
                        for j in range(2):
                            for s in range(NT):
                                last = pe.matmul(Z[b][j][:], wt[b][:, s, :],
                                                 h[:, s, bass.ds(hd, 1), j * HC:(j + 1) * HC + j],
                                                 start=(s == 0), stop=(s == NT - 1))
                        last.then_inc(agg, 1)
                    if t >= 1:
                        b = (t - 1) % 2
                        pe.wait_ge(elu_ready, hd * NT + t)
                        pe.wait_ge(t_evac, hd * NT + t)
                        for f in range(4):
                            last = pe.transpose(T[b][:, f, :], o[b][:, f * 128:(f + 1) * 128], ident[0:P, 0:P])
                        last.then_inc(turned, 1)


def gat2_project_phase(nc, cx, W2, a_src, a_dst, h1T_dram, ident, h2, al2, al2T_dram):
    loaded, wa_step, w2_ready, projected, ev_a, ev_d, turned, copied, stored = (
        cx.sem("gat2p_" + s) for s in
        ("loaded", "wa_step", "w2_ready", "projected", "ev_a", "ev_d", "turned", "copied", "stored"))
    in_loaded = [cx.sem(f"gat2p_in{b}") for b in range(2)]
    W = D + 2
    HW = W // 2
    with ExitStack() as st:
        w = sb(nc, st, "gat2p_w", [128, KF, W])
        ab = sb(nc, st, "gat2p_a", [128, 2, D])
        junk = sb(nc, st, "gat2p_junk", [128, 2, D])
        hT = [sb(nc, st, f"gat2p_hT{b}", [128, KF, P]) for b in range(2)]
        alT = sb(nc, st, "gat2p_alT", [2, N])
        Y = [[pb(nc, st, f"gat2p_Y{b}{j}", [P, HW]) for j in range(2)] for b in range(2)]
        T = [pb(nc, st, f"gat2p_T{j}", [2, 4, P]) for j in range(3)]
        width = [4, 4, 2]
        block = st.enter_context(nc.Block())

        @block.sync
        def _(sp):
            sp.dma_start(ab[:, 0, :], a_src[0, :].partition_broadcast(128)).then_inc(loaded, 16)
            sp.dma_start(ab[:, 1, :], a_dst[0, :].partition_broadcast(128)).then_inc(loaded, 16)
            sp.dma_start(w[:, :, 0:D], W2.rearrange("(k p) n -> p k n", p=128)).then_inc(loaded, 16)
            with sp.Fori(0, NT // 2) as i:
                for b in range(2):
                    sp.wait_ge(projected, i * 2 + (b + 1))
                    sp.dma_start(hT[b][:], h1T_dram[bass.ds(i * 2 + b, 1), :, :]
                                 .rearrange("o p (f d) -> p (o f) d", d=P)).then_inc(in_loaded[b], 16)
            sp.wait_ge(copied, 3)
            sp.dma_start(al2T_dram, alT[:]).then_inc(stored, 16)
            sp.wait_ge(stored, 16)

        @block.vector
        def _(dve):
            dve.sem_inc(ev_d, 2)
            dve.memset(h2[:, :, D:D + 1], 1.0).then_inc(w2_ready, 1)
            dve.wait_ge(loaded, 48)
            n = 0
            for k in range(KF):
                for s in range(2):
                    if n >= 2:
                        dve.wait_ge(wa_step, n - 1)
                    dve.tensor_tensor_reduce(out=junk[:, n % 2, :], in0=w[:, k, 0:D], in1=ab[:, s, :], scale=1.0,
                                             scalar=0.0, op0=ALU.mult, op1=ALU.add,
                                             accum_out=w[:, k, D + s:D + s + 1]).then_inc(wa_step, 1)
                    n += 1
            with dve.Fori(0, NT // 2) as i:
                for b in range(2):
                    dve.wait_ge(projected, i * 2 + (b + 3))
                    dve.tensor_copy(h2[:, bass.ds(i * 2 + b, 1), HW:D], Y[b][1][:, 0:HW - 2].unsqueeze(1))
                    dve.tensor_copy(al2[:, bass.ds(i * 2 + b, 1), :], Y[b][1][:, HW - 2:HW].unsqueeze(1)
                                    ).then_inc(ev_d, 1)
            for j in range(3):
                dve.wait_ge(turned, j + 1)
                dve.tensor_copy(alT[:, 4 * j * P:(4 * j + width[j]) * P],
                                T[j][:, 0:width[j], :].rearrange("p t d -> p (t d)")).then_inc(copied, 1)

        @block.scalar
        def _(act):
            act.sem_inc(ev_a, 2)
            with act.Fori(0, NT // 2) as i:
                for b in range(2):
                    act.wait_ge(projected, i * 2 + (b + 3))
                    act.activation(h2[:, bass.ds(i * 2 + b, 1), 0:HW], Y[b][0][:].unsqueeze(1), ACT.Copy
                                   ).then_inc(ev_a, 1)

        @block.tensor
        def _(pe):
            pe.sem_inc(projected, 2)
            pe.wait_ge(loaded, 48)
            pe.wait_ge(wa_step, 2 * KF)
            with pe.Fori(0, NT // 2) as i:
                for b in range(2):
                    pe.wait_ge(in_loaded[b], i * 16 + 16)
                    pe.wait_ge(ev_a, i * 2 + (b + 1))
                    pe.wait_ge(ev_d, i * 2 + (b + 1))
                    for j in range(2):
                        for k in range(KF):
                            last = pe.matmul(Y[b][j][:], hT[b][:, k, :], w[:, k, j * HW:(j + 1) * HW],
                                             start=(k == 0), stop=(k == KF - 1))
                    last.then_inc(projected, 1)
            pe.wait_ge(ev_d, NT + 2)
            for j in range(3):
                for t in range(width[j]):
                    last = pe.transpose(T[j][:, t, :], al2[:, 4 * j + t, :], ident[0:P, 0:P])
                last.then_inc(turned, 1)


def gat2_max_phase(nc, cx, mask_dram, al2, al2T_dram, m2T_dram, ident):
    row_loaded, m_ready, turned, copied, stored = (
        cx.sem("gat2m_" + s) for s in ("row_loaded", "m_ready", "turned", "copied", "stored"))
    loads = [cx.sem(f"gat2m_in{b}") for b in range(2)]
    maxed = cx.sem("gat2m_maxed")
    dve_step = cx.sem("gat2m_step")
    with ExitStack() as st:
        row = sb(nc, st, "gat2m_row", [P, N])
        mk = [sb(nc, st, f"gat2m_mk{b}", [P, N]) for b in range(2)]
        junk = [sb(nc, st, f"gat2m_junk{b}", [P, N]) for b in range(2)]
        big = sb(nc, st, "gat2m_big", [P, NT])
        m = sb(nc, st, "gat2m_m", [P, NT])
        mT = sb(nc, st, "gat2m_mT", [1, N])
        T = [pb(nc, st, f"gat2m_T{j}", [1, 4, P]) for j in range(3)]
        width = [4, 4, 2]
        block = st.enter_context(nc.Block())

        @block.sync
        def _(sp):
            sp.dma_start(row[:], al2T_dram[0, :].partition_broadcast(P)).then_inc(row_loaded, 16)
            with sp.Fori(0, NT // 2) as i:
                for b in range(2):
                    sp.wait_ge(maxed, i * 2 + (b + 1))
                    sp.dma_start(mk[b][:], mask_dram[bass.ds(i * 2 + b, 1), :, :].rearrange("o p n -> p (o n)")
                                 ).then_inc(loads[b], 16)
            sp.wait_ge(copied, 3)
            sp.dma_start(m2T_dram, mT[:]).then_inc(stored, 16)
            sp.wait_ge(stored, 16)

        @block.vector
        def _(dve):
            step = Chain(dve, dve_step)
            dve.sem_inc(maxed, 2)
            dve.wait_ge(row_loaded, 16)
            for t in range(NT):
                b = t % 2
                dve.wait_ge(loads[b], 16 * (t // 2 + 1))
                dve.wait_ge(maxed, t + 1)
                dve.tensor_tensor_reduce(out=junk[b][:], in0=mk[b][:], in1=row[:], scale=1.0, scalar=-3.0e38,
                                         op0=ALU.add, op1=ALU.max, accum_out=big[:, t:t + 1]).then_inc(maxed, 1)
            dve.wait_ge(maxed, NT + 2)
            step(dve.tensor_tensor(big[:], big[:], al2[:, :, 1], ALU.add))
            dve.scalar_tensor_tensor(m[:], big[:], SLOPE, big[:], ALU.mult, ALU.max).then_inc(m_ready, 1)
            for j in range(3):
                dve.wait_ge(turned, j + 1)
                dve.tensor_copy(mT[:, 4 * j * P:(4 * j + width[j]) * P],
                                T[j][:, 0:width[j], :].rearrange("p t d -> p (t d)")).then_inc(copied, 1)

        @block.tensor
        def _(pe):
            pe.wait_ge(m_ready, 1)
            for j in range(3):
                for t in range(width[j]):
                    last = pe.transpose(T[j][:, t, :], m[:, 4 * j + t:4 * j + t + 1], ident[0:P, 0:P])
                last.then_inc(turned, 1)


def gat2_phase(nc, cx, al2, al2T_dram, m2T_dram, c_dram, h2, x1_dram, x1):
    (rows_loaded, x_loaded, e_ready, exp_done, w_ready, agg, summed, dve_step) = (
        cx.sem("gat2_" + s) for s in
        ("rows_loaded", "x_loaded", "e_ready", "exp_done", "w_ready", "agg", "summed", "dve_step"))
    c_loaded = [cx.sem(f"gat2_c_loaded{b}") for b in range(2)]
    CW = [385, 384]
    with ExitStack() as st:
        rows = sb(nc, st, "gat2_rows", [P, 2, N])
        u = sb(nc, st, "gat2_u", [P, NT, P])
        e = [sb(nc, st, f"gat2_e{b}", [P, NT, P]) for b in range(2)]
        wt = [sb(nc, st, f"gat2_wt{b}", [P, NT, P]) for b in range(2)]
        cnt = [sb(nc, st, f"gat2_cnt{b}", [P, NT, P]) for b in range(2)]
        rden = [sb(nc, st, f"gat2_rden{b}", [P, 1]) for b in range(2)]
        Z = [[pb(nc, st, f"gat2_Z{b}{j}", [P, CW[j]]) for j in range(2)] for b in range(2)]
        block = st.enter_context(nc.Block())

        @block.sync
        def _(sp):
            sp.dma_start(rows[:, 0, :], al2T_dram[1, :].partition_broadcast(P)).then_inc(rows_loaded, 16)
            sp.dma_start(rows[:, 1, :], m2T_dram[0, :].partition_broadcast(P)).then_inc(rows_loaded, 16)
            sp.dma_start(x1[:], x1_dram.rearrange("(t p) d -> p t d", p=P)).then_inc(x_loaded, 16)
            for t in range(NT):
                sp.wait_ge(w_ready, t + 1)
                sp.dma_start(cnt[t % 2][:], c_dram[t, :, :].rearrange("p (t d) -> p t d", d=P)
                             ).then_inc(c_loaded[t % 2], 16)

        @block.vector
        def _(dve):
            step = Chain(dve, dve_step)
            dve.sem_inc(w_ready, 2)
            dve.sem_inc(summed, 2)

            def scores(t):
                b = t % 2
                dve.wait_ge(e_ready, t)
                step(dve.tensor_tensor(u[:], al2[:, :, 0:1].to_broadcast([P, NT, P]),
                                       rows[:, 0:1, t * P:(t + 1) * P].to_broadcast([P, NT, P]), ALU.add))
                step(dve.scalar_tensor_tensor(u[:], u[:], SLOPE, u[:], ALU.mult, ALU.max))
                dve.wait_ge(w_ready, t + 1)
                dve.tensor_tensor(e[b][:], u[:], rows[:, 1:2, t * P:(t + 1) * P].to_broadcast([P, NT, P]),
                                  ALU.subtract).then_inc(e_ready, 1)

            def weights(t):
                b = t % 2
                dve.wait_ge(exp_done, t + 1)
                dve.wait_ge(c_loaded[b], 16 * (t // 2 + 1))
                dve.wait_ge(agg, t + 1)
                dve.tensor_tensor(wt[b][:], e[b][:], cnt[b][:], ALU.mult).then_inc(w_ready, 1)

            def add(t):
                b = t % 2
                dve.wait_ge(agg, t + 3)
                dve.wait_ge(summed, t + 1)
                step(dve.tensor_scalar(rden[b][:], Z[b][1][:, 383:384], 1e-16, None, ALU.add))
                step(dve.reciprocal(rden[b][:], rden[b][:]))
                dve.scalar_tensor_tensor(x1[:, t, 0:385], Z[b][0][:], rden[b][:], x1[:, t, 0:385], ALU.mult, ALU.add)
                dve.scalar_tensor_tensor(x1[:, t, 385:D], Z[b][1][:, 0:383], rden[b][:], x1[:, t, 385:D],
                                         ALU.mult, ALU.add).then_inc(summed, 1)

            dve.wait_ge(rows_loaded, 32)
            dve.wait_ge(x_loaded, 16)
            scores(0)
            weights(0)
            for t in range(NT + 1):
                if t + 1 < NT:
                    scores(t + 1)
                if t >= 1:
                    add(t - 1)
                if t + 1 < NT:
                    weights(t + 1)

        @block.scalar
        def _(act):
            for t in range(NT):
                act.wait_ge(e_ready, t + 1)
                act.activation(e[t % 2][:], e[t % 2][:], ACT.Exp).then_inc(exp_done, 1)

        @block.tensor
        def _(pe):
            pe.sem_inc(agg, 2)
            for t in range(NT):
                b = t % 2
                pe.wait_ge(w_ready, t + 3)
                pe.wait_ge(summed, t + 1)
                for j in range(2):
                    for s in range(NT):
                        last = pe.matmul(Z[b][j][:], wt[b][:, s, :], h2[:, s, 385 * j:385 * j + CW[j]],
                                         start=(s == 0), stop=(s == NT - 1))
                last.then_inc(agg, 1)


def route_norm_phase(nc, cx, x1, wg, wge, bg, bge, xn2_dram, ident, lg):
    (stats_done, sqrt_done, xn_ready, turned, ev_d, ev_a, w_loaded, mm, lg_done, zeroed) = (
        cx.sem("rn_" + s) for s in
        ("stats_done", "sqrt_done", "xn_ready", "turned", "ev_d", "ev_a", "w_loaded", "mm", "lg_done", "zeroed"))
    stored = [cx.sem(f"rn_stored{b}") for b in range(2)]
    zstored = cx.sem("rn_zstored")
    dve_step = cx.sem("rn_step")
    L = NG + NE
    with ExitStack() as st:
        stats = sb(nc, st, "rn_stats", [P, NT, 2, 6])
        mv = sb(nc, st, "rn_mv", [P, NT, 2])
        std = sb(nc, st, "rn_std", [P, NT])
        veps = sb(nc, st, "rn_veps", [P, NT])
        tmp = sb(nc, st, "rn_tmp", [P, NT])
        rstd = sb(nc, st, "rn_rstd", [P, NT])
        w = sb(nc, st, "rn_w", [128, KD, L])
        brow = sb(nc, st, "rn_brow", [P, L])
        zero = sb(nc, st, "rn_zero", [SLOT, D])
        xn = [sb(nc, st, f"rn_xn{b}", [P, D]) for b in range(2)]
        xT = [sb(nc, st, f"rn_xT{b}", [128, KD, P]) for b in range(2)]
        T = [[pb(nc, st, f"rn_T{b}{j}", [128, 3, P]) for j in range(2)] for b in range(2)]
        Y = [pb(nc, st, f"rn_Y{b}", [P, L]) for b in range(2)]
        block = st.enter_context(nc.Block())

        @block.sync
        def _(sp):
            sp.dma_start(w[:, :, 0:NG], wg.rearrange("(k p) n -> p k n", p=128)).then_inc(w_loaded, 16)
            sp.dma_start(w[:, :, NG:L], wge.rearrange("(k p) n -> p k n", p=128)).then_inc(w_loaded, 16)
            sp.dma_start(brow[:, 0:NG], bg.partition_broadcast(P)).then_inc(w_loaded, 16)
            sp.dma_start(brow[:, NG:L], bge.rearrange("g e -> (g e)").partition_broadcast(P)).then_inc(w_loaded, 16)
            sp.wait_ge(zeroed, 1)
            sp.dma_start(xn2_dram[N:N + SLOT, :], zero[:]).then_inc(zstored, 16)
            with sp.Fori(0, NT // 2) as i:
                for b in range(2):
                    sp.wait_ge(xn_ready, i * 2 + (b + 1))
                    sp.dma_start(xn2_dram[bass.ds(i * (2 * P) + b * P, P), :], xn[b][:]).then_inc(stored[b], 16)
            sp.wait_ge(zstored, 16)
            for b in range(2):
                sp.wait_ge(stored[b], 16 * (NT // 2))

        @block.gpsimd
        def _(pool):
            pool.memset(zero[:], 0.0).then_inc(zeroed, 1)

        @block.vector
        def _(dve):
            step = Chain(dve, dve_step)
            for t in range(NT):
                for h in range(2):
                    last = dve.bn_stats(stats[:, t, h, :], x1[:, t, h * 384:(h + 1) * 384])
            step(last)
            for t in range(NT):
                last = dve.bn_aggr(mv[:, t, :], stats[:, t, :, :])
            step(last)
            dve.tensor_scalar(veps[:], mv[:, :, 1], EPS, None, ALU.add).then_inc(stats_done, 1)
            dve.wait_ge(sqrt_done, 1)
            refine_rstd(step, dve, rstd[:], std[:], veps[:], tmp[:])
            dve.wait_ge(w_loaded, 64)
            dve.sem_inc(ev_d, 2)
            with dve.Fori(0, NT // 2) as i:
                for b in range(2):
                    dve.wait_ge(turned, i * 2 + (b + 1))
                    dve.wait_ge(stored[b], i * 16)
                    dve.tensor_scalar(xn[b][:], x1[:, bass.ds(i * 2 + b, 1), :],
                                      mv[:, bass.ds(i * 2 + b, 1), 0], rstd[:, bass.ds(i * 2 + b, 1)],
                                      ALU.subtract, ALU.mult).then_inc(xn_ready, 1)
                    dve.wait_ge(turned, i * 2 + (b + 3))
                    dve.wait_ge(mm, i * 2 + (b + 1))
                    dve.tensor_copy(xT[b][:, 0:3, :], T[b][0][:]).then_inc(ev_d, 1)
                    dve.wait_ge(mm, i * 2 + (b + 3))
                    dve.tensor_tensor(lg[:, bass.ds(i * 2 + b, 1), :], Y[b][:].unsqueeze(1), brow[:].unsqueeze(1),
                                      ALU.add).then_inc(lg_done, 1)

        @block.scalar
        def _(act):
            act.sem_inc(ev_a, 2)
            act.wait_ge(stats_done, 1)
            act.activation(std[:], veps[:], ACT.Sqrt).then_inc(sqrt_done, 1)
            with act.Fori(0, NT // 2) as i:
                for b in range(2):
                    act.wait_ge(turned, i * 2 + (b + 3))
                    act.wait_ge(mm, i * 2 + (b + 1))
                    act.activation(xT[b][:, 3:6, :], T[b][1][:], ACT.Copy).then_inc(ev_a, 1)

        @block.tensor
        def _(pe):
            pe.sem_inc(turned, 2)
            pe.sem_inc(mm, 2)
            pe.wait_ge(w_loaded, 64)
            with pe.Fori(0, NT // 2) as i:
                for b in range(2):
                    pe.wait_ge(xn_ready, i * 2 + (b + 1))
                    pe.wait_ge(ev_d, i * 2 + (b + 1))
                    pe.wait_ge(ev_a, i * 2 + (b + 1))
                    for k in range(KD):
                        last = pe.transpose(T[b][k // 3][:, k % 3, :], xn[b][:, k * 128:(k + 1) * 128],
                                            ident[0:P, 0:P])
                    last.then_inc(turned, 1)
                    pe.wait_ge(ev_d, i * 2 + (b + 3))
                    pe.wait_ge(ev_a, i * 2 + (b + 3))
                    pe.wait_ge(lg_done, i * 2)
                    for k in range(KD):
                        last = pe.matmul(Y[b][:], xT[b][:, k, :], w[:, k, :], start=(k == 0), stop=(k == KD - 1))
                    last.then_inc(mm, 1)


def route_phase(nc, cx, lg, x1, b2, out, ident, codes, posm, ntile, tstart):
    (consts, exp_in, exp_out, sel_ready, counted, comb_ready, turned, copied, mm, summed, b2_loaded, stored) = (
        cx.sem("rt_" + s) for s in
        ("consts", "exp_in", "exp_out", "sel_ready", "counted", "comb_ready", "turned", "copied", "mm", "summed",
         "b2_loaded", "stored"))
    pre = cx.sem("rt_pre")
    dve_step = cx.sem("rt_step")
    TG = NT * NG
    with ExitStack() as st:
        gl = sb(nc, st, "rt_gl", [P, NT, NG])
        el = sb(nc, st, "rt_el", [P, TG, EPG])
        tri = sb(nc, st, "rt_tri", [P, EPG, EPG])
        low = sb(nc, st, "rt_low", [P, P])
        ones = sb(nc, st, "rt_ones", [P, P])
        cmp = sb(nc, st, "rt_cmp", [P, TG, EPG, EPG])
        eq = sb(nc, st, "rt_eq", [P, TG, EPG, EPG])
        rank = [sb(nc, st, "rt_rank0", [P, NT, NG]), sb(nc, st, "rt_rank1", [P, TG, EPG])]
        sel = [sb(nc, st, "rt_sel0", [P, NT, NG]), sb(nc, st, "rt_sel1", [P, TG, EPG])]
        mx = [sb(nc, st, "rt_mx0", [P, NT]), sb(nc, st, "rt_mx1", [P, TG])]
        gate = [sb(nc, st, "rt_gate0", [P, NT, NG]), sb(nc, st, "rt_gate1", [P, TG, EPG])]
        comb = sb(nc, st, "rt_comb", [P, TG, EPG])
        sele = sb(nc, st, "rt_sele", [P, TG, EPG])
        rest = sb(nc, st, "rt_rest", [P, TG, EPG])
        cum = sb(nc, st, "rt_cum", [P, NT + 1, NE])
        tot = sb(nc, st, "rt_tot", [P, NT, NE])
        ci = sb(nc, st, "rt_ci", [1, NE], I32)
        cf = sb(nc, st, "rt_cf", [1, 2, NE])
        ip = sb(nc, st, "rt_ip", [P, NT, NE], BF16)
        it = sb(nc, st, "rt_it", [P, NT, NE], BF16)
        b2s = sb(nc, st, "rt_b2", [NE, D])
        cT = sb(nc, st, "rt_cT", [NE, NT, P])
        zero = sb(nc, st, "rt_zero", [SLOT, D])
        PW = pb(nc, st, "rt_PW", [P, NT * NE])
        PT = pb(nc, st, "rt_PT", [P, NT * NE])
        T = [pb(nc, st, f"rt_T{j}", [NE, 4, P]) for j in range(3)]
        Y = [pb(nc, st, f"rt_Y{j}", [P, 384]) for j in range(2)]
        width = [4, 4, 2]
        block = st.enter_context(nc.Block())

        @block.sync
        def _(sp):
            sp.dma_start(b2s[:], b2).then_inc(b2_loaded, 16)
            sp.wait_ge(consts, 8)
            sp.dma_start(out[N:N + SLOT, :], zero[:]).then_inc(stored, 16)
            sp.wait_ge(summed, 2 * NT)
            sp.dma_start(out[0:N, :].rearrange("(t p) d -> p t d", p=P), x1[:]).then_inc(stored, 16)
            sp.wait_ge(stored, 32)

        @block.gpsimd
        def _(pool):
            kw = dict(allow_small_or_imprecise_dtypes=True)
            pool.memset(tri[:], 1.0).then_inc(pre, 1)
            pool.memset(low[:], 1.0).then_inc(pre, 1)
            pool.wait_ge(pre, 2)
            pool.affine_select(out=tri[:], in_=tri[:], compare_op=ALU.is_gt, fill=0.0, base=0,
                               pattern=[[1, EPG], [-1, EPG]], channel_multiplier=0).then_inc(consts, 1)
            pool.affine_select(out=low[:], in_=low[:], compare_op=ALU.is_gt, fill=0.0, base=0,
                               pattern=[[1, P]], channel_multiplier=-1).then_inc(consts, 1)
            pool.memset(ones[:], 1.0).then_inc(consts, 1)
            pool.memset(zero[:], 0.0).then_inc(consts, 1)
            pool.iota(ip[:], [[0, NT * NE]], base=0, channel_multiplier=1, **kw).then_inc(consts, 1)
            pool.iota(it[:], [[1, NT], [0, NE]], base=0, channel_multiplier=0, **kw).then_inc(consts, 1)
            pool.memset(codes[:, :, :, 2:3], 1.0).then_inc(consts, 1)
            pool.memset(cum[:, 0, :], 0.0).then_inc(consts, 1)

        @block.vector
        def _(dve):
            step = Chain(dve, dve_step)
            step(dve.tensor_copy(gl[:], lg[:, :, 0:NG]))
            step(dve.tensor_copy(el[:].rearrange("p (t g) e -> p t (g e)", g=NG), lg[:, :, NG:NG + NE]))
            dve.wait_ge(consts, 8)
            for s, (l, a, n) in enumerate(((gl, NT, NG), (el, TG, EPG))):
                flat = lambda buf: buf[:].rearrange("p a i j -> p (a i j)")[:, 0:a * n * n].rearrange(
                    "p (a i j) -> p a i j", i=n, j=n)
                lj = l[:].unsqueeze(2).to_broadcast([P, a, n, n])
                li = l[:].unsqueeze(3).to_broadcast([P, a, n, n])
                step(dve.tensor_tensor(flat(cmp), lj, li, ALU.is_gt))
                step(dve.tensor_tensor(flat(eq), lj, li, ALU.is_equal))
                step(dve.tensor_tensor(flat(eq), flat(eq), tri[:, 0:n, 0:n].unsqueeze(1).to_broadcast([P, a, n, n]),
                                       ALU.mult))
                step(dve.tensor_tensor(flat(cmp), flat(cmp), flat(eq), ALU.add))
                step(dve.tensor_reduce(rank[s][:], flat(cmp), AX.X, ALU.add))
                step(dve.tensor_scalar(sel[s][:], rank[s][:], 2.0, None, ALU.is_lt))
                step(dve.tensor_reduce(mx[s][:], l[:], AX.X, ALU.max))
                dve.tensor_tensor(gate[s][:], l[:], mx[s][:].unsqueeze(2).to_broadcast([P, a, n]),
                                  ALU.subtract).then_inc(exp_in, 1)
                dve.wait_ge(exp_out, s + 1)
                step(dve.tensor_tensor(gate[s][:], gate[s][:], sel[s][:], ALU.mult))
                step(dve.tensor_reduce(mx[s][:], gate[s][:], AX.X, ALU.add))
                step(dve.reciprocal(mx[s][:], mx[s][:]))
                step(dve.tensor_tensor(gate[s][:], gate[s][:], mx[s][:].unsqueeze(2).to_broadcast([P, a, n]),
                                       ALU.mult))
            g4 = lambda a: a[:].rearrange("p t g -> p (t g)").unsqueeze(2).to_broadcast([P, TG, EPG])
            dve.tensor_tensor(sele[:], sel[1][:], g4(sel[0]), ALU.mult).then_inc(sel_ready, 1)
            dve.tensor_tensor(comb[:], gate[1][:], g4(gate[0]), ALU.mult).then_inc(comb_ready, 1)
            dve.wait_ge(comb_ready, 1)
            c3 = lambda j: codes[:, :, :, j]
            combf = comb[:].rearrange("p (t g) e -> p t (g e)", g=NG)
            restf = rest[:].rearrange("p (t g) e -> p t (g e)", g=NG)
            step(dve.tensor_copy(c3(3), combf))
            step(dve.tensor_tensor(restf, combf, c3(3), ALU.subtract))
            step(dve.tensor_copy(c3(4), restf))
            step(dve.tensor_tensor(c3(5), restf, c3(4), ALU.subtract))
            step(dve.tensor_copy(c3(0), ip[:]))
            step(dve.tensor_copy(c3(1), it[:]))
            dve.wait_ge(counted, 2)
            step(dve.tensor_copy(tot[:].rearrange("p t e -> p (t e)"), PT[:]))
            for t in range(NT):
                step(dve.tensor_tensor(cum[:, t + 1, :], cum[:, t, :], tot[:, t, :], ALU.add))
            step(dve.tensor_tensor(posm[:].rearrange("p t e -> p (t e)"), PW[:],
                                   cum[:, 0:NT, :].rearrange("p t e -> p (t e)"), ALU.add))
            selef = sele[:].rearrange("p (t g) e -> p t (g e)", g=NG)
            step(dve.tensor_scalar(posm[:], posm[:], 1.0, None, ALU.add))
            step(dve.tensor_tensor(posm[:], posm[:], selef, ALU.mult))
            step(dve.tensor_scalar(posm[:], posm[:], -1.0, None, ALU.add))
            step(dve.tensor_scalar(cf[:, 0, :], cum[0:1, NT, :], float(SLOT - 1), None, ALU.add))
            step(dve.tensor_copy(ci[:], cf[:, 0, :]))
            step(dve.tensor_scalar(ci[:], ci[:], SLOT.bit_length() - 1, None, ALU.logical_shift_right))
            step(dve.tensor_copy(cf[:, 0, :], ci[:]))
            step(dve.tensor_scalar(cf[:, 0, :], cf[:, 0, :], 1.0, None, ALU.max))
            step(dve.tensor_copy(ntile[:], cf[:, 0, :]))
            step(dve.tensor_tensor_scan(cf[:, 1, :], ones[0:1, 0:NE], cf[:, 0, :], 0.0, ALU.mult, ALU.add))
            step(dve.tensor_tensor(cf[:, 1, :], cf[:, 1, :], cf[:, 0, :], ALU.subtract))
            step(dve.tensor_copy(tstart[:], cf[:, 1, :]))
            for j in range(3):
                dve.wait_ge(turned, j + 1)
                dve.tensor_copy(cT[:, 4 * j:4 * j + width[j], :], T[j][:, 0:width[j], :]).then_inc(copied, 1)
            for t in range(NT):
                for j in range(2):
                    col = x1[:, t, j * 384:(j + 1) * 384]
                    dve.wait_ge(mm, 2 * t + j + 1)
                    dve.tensor_tensor(col, Y[j][:], col, ALU.add).then_inc(summed, 1)

        @block.scalar
        def _(act):
            for s in range(2):
                act.wait_ge(exp_in, s + 1)
                act.activation(gate[s][:], gate[s][:], ACT.Exp).then_inc(exp_out, 1)

        @block.tensor
        def _(pe):
            pe.wait_ge(sel_ready, 1)
            pe.wait_ge(consts, 8)
            rhs = sele[:].rearrange("p a e -> p (a e)")
            pe.matmul(PW[:], low[:], rhs, start=True, stop=True).then_inc(counted, 1)
            pe.matmul(PT[:], ones[:], rhs, start=True, stop=True).then_inc(counted, 1)
            pe.wait_ge(comb_ready, 1)
            pe.wait_ge(b2_loaded, 16)
            for j in range(3):
                for t in range(width[j]):
                    tt = 4 * j + t
                    last = pe.transpose(T[j][:, t, :], comb[:, tt * NG:(tt + 1) * NG, :].rearrange("p a e -> p (a e)"),
                                        ident[0:P, 0:P])
                last.then_inc(turned, 1)
            pe.wait_ge(copied, 3)
            for t in range(NT):
                for j in range(2):
                    if t >= 1:
                        pe.wait_ge(summed, 2 * (t - 1) + j + 1)
                    pe.matmul(Y[j][:], cT[:, t, :], b2s[:, j * 384:(j + 1) * 384], start=True, stop=True
                              ).then_inc(mm, 1)


def expert_phase(nc, cx, W1, b1, W2, xn2_dram, out, ident, codes, posm, ntile, tstart):
    NB = 4
    (consts, q_ready, ids_done, idx_ready, gathered, x_turned, xT_d, xT_a, gemm1, h_biased, h_gelu, h_turned,
     hT_ready, gemm2, y_d, y_a, added, flat, g_ready) = (
        cx.sem("ex_" + s) for s in
        ("consts", "q_ready", "ids_done", "idx_ready", "gathered", "x_turned", "xT_d", "xT_a", "gemm1", "h_biased",
         "h_gelu", "h_turned", "hT_ready", "gemm2", "y_d", "y_a", "added", "flat", "g_ready"))
    w_loaded = [cx.sem(f"ex_w_loaded{b}") for b in range(NB)]
    passed = cx.sem("ex_passed")
    dve_step = cx.sem("ex_step")
    STEPS = 8
    CONSTS = 11
    with ExitStack() as st:
        w1 = sb(nc, st, "ex_w1", [128, NB, KD, FM])
        w2 = sb(nc, st, "ex_w2", [128, NB, KM, D])
        b1r = sb(nc, st, "ex_b1", [SLOT, NB, FM])
        iot = sb(nc, st, "ex_iota", [P, SLOT])
        pad = sb(nc, st, "ex_pad", [SLOT, 1])
        rel = sb(nc, st, "ex_rel", [P, NT])
        Q = sb(nc, st, "ex_Q", [P, NT, SLOT], BF16)
        cod = sb(nc, st, "ex_cod", [SLOT, 6])
        idf = sb(nc, st, "ex_idf", [SLOT, 2])
        found, waiting, leaving = (sb(nc, st, "ex_" + s, [SLOT, 2]) for s in ("found", "waiting", "leaving"))
        idG = sb(nc, st, "ex_idG", [SLOT, 1], I32)
        idS = sb(nc, st, "ex_idS", [SLOT, 1], I32)
        gS = sb(nc, st, "ex_gS", [SLOT, 1])
        X = sb(nc, st, "ex_X", [SLOT, D])
        xT = sb(nc, st, "ex_xT", [128, KD, SLOT])
        h = sb(nc, st, "ex_h", [SLOT, FM])
        hT = sb(nc, st, "ex_hT", [128, KM, SLOT])
        y = sb(nc, st, "ex_y", [SLOT, D])
        PI = pb(nc, st, "ex_PI", [SLOT, 6])
        TX = [pb(nc, st, f"ex_TX{j}", [128, 3, SLOT]) for j in range(2)]
        PH = pb(nc, st, "ex_PH", [SLOT, FM])
        TH = pb(nc, st, "ex_TH", [128, KM, SLOT])
        PY = [pb(nc, st, f"ex_PY{j}", [SLOT, 384]) for j in range(2)]
        block = st.enter_context(nc.Block())

        def turns(eng, turn, body, enter=None):
            eng.reg_mov(turn, 1)
            with eng.Fori(0, NE // NB) as i:
                for b in range(NB):
                    if enter is not None:
                        enter(i, b)
                    count = eng.value_load(ntile[0:1, bass.ds(i * NB + b, 1)], min_val=1, max_val=NT)
                    with eng.Fori(0, count) as _:
                        body(eng.snap(turn), b)
                        eng.reg_add(turn, turn, 1)
            return eng.snap(turn)

        @block.sync
        def _(sp):
            def load_first(e, b):
                sp.dma_start(w1[:, b, :, :], W1[e, :, :].rearrange("o (k p) n -> p (o k) n", p=128)
                             ).then_inc(w_loaded[b], 16)

            def load_second(e, b):
                sp.dma_start(b1r[:, b, :], b1[e, :].partition_broadcast(SLOT)).then_inc(w_loaded[b], 16)
                sp.dma_start(w2[:, b, :, :], W2[e, :, :].rearrange("o (k p) n -> p (o k) n", p=128)
                             ).then_inc(w_loaded[b], 16)

            for b in range(NB):
                load_first(slice(b, b + 1), b)
                load_second(slice(b, b + 1), b)
            with sp.Fori(1, NE // NB) as i:
                for b in range(NB):
                    done = sp.value_load(tstart[0:1, bass.ds(i * NB + (b + 1 - NB), 1)], min_val=0, max_val=MAXT)
                    sp.wait_ge(gemm1, done + 2)
                    load_first(bass.ds(i * NB + b, 1), b)
                    sp.wait_ge(gemm2, done + 3)
                    load_second(bass.ds(i * NB + b, 1), b)

        @block.gpsimd
        def _(pool):
            kw = dict(allow_small_or_imprecise_dtypes=True)
            pool.iota(iot[:], [[1, SLOT]], base=0, channel_multiplier=0, **kw).then_inc(consts, 1)
            pool.iota(pad[:], [[0, 1]], base=N, channel_multiplier=1, **kw).then_inc(consts, 1)
            for m in (found, waiting, leaving):
                pool.iota(m[:, 0:1], [[0, 1]], base=N, channel_multiplier=1, **kw).then_inc(consts, 1)
                pool.memset(m[:, 1:2], 0.0).then_inc(consts, 1)
            pool.memset(X[:], 0.0).then_inc(consts, 1)
            pool.memset(h[:], 0.0).then_inc(consts, 1)
            pool.memset(hT[:], 0.0).then_inc(consts, 1)
            pool.wait_ge(consts, CONSTS)

            def scatter(n):
                pool.wait_ge(y_d, n)
                pool.wait_ge(y_a, n)
                pool.sem_inc(passed, 1)
                pool.indirect_dma_start(out, bass.IndirectOffsetOnAxis(ap=idS[:, 0:1], axis=0), y[:], None,
                                        compute_op=ALU.add).then_inc(added, 16)

            def body(n, b):
                scatter(n)
                pool.wait_ge(idx_ready, n)
                pool.wait_ge(x_turned, n)
                pool.sem_inc(passed, 1)
                pool.indirect_dma_start(X[:], None, xn2_dram, bass.IndirectOffsetOnAxis(ap=idG[:, 0:1], axis=0)
                                        ).then_inc(gathered, 16)

            with pool.register("ex_turn_pool") as turn:
                end = turns(pool, turn, body)
                for k in range(3):
                    scatter(end + k)
                pool.wait_ge(added, (end + 2) * 16)

        @block.vector
        def _(dve):
            def steps(n):
                state = [0]

                def step(ins):
                    state[0] += 1
                    ins.then_inc(dve_step, 1)
                    dve.wait_ge(dve_step, n * STEPS + (state[0] - STEPS))
                return step, state

            def turn_x(n):
                dve.wait_ge(x_turned, n)
                dve.wait_ge(gemm1, n)
                dve.tensor_copy(xT[:, 0:3, :], TX[0][:]).then_inc(xT_d, 1)

            def turn_h(n):
                dve.wait_ge(h_turned, n)
                dve.wait_ge(gemm2, n)
                dve.tensor_copy(hT[:], TH[:]).then_inc(hT_ready, 1)

            def find(step, n):
                dve.wait_ge(ids_done, n + 1)
                step(dve.tensor_copy(cod[:], PI[:]))
                step(dve.tensor_copy(waiting[:], found[:]))
                step(dve.scalar_tensor_tensor(idf[:, 0:1], cod[:, 1:2], float(P), cod[:, 0:1], ALU.mult, ALU.add))
                step(dve.scalar_tensor_tensor(idf[:, 1:2], cod[:, 2:3], -1.0, pad[:], ALU.add, ALU.mult))
                step(dve.scalar_tensor_tensor(found[:, 1:2], cod[:, 5:6], cod[:, 4:5], cod[:, 3:4], ALU.add, ALU.add))
                step(dve.tensor_tensor(found[:, 0:1], idf[:, 0:1], idf[:, 1:2], ALU.subtract))
                dve.wait_ge(gathered, n * 16 - 16)
                dve.tensor_copy(idG[:], found[:, 0:1]).then_inc(idx_ready, 1)

            def second(n, step=None, then=None):
                dve.wait_ge(added, n * 16 - 16)
                dve.tensor_copy(idS[:], leaving[:, 0:1])
                dve.tensor_copy(gS[:], leaving[:, 1:2]).then_inc(g_ready, 1)
                dve.wait_ge(g_ready, n)
                if then is not None:
                    step(dve.tensor_copy(leaving[:], then[:]))
                dve.wait_ge(gemm2, n)
                dve.tensor_scalar(y[:, 0:384], PY[0][:], gS[:], None, ALU.mult).then_inc(y_d, 1)

            def bias(n, b_prev):
                dve.wait_ge(gemm1, n + 1)
                dve.wait_ge(h_turned, n)
                dve.tensor_tensor(h[:].unsqueeze(1), PH[:].unsqueeze(1), b1r[:, bass.ds(b_prev, 1), :], ALU.add
                                  ).then_inc(h_biased, 1)

            dve.wait_ge(consts, CONSTS)
            with dve.register("ex_b_prev") as b_prev, dve.register("ex_turn_dve") as turn:
                dve.reg_mov(b_prev, 0)

                def enter(i, b):
                    dve.wait_ge(w_loaded[b], i * 48 + 48)
                    dve.tensor_copy(rel[:], posm[:, :, bass.ds(i * NB + b, 1)].rearrange("p t o -> p (t o)")
                                    ).then_inc(flat, 1)
                    dve.wait_ge(flat, i * NB + (b + 1))

                def body(n, b):
                    step, state = steps(n)
                    dve.wait_ge(ids_done, n)
                    dve.tensor_tensor(Q[:], rel[:].unsqueeze(2).to_broadcast([P, NT, SLOT]),
                                      iot[:].unsqueeze(1).to_broadcast([P, NT, SLOT]), ALU.is_equal
                                      ).then_inc(q_ready, 1)
                    second(n, step, waiting)
                    turn_h(n)
                    turn_x(n)
                    dve.wait_ge(q_ready, n)
                    step(dve.tensor_scalar(rel[:], rel[:], -float(SLOT), None, ALU.add))
                    find(step, n)
                    bias(n, dve.snap(b_prev))
                    assert state[0] == STEPS
                    dve.reg_mov(b_prev, b)

                end = turns(dve, turn, body, enter)
                last = dve.snap(b_prev)
                step, state = steps(end)
                second(end, step, waiting)
                turn_h(end)
                turn_x(end)
                bias(end, last)
                second(end + 1, step, found)
                turn_h(end + 1)
                second(end + 2)

        @block.scalar
        def _(act):
            def turn_x(n):
                act.wait_ge(x_turned, n)
                act.wait_ge(gemm1, n)
                act.activation(xT[:, 3:6, :], TX[1][:], ACT.Copy).then_inc(xT_a, 1)

            def second(n):
                act.wait_ge(gemm2, n)
                act.wait_ge(g_ready, n)
                act.activation(y[:, 384:768], PY[1][:], ACT.Copy, scale=gS[:]).then_inc(y_a, 1)

            def gelu(n):
                act.wait_ge(h_biased, n)
                act.activation(h[:], h[:], ACT.Gelu).then_inc(h_gelu, 1)

            act.wait_ge(consts, CONSTS)

            def body(n, b):
                second(n)
                turn_x(n)
                gelu(n)

            with act.register("ex_turn_act") as turn:
                end = turns(act, turn, body)
                body(end, None)
                second(end + 1)
                second(end + 2)

        @block.tensor
        def _(pe):
            pe.wait_ge(consts, CONSTS)

            def find(n, e):
                pe.wait_ge(q_ready, n)
                pe.wait_ge(idx_ready, n - 1)
                for t in range(NT):
                    last = pe.matmul(PI[:], Q[:, t, :], codes[:, t, bass.ds(e, 1), :].rearrange("p o c -> p (o c)"),
                                     start=(t == 0), stop=(t == NT - 1))
                last.then_inc(ids_done, 1)

            def turn_x(n):
                pe.wait_ge(gathered, n * 16 - 16)
                pe.wait_ge(xT_d, n - 1)
                pe.wait_ge(xT_a, n - 1)
                for k in range(KD):
                    last = pe.transpose(TX[k // 3][:, k % 3, :], X[:, k * 128:(k + 1) * 128], ident[:])
                last.then_inc(x_turned, 1)

            def turn_h(n):
                if n is not None:
                    pe.wait_ge(h_gelu, n)
                    pe.wait_ge(hT_ready, n)
                for k in range(KM):
                    last = pe.transpose(TH[:, k, :], h[:, k * 128:(k + 1) * 128], ident[:])
                last.then_inc(h_turned, 1)

            def second(n, b):
                if n is not None:
                    pe.wait_ge(hT_ready, n)
                    pe.wait_ge(y_d, n)
                    pe.wait_ge(y_a, n)
                for j in range(2):
                    for k in range(KM):
                        last = pe.matmul(PY[j][:], hT[:, k, :], w2[:, bass.ds(b, 1), k, j * 384:(j + 1) * 384],
                                         start=(k == 0), stop=(k == KM - 1))
                last.then_inc(gemm2, 1)

            def first(n, b):
                pe.wait_ge(xT_d, n)
                pe.wait_ge(xT_a, n)
                pe.wait_ge(h_biased, n - 1)
                for k in range(KD):
                    last = pe.matmul(PH[:], xT[:, k, :], w1[:, bass.ds(b, 1), k, :], start=(k == 0),
                                     stop=(k == KD - 1))
                last.then_inc(gemm1, 1)

            pe.sem_inc(ids_done, 1)
            pe.sem_inc(gemm1, 1)
            with pe.register("ex_b1_prev") as b1_prev, pe.register("ex_b2_prev") as b2_prev, \
                    pe.register("ex_turn_pe") as turn:
                pe.reg_mov(b1_prev, 0)
                pe.reg_mov(b2_prev, 0)
                expert = [None]
                pe.wait_ge(w_loaded[0], 48)
                second(None, 0)
                turn_h(None)

                def enter(i, b):
                    pe.wait_ge(w_loaded[b], i * 48 + 48)
                    expert[0] = i * NB + b

                def body(n, b):
                    turn_x(n)
                    find(n, expert[0])
                    first(n, pe.snap(b1_prev))
                    second(n, pe.snap(b2_prev))
                    turn_h(n)
                    pe.reg_mov(b2_prev, pe.snap(b1_prev))
                    pe.reg_mov(b1_prev, b)

                end = turns(pe, turn, body, enter)
                turn_x(end)
                first(end, pe.snap(b1_prev))
                second(end, pe.snap(b2_prev))
                turn_h(end)
                second(end + 1, pe.snap(b1_prev))


def host_layout(i):
    import numpy as np
    o = dict(i)
    for name in ("L0_mix_qkv_w", "L0_mix_proj_w", "L0_mix_rf"):
        o[name] = np.ascontiguousarray(np.asarray(i[name]).T)
    o["L0_ffn_Wge"] = np.asarray(i["L0_ffn_Wge"]).transpose(1, 0, 2).reshape(D, NE)
    return {k: np.ascontiguousarray(v) for k, v in o.items()}


def build(nc, ins, out, stages=99):
    x = ins["x"]
    dram = lambda name, *shape: nc.dram_tensor(name, shape, F32).ap()
    with ExitStack() as st:
        cx = Ctx(nc)
        x1_dram = dram("x1_dram", N, D)
        alT_dram = dram("alT_dram", 2 * H1, N)
        mT_dram = dram("mT_dram", H1, N)
        al2T_dram = dram("al2T_dram", 2, N)
        m2T_dram = dram("m2T_dram", 1, N)
        ct_dram = dram("ct_dram", NW * 128, SLO)
        c_dram = dram("c_dram", NT, P, N)
        mask_dram = dram("mask_dram", NT, P, N)
        h1T_dram = dram("h1T_dram", NT, 128, KF * P)
        ident = sb(nc, st, "ident", [128, 128])
        with ExitStack() as st1:
            xnT = sb(nc, st1, "xnT", [128, KD, N])
            norm_phase(nc, cx, x, ident, xnT)
            if stages == 1:
                return
            if stages != 5:
              with ExitStack() as st2:
                attn = sb(nc, st2, "attn", [P, NT, D])
                for half in range(2):
                    mix_half_phase(nc, cx, half, ins["L0_mix_qkv_w"], ins["L0_mix_qkv_b"], ins["L0_mix_rf"], xnT,
                                   ident, None, attn)
                proj_phase(nc, cx, attn, ins["L0_mix_proj_w"], ins["L0_mix_proj_b"], ins["L0_gnn_b2"], x, x1_dram,
                           ident)
            if stages == 3:
                return
            al = sb(nc, st1, "al", [P, NT, 2 * H1])
            h = sb(nc, st1, "h", [P, NT, H1, C1 + 1])
            with ExitStack() as st2:
                w1 = sb(nc, st2, "gnn_w1", [128, KD, F1])
                logits_phase(nc, cx, ins["L0_gnn_W1"], ins["L0_gnn_att_src1"], ins["L0_gnn_att_dst1"], xnT, ident, w1,
                             al, alT_dram)
                keyT = sb(nc, st2, "keyT", [128, EROWS])
                sloT = sb(nc, st2, "sloT", [128, EROWS])
                spans = sb(nc, st2, "spans", [1, 2 * NW], I32)
                edge_table_phase(nc, cx, ins["src"], ins["dst"], ident, keyT, sloT, spans)
                count_phase(nc, cx, keyT, sloT, spans, ct_dram, xnT, w1, h)
            mask_phase(nc, cx, ct_dram, c_dram, mask_dram, alT_dram, ident, al, mT_dram)
            if stages == 4:
                return
            cx.clear()
            gat1_phase(nc, cx, ins["L0_gnn_b1"], h, al, alT_dram, mT_dram, c_dram, h1T_dram, ident)
        x1 = sb(nc, st, "x1", [P, NT, D])
        with ExitStack() as st1:
            h2 = sb(nc, st1, "h2", [P, NT, D + 1])
            al2 = sb(nc, st1, "al2", [P, NT, 2])
            gat2_project_phase(nc, cx, ins["L0_gnn_W2"], ins["L0_gnn_att_src2"], ins["L0_gnn_att_dst2"], h1T_dram,
                               ident, h2, al2, al2T_dram)
            gat2_max_phase(nc, cx, mask_dram, al2, al2T_dram, m2T_dram, ident)
            if stages == 5:
                return
            gat2_phase(nc, cx, al2, al2T_dram, m2T_dram, c_dram, h2, x1_dram, x1)
        if stages == 6:
            return
        xn2_dram = dram("xn2_dram", N + SLOT, D)
        codes = sb(nc, st, "codes", [P, NT, NE, 6], BF16)
        posm = sb(nc, st, "posm", [P, NT, NE])
        ntile = sb(nc, st, "ntile", [1, NE], I32)
        tstart = sb(nc, st, "tstart", [1, NE], I32)
        lg = sb(nc, st, "lg", [P, NT, NG + NE])
        route_norm_phase(nc, cx, x1, ins["L0_ffn_Wg"], ins["L0_ffn_Wge"], ins["L0_ffn_bg"], ins["L0_ffn_bge"],
                         xn2_dram, ident, lg)
        route_phase(nc, cx, lg, x1, ins["L0_ffn_b2"], out, ident, codes, posm, ntile, tstart)
        if stages == 7:
            return
        expert_phase(nc, cx, ins["L0_ffn_W1"], ins["L0_ffn_b1"], ins["L0_ffn_W2"], xn2_dram, out, ident, codes, posm,
                     ntile, tstart)


def kernel(**inputs):
    import concourse.bacc as bacc
    from concourse.bass_utils import run_bass_kernel_spmd

    nc = bacc.Bacc("TRN2", target_bir_lowering=False, num_devices=1)
    arrays = host_layout(inputs)
    ins = {k: nc.dram_tensor(f"in_{k}", a.shape, mybir.dt.from_np(a.dtype), kind="ExternalInput").ap()
           for k, a in arrays.items()}
    out = nc.dram_tensor("out_rows", (N + SLOT, D), F32, kind="ExternalOutput").ap()
    build(nc, ins, out)
    r = run_bass_kernel_spmd(nc, [{f"in_{k}": a for k, a in arrays.items()}], core_ids=[0])
    return r.results[0]["out_rows"][0:N]
```

```python
from contextlib import ExitStack

import concourse.bass as bass
from concourse import mybir

F32 = mybir.dt.float32
F16 = mybir.dt.float16
BF16 = mybir.dt.bfloat16
I32 = mybir.dt.int32
U32 = mybir.dt.uint32
ALU = mybir.AluOpType
ACT = mybir.ActivationFunctionType
AX = mybir.AxisListType

N = 1250
NT = 10
P = N // NT
D = 768
KD = D // 128
H1 = 4
C1 = 512
F1 = H1 * C1
KF = F1 // 128
CH = 3
CHW = [416, 416, 418]
CHO = [0, 416, 832]
EDGES = 41250
ER = 128
RB = 4
EROWS = 324
EG = 3
EGP = EROWS // EG
WIN = 32
NW = 40
SPLIT = 4
SLO = 314
CTW = SPLIT * SLO
PADNODE = NW * WIN - 1
BIG = 1.0e30
MH = 8
MD = D // MH
RF = 256
NE = 32
NG = 4
EPG = NE // NG
FM = 384
KM = FM // 128
SLOT = 128
MAXT = (4 * N + NE * (SLOT - 1)) // SLOT + NE // 4
SLOPE = 0.2
EPS = 1e-5


class Chain:

    def __init__(self, eng, sem):
        self.eng, self.sem, self.base, self.i, self.per, self.j = eng, sem, 0, 0, 0, 0

    def start(self, i, per):
        self.i, self.per, self.j = i, per, 0

    def end(self, count):
        assert self.j == self.per, (self.j, self.per)
        self.base += count * self.per
        self.i, self.per, self.j = 0, 0, 0

    def __call__(self, ins):
        self.j += 1
        ins.then_inc(self.sem, 1)
        self.eng.wait_ge(self.sem, self.i * self.per + (self.base + self.j))

    def flat_end(self):
        self.base += self.j
        self.j = 0


class Ctx:

    def __init__(self, nc):
        self.nc, self.sems = nc, []

    def sem(self, name):
        self.sems.append(self.nc.alloc_semaphore(name=name))
        return self.sems[-1]

    def clear(self):
        self.nc.clear_and_free_semaphores(self.sems)
        self.sems = []
        with self.nc.Block():
            pass


def sb(nc, st, name, shape, dt=F32):
    return st.enter_context(nc.sbuf_tensor(name, shape, dt))


def pb(nc, st, name, shape, dt=F32):
    return st.enter_context(nc.psum_tensor(name, shape, dt))


def refine_rstd(step, dve, rstd, std, veps, tmp):
    step(dve.reciprocal(rstd, std))
    step(dve.tensor_tensor(tmp, rstd, rstd, ALU.mult))
    step(dve.tensor_tensor(tmp, tmp, veps, ALU.mult))
    step(dve.tensor_scalar(tmp, tmp, -0.5, 1.5, ALU.mult, ALU.add))
    step(dve.tensor_tensor(rstd, rstd, tmp, ALU.mult))


def norm_phase(nc, cx, x, ident, xnT, load_next):
    x_loaded = [cx.sem(f"norm_x_loaded{h}") for h in range(2)]
    stats_done, sqrt_done, xn_ready, transposed, used_dve, used_act, id_done = (
        cx.sem(f"norm_{s}") for s in
        ("stats_done", "sqrt_done", "xn_ready", "transposed", "used_dve", "used_act", "id_done"))
    dve_step = cx.sem("norm_dve_step")
    HT = NT // 2
    with ExitStack() as st:
        xa = sb(nc, st, "xa", [P, NT, D])
        stats = sb(nc, st, "stats", [P, NT, 2, 6])
        mv = sb(nc, st, "mv", [P, NT, 2])
        std = sb(nc, st, "std", [P, NT])
        veps = sb(nc, st, "veps", [P, NT])
        tmp = sb(nc, st, "tmp", [P, NT])
        rstd = sb(nc, st, "rstd", [P, NT])
        xn = [sb(nc, st, f"xn{b}", [P, D]) for b in range(2)]
        tp = [[pb(nc, st, f"tp{b}{h}", [128, 3, P]) for h in range(2)] for b in range(2)]
        block = st.enter_context(nc.Block())

        @block.sync
        def _(sp):
            for h in range(2):
                sp.dma_start(xa[:, h * HT:(h + 1) * HT, :], x.rearrange("(t p) d -> p t d", p=P)
                             [:, h * HT:(h + 1) * HT, :]).then_inc(x_loaded[h], 16)
            load_next(sp)

        @block.gpsimd
        def _(pool):
            pool.memset(ident[:], 0.0).then_inc(id_done, 1)
            pool.wait_ge(id_done, 1)
            pool.affine_select(out=ident[:], in_=ident[:], compare_op=ALU.not_equal, fill=1.0, base=0,
                               pattern=[[-1, 128]], channel_multiplier=1).then_inc(id_done, 1)

        @block.vector
        def _(dve):
            step = Chain(dve, dve_step)
            for t in range(NT):
                if t % HT == 0:
                    dve.wait_ge(x_loaded[t // HT], 16)
                for h in range(2):
                    last = dve.bn_stats(stats[:, t, h, :], xa[:, t, h * 384:(h + 1) * 384])
            step(last)
            for t in range(NT):
                last = dve.bn_aggr(mv[:, t, :], stats[:, t, :, :])
            step(last)
            dve.tensor_scalar(veps[:], mv[:, :, 1], EPS, None, ALU.add).then_inc(stats_done, 1)
            dve.wait_ge(sqrt_done, 1)
            refine_rstd(step, dve, rstd[:], std[:], veps[:], tmp[:])
            step.flat_end()

            def scaled(t, b):
                dve.wait_ge(transposed, t + 1)
                dve.tensor_scalar(xn[b][:], xa[:, bass.ds(t, 1), :], mv[:, bass.ds(t, 1), 0],
                                  rstd[:, bass.ds(t, 1)], ALU.subtract, ALU.mult).then_inc(xn_ready, 1)

            def copy(t, b):
                dve.wait_ge(transposed, t + 3)
                dve.tensor_copy(xnT[:, 0:3, bass.ds(t * P, P)], tp[b][0][:]).then_inc(used_dve, 1)

            scaled(0, 0)
            with dve.Fori(0, NT // 2 - 1) as i:
                for b in range(2):
                    scaled(i * 2 + (b + 1), 1 - b)
                    copy(i * 2 + b, b)
            scaled(NT - 1, 1)
            copy(NT - 2, 0)
            copy(NT - 1, 1)

        @block.scalar
        def _(act):
            act.wait_ge(stats_done, 1)
            act.activation(std[:], veps[:], ACT.Sqrt).then_inc(sqrt_done, 1)
            with act.Fori(0, NT // 2) as i:
                for b in range(2):
                    act.wait_ge(transposed, i * 2 + (b + 3))
                    act.activation(xnT[:, 3:6, bass.ds(i * (2 * P) + b * P, P)], tp[b][1][:],
                                   ACT.Copy).then_inc(used_act, 1)

        @block.tensor
        def _(pe):
            pe.sem_inc(transposed, 2)
            pe.sem_inc(used_dve, 2)
            pe.sem_inc(used_act, 2)
            pe.wait_ge(id_done, 2)
            with pe.Fori(0, NT // 2) as i:
                for b in range(2):
                    pe.wait_ge(xn_ready, i * 2 + (b + 1))
                    pe.wait_ge(used_dve, i * 2 + (b + 1))
                    pe.wait_ge(used_act, i * 2 + (b + 1))
                    for k in range(KD):
                        last = pe.transpose(tp[b][k // 3][:, k % 3, :], xn[b][:, k * 128:(k + 1) * 128],
                                            ident[0:P, 0:P])
                    last.then_inc(transposed, 1)


def numerator(nc, cx, tag, half, rfT, qT, kv, attn, a_loaded, slice_loaded, ws, ab, wa, load_next):
    KH = KD // 2
    HH, A, HT = MH // 2, MD + 1, NT // 2
    feat, exped, num, num_used = (cx.sem(tag + s) for s in ("feat", "exped", "num", "num_used"))
    dve_step = cx.sem(tag + "num_step")
    wa_step = cx.sem(tag + "wa_step")
    with ExitStack() as st:
        junk = sb(nc, st, tag + "junk", [128, 2, C1])
        phiq = [sb(nc, st, tag + f"phiq{b}", [128, 2, N]) for b in range(2)]
        den = sb(nc, st, tag + "den", [P, 2, HT])
        F = [pb(nc, st, tag + f"F{j}", [128, 512]) for j in range(6)]
        R = [pb(nc, st, tag + f"R{j}", [P, HT, A]) for j in range(2)]
        block = st.enter_context(nc.Block())

        @block.sync
        def _(sp):
            load_next(sp)

        @block.tensor
        def _(pe):
            pe.sem_inc(num, 4)
            with pe.Fori(0, HH // 2) as i:
                for b in range(2):
                    for j in range(6):
                        m, c = j // CH, j % CH
                        pe.wait_ge(exped, i * 12 + (6 * b + j + 1))
                        pe.matmul(F[j][:, 0:CHW[c]], rfT[:, m * 128:(m + 1) * 128],
                                  qT[:, bass.ds(i * 2 + b, 1), CHO[c]:CHO[c] + CHW[c]],
                                  start=True, stop=True).then_inc(feat, 1)
                for b in range(2):
                    pe.wait_ge(exped, i * 12 + (6 * b + 12))
                    for j in range(2):
                        pe.wait_ge(num_used, i * 4 + (2 * b + j + 1))
                        for t in range(HT):
                            tt = j * HT + t
                            for m in range(2):
                                last = pe.matmul(R[j][:, t, :], phiq[b][:, m, tt * P:(tt + 1) * P],
                                                 kv[:, bass.ds(i * 2 + b, 1), m, :], start=(m == 0), stop=(m == 1),
                                                 skip_group_check=True)
                        last.then_inc(num, 1)

        @block.scalar
        def _(act):
            act.sem_inc(exped, 6)
            with act.Fori(0, HH // 2) as i:
                for b in range(2):
                    act.wait_ge(num, i * 4 + (2 * b + 2))
                    for j in range(6):
                        m, c = j // CH, j % CH
                        act.wait_ge(feat, i * 12 + (6 * b + j + 1))
                        act.activation(phiq[b][:, m, CHO[c]:CHO[c] + CHW[c]], F[j][:, 0:CHW[c]],
                                       ACT.Exp).then_inc(exped, 1)

        @block.vector
        def _(dve):
            step = Chain(dve, dve_step)
            dve.wait_ge(a_loaded, 32)
            n = 0
            for k in range(KH):
                dve.wait_ge(slice_loaded[k], 16)
                for s in range(2):
                    for h in range(H1):
                        if n >= 2:
                            dve.wait_ge(wa_step, n - 1)
                        col = s * H1 + h
                        dve.tensor_tensor_reduce(out=junk[:, n % 2, :], in0=ws[k][:, h * C1:(h + 1) * C1],
                                                 in1=ab[:, s, h * C1:(h + 1) * C1], scale=1.0, scalar=0.0,
                                                 op0=ALU.mult, op1=ALU.add,
                                                 accum_out=wa[:, half * KH + k, col:col + 1]).then_inc(wa_step, 1)
                        n += 1
            dve.sem_inc(num_used, 2)
            with dve.Fori(0, HH // 2) as i:
                step.start(i, 8)
                for b in range(2):
                    for j in range(2):
                        dve.wait_ge(num, i * 4 + (2 * b + j + 5))
                        dve.wait_ge(num_used, i * 4 + (2 * b + j + 1))
                        step(dve.tensor_scalar(den[:, j, :], R[j][:, :, MD], 1e-6, None, ALU.max))
                        step(dve.reciprocal(den[:, j, :], den[:, j, :]))
                        dve.tensor_tensor(attn[:, j * HT:(j + 1) * HT, bass.ds((i * 2 + b) * MD + half * HH * MD, MD)],
                                          R[j][:, :, 0:MD], den[:, j, :].unsqueeze(2).to_broadcast([P, HT, MD]),
                                          ALU.mult).then_inc(num_used, 1)
            step.end(HH // 2)


def proj_phase(nc, cx, attn, w, w_loaded, proj_b, gnn_b2, x, x1_dram, ident):
    (loaded, x_loaded, staged, turned, copied_a, copied_d, projected, summed, stored, stores) = (
        cx.sem("proj_" + s) for s in ("loaded", "x_loaded", "staged", "turned", "copied_a", "copied_d", "projected",
                                      "summed", "stored", "stores"))
    dve_step = cx.sem("proj_step")
    with ExitStack() as st:
        bias = sb(nc, st, "proj_bias", [P, 2, D])
        xr = sb(nc, st, "proj_x", [P, NT, D])
        at = sb(nc, st, "proj_at", [P, D])
        aT = [sb(nc, st, f"proj_aT{b}", [128, KD, P]) for b in range(2)]
        TP = [pb(nc, st, f"proj_T{j}", [128, 3, P]) for j in range(2)]
        Y = [pb(nc, st, f"proj_Y{j}", [P, 384]) for j in range(2)]
        block = st.enter_context(nc.Block())

        @block.sync
        def _(sp):
            sp.dma_start(bias[:, 0, :], proj_b.partition_broadcast(P)).then_inc(loaded, 16)
            sp.dma_start(bias[:, 1, :], gnn_b2.partition_broadcast(P)).then_inc(loaded, 16)
            sp.dma_start(xr[:], x.rearrange("(t p) d -> p t d", p=P)).then_inc(x_loaded, 16)
            sp.wait_ge(summed, 2 * NT)
            sp.dma_start(x1_dram.rearrange("(t p) d -> p t d", p=P), xr[:]).then_inc(stores, 16)
            sp.wait_ge(stores, 16)

        @block.gpsimd
        def _(pool):
            with pool.Fori(0, NT) as t:
                pool.wait_ge(turned, t + 1)
                pool.tensor_copy(at[:], attn[:, bass.ds(t, 1), :]).then_inc(staged, 1)

        @block.tensor
        def _(pe):
            pe.sem_inc(turned, 1)
            pe.sem_inc(projected, 4)

            def turn(t):
                pe.wait_ge(staged, t + 1)
                pe.wait_ge(copied_a, t + 1)
                pe.wait_ge(copied_d, t + 1)
                for k in range(KD):
                    last = pe.transpose(TP[k // 3][:, k % 3, :], at[:, k * 128:(k + 1) * 128], ident[0:P, 0:P])
                last.then_inc(turned, 1)

            def project(t, b):
                pe.wait_ge(copied_a, t + 2)
                pe.wait_ge(copied_d, t + 2)
                for j in range(2):
                    pe.wait_ge(stored, 2 * t + (j + 1))
                    for k in range(KD):
                        last = pe.matmul(Y[j][:], aT[b][:, k, :], w[:, k, j * 384:(j + 1) * 384],
                                         start=(k == 0), stop=(k == KD - 1))
                    last.then_inc(projected, 1)

            pe.wait_ge(w_loaded, 16)
            turn(0)
            with pe.Fori(0, NT // 2 - 1) as i:
                for b in range(2):
                    turn(i * 2 + (b + 1))
                    project(i * 2 + b, b)
            turn(NT - 1)
            project(NT - 2, 0)
            project(NT - 1, 1)

        @block.scalar
        def _(act):
            act.sem_inc(copied_a, 1)
            with act.Fori(0, NT // 2) as i:
                for b in range(2):
                    act.wait_ge(turned, i * 2 + (b + 2))
                    act.wait_ge(projected, i * 4 + (2 * b + 2))
                    act.activation(aT[b][:, 0:3, :], TP[0][:], ACT.Copy).then_inc(copied_a, 1)

        @block.vector
        def _(dve):
            step = Chain(dve, dve_step)
            dve.sem_inc(copied_d, 1)
            dve.sem_inc(stored, 2)
            dve.wait_ge(loaded, 32)
            dve.wait_ge(x_loaded, 16)
            step(dve.tensor_tensor(bias[:, 0, :], bias[:, 0, :], bias[:, 1, :], ALU.add))

            def turn(t, b):
                dve.wait_ge(turned, t + 2)
                dve.wait_ge(projected, 2 * t + 2)
                dve.tensor_copy(aT[b][:, 3:6, :], TP[1][:]).then_inc(copied_d, 1)

            def add(t):
                for j in range(2):
                    dve.wait_ge(projected, 2 * t + (j + 5))
                    col = xr[:, bass.ds(t, 1), j * 384:(j + 1) * 384]
                    dve.tensor_tensor(col, Y[j][:].unsqueeze(1), col, ALU.add).then_inc(stored, 1)

            turn(0, 0)
            step(dve.tensor_tensor(xr[:], xr[:], bias[:, 0:1, :].to_broadcast([P, NT, D]), ALU.add))
            with dve.Fori(0, NT // 2 - 1) as i:
                for b in range(2):
                    turn(i * 2 + (b + 1), 1 - b)
                    add(i * 2 + b)
            turn(NT - 1, 1)
            for t in range(NT - 2, NT):
                for j in range(2):
                    dve.wait_ge(projected, 2 * t + j + 5)
                    col = xr[:, t, j * 384:(j + 1) * 384]
                    dve.tensor_tensor(col, Y[j][:], col, ALU.add).then_inc(stored, 1)
            dve.drain().then_inc(summed, 2 * NT)


def load_mix_weights(sp, half, wqkvT, qkv_b, w, brow, w_loaded):
    HW = D // 2
    for c in range(3):
        cols = slice(c * D + half * HW, c * D + (half + 1) * HW)
        sp.dma_start(w[:, :, c, :], wqkvT[:, cols].rearrange("(k p) n -> p k n", p=128)).then_inc(w_loaded, 16)
        sp.dma_start(brow[:, c, :], qkv_b[cols].partition_broadcast(P)).then_inc(w_loaded, 16)


def mix_half_phase(nc, cx, half, rfT_dram, xnT, ident, w, brow, w_loaded, attn, gnn_w1, a_src, a_dst, wa, load_next):
    HH = MH // 2
    HW = HH * MD
    A = MD + 1
    SCALE = MD ** -0.5
    tag = f"mix{half}_"
    (rf_loaded, staged, q_done, k_done, v_done, q_evac, k_evac, v_evac, qsq, ksq, q_ready, k_ready, q_turned,
     k_turned, qT_done, kT_done, phi_a, phi_b, exp_a, exp_b, kv_step, kv_copied, consts) = (
        cx.sem(tag + s) for s in
        ("rf_loaded", "staged", "q_done", "k_done", "v_done", "q_evac", "k_evac", "v_evac", "qsq", "ksq", "q_ready",
         "k_ready", "q_turned", "k_turned", "qT_done", "kT_done", "phi_a", "phi_b", "exp_a", "exp_b", "kv_step",
         "kv_copied", "consts"))
    dve_step = cx.sem(tag + "dve_step")
    a_loaded = cx.sem(tag + "a_loaded")
    slice_loaded = [cx.sem(tag + f"slice_loaded{k}") for k in range(KD // 2)]
    with ExitStack() as st:
        rfT = sb(nc, st, tag + "rfT", [A, RF])
        qT = sb(nc, st, tag + "qT", [A, HH, N])
        kv = sb(nc, st, tag + "kv", [128, HH, 2, A])
        ws = [sb(nc, st, tag + f"w1_slice{k}", [128, F1]) for k in range(KD // 2)]
        ab = sb(nc, st, tag + "a", [128, 2, F1])
        with ExitStack() as st1:
            xs = sb(nc, st1, tag + "xs", [128, KD, P])
            qs = sb(nc, st1, tag + "qs", [P, 2, HH, A])
            sq = sb(nc, st1, tag + "sq", [P, 2, HH, MD])
            nrm = sb(nc, st1, tag + "nrm", [P, 2, HH])
            vs = sb(nc, st1, tag + "vs", [P, HH, A])
            kT = sb(nc, st1, tag + "kT", [A, HH, P])
            phik = sb(nc, st1, tag + "phik", [P, HH, RF])
            zero = sb(nc, st1, tag + "zero", [P, 128])
            G = [pb(nc, st1, tag + f"G{j}", [P, HW]) for j in range(3)]
            TQ = pb(nc, st1, tag + "TQ", [A, HH, P])
            PH = [pb(nc, st1, tag + f"PH{j}", [P, 2, RF]) for j in range(2)]
            KV = [pb(nc, st1, tag + f"KV{j}", [128, 2, 2, A]) for j in range(2)]
            block = st1.enter_context(nc.Block())

            @block.sync
            def _(sp):
                sp.dma_start(rfT[0:MD, :], rfT_dram).then_inc(rf_loaded, 16)
                sp.dma_start(ab[:, 0, :], a_src.rearrange("h c -> (h c)").partition_broadcast(128)
                             ).then_inc(a_loaded, 16)
                sp.dma_start(ab[:, 1, :], a_dst.rearrange("h c -> (h c)").partition_broadcast(128)
                             ).then_inc(a_loaded, 16)
                for k in range(KD // 2):
                    row = (half * (KD // 2) + k) * 128
                    sp.dma_start(ws[k][:], gnn_w1[row:row + 128, :]).then_inc(slice_loaded[k], 16)

            @block.gpsimd
            def _(pool):
                pool.memset(zero[:], 0.0).then_inc(consts, 1)
                pool.memset(vs[:], 1.0).then_inc(consts, 1)
                pool.tensor_copy(xs[:], xnT[:, :, 0:P]).then_inc(staged, 1)
                with pool.Fori(1, NT) as t:
                    pool.wait_ge(v_done, t)
                    pool.tensor_copy(xs[:], xnT[:, :, bass.ds(t * P, P)]).then_inc(staged, 1)

            @block.vector
            def _(dve):
                step = Chain(dve, dve_step)
                dve.sem_inc(q_ready, 1)
                dve.sem_inc(k_ready, 1)
                dve.wait_ge(w_loaded, 16 * 6 * (half + 1))
                dve.wait_ge(rf_loaded, 16)
                step(dve.memset(rfT[MD:A, :], 1.0))
                step(dve.tensor_scalar(brow[:, 0:2, :], brow[:, 0:2, :], SCALE, None, ALU.mult))
                step.flat_end()
                dve.wait_ge(consts, 2)
                with dve.Fori(0, NT) as t:
                    step.start(t, 2)
                    for c, (done, turned, evac, squared, ready) in enumerate(
                            ((q_done, q_turned, q_evac, qsq, q_ready), (k_done, k_turned, k_evac, ksq, k_ready))):
                        dve.wait_ge(done, t + 1)
                        dve.wait_ge(turned, t + 1)
                        dve.scalar_tensor_tensor(qs[:, c, :, 0:MD], G[c][:].rearrange("p (h d) -> p h d", d=MD), SCALE,
                                                 brow[:, c, :].rearrange("p (h d) -> p h d", d=MD),
                                                 ALU.mult, ALU.add).then_inc(evac, 1)
                        dve.wait_ge(squared, t + 1)
                        step(dve.tensor_reduce(nrm[:, c, :], sq[:, c, :, :], AX.X, ALU.add))
                        dve.tensor_scalar(qs[:, c, :, MD:A], nrm[:, c, :].unsqueeze(2), -0.5, None,
                                          ALU.mult).then_inc(ready, 1)
                    dve.wait_ge(v_done, t + 1)
                    dve.wait_ge(kv_step, t + 1)
                    dve.tensor_tensor(vs[:, :, 0:MD], G[2][:].rearrange("p (h d) -> p h d", d=MD),
                                      brow[:, 2, :].rearrange("p (h d) -> p h d", d=MD), ALU.add).then_inc(v_evac, 1)
                step.end(NT)
                dve.wait_ge(kv_step, NT + 1)
                for j in range(2):
                    dve.tensor_copy(kv[:, 2 * j:2 * j + 2, :, :], KV[j][:]).then_inc(kv_copied, 1)

            @block.scalar
            def _(act):
                for freed in (kT_done, exp_a, exp_b):
                    act.sem_inc(freed, 1)
                with act.Fori(0, NT) as t:
                    for c, (evac, squared, ready) in enumerate(((q_evac, qsq, q_ready), (k_evac, ksq, k_ready))):
                        act.wait_ge(evac, t + 1)
                        act.wait_ge(ready, t + 1)
                        act.activation(sq[:, c, :, :], qs[:, c, :, 0:MD], ACT.Square).then_inc(squared, 1)
                        if c == 0:
                            act.wait_ge(q_turned, t + 2)
                            act.activation(qT[:, :, bass.ds(t * P, P)], TQ[:], ACT.Copy).then_inc(qT_done, 1)
                    act.wait_ge(k_turned, t + 2)
                    act.wait_ge(phi_b, t + 1)
                    act.activation(kT[:], TQ[:], ACT.Copy).then_inc(kT_done, 1)
                    act.wait_ge(kv_step, t + 1)
                    act.wait_ge(phi_a, t + 1)
                    act.activation(phik[:, 0:2, :], PH[0][:], ACT.Exp).then_inc(exp_a, 1)
                    act.wait_ge(phi_b, t + 2)
                    act.activation(phik[:, 2:4, :], PH[1][:], ACT.Exp).then_inc(exp_b, 1)

            @block.tensor
            def _(pe):
                pe.sem_inc(q_turned, 1)
                pe.sem_inc(k_turned, 1)
                pe.sem_inc(kv_step, 1)
                pe.sem_inc(phi_b, 1)

                def gemm(c, t, done, evac):
                    if c == 0:
                        pe.wait_ge(staged, t + 1)
                    if evac is not None:
                        pe.wait_ge(evac, t)
                    for k in range(KD):
                        last = pe.matmul(G[c][:], xs[:, k, :], w[:, k, c, :], start=(k == 0), stop=(k == KD - 1))
                    last.then_inc(done, 1)

                def turn(c, t):
                    pe.wait_ge(k_ready if c else q_ready, t + 2)
                    if c == 0:
                        pe.wait_ge(kT_done, t + 1)
                    else:
                        pe.wait_ge(qT_done, t + 1)
                    for h in range(HH):
                        last = pe.transpose(TQ[:, h, :], qs[:, c, h, :], ident[0:P, 0:P])
                    last.then_inc(k_turned if c else q_turned, 1)

                def features(t):
                    pe.wait_ge(kT_done, t + 2)
                    for j, (done, used) in enumerate(((phi_a, exp_a), (phi_b, exp_b))):
                        pe.wait_ge(used, t + 1)
                        for h in range(2):
                            last = pe.matmul(PH[j][:, h, :], kT[:, 2 * j + h, :], rfT[:], start=True, stop=True,
                                             skip_group_check=True)
                        last.then_inc(done, 1)

                def keys_values(t, stop):
                    pe.wait_ge(exp_b, t + 2)
                    pe.wait_ge(exp_a, t + 2)
                    pe.wait_ge(v_evac, t + 1)
                    for h in range(HH):
                        for m in range(2):
                            last = pe.matmul(KV[h // 2][:, h % 2, m, :], phik[:, h, m * 128:(m + 1) * 128],
                                             vs[:, h, :], start=False, stop=stop, skip_group_check=True)
                    last.then_inc(kv_step, 1)

                pe.wait_ge(consts, 2)
                pe.wait_ge(w_loaded, 16 * 6 * (half + 1))
                pe.wait_ge(rf_loaded, 16)
                for j in range(2):
                    pe.matmul(KV[j][:].rearrange("p h m a -> p (h m a)"), zero[:],
                              vs[:].rearrange("p h a -> p (h a)"), start=True, stop=False, skip_group_check=True)
                gemm(0, 0, q_done, None)
                gemm(1, 0, k_done, None)
                gemm(2, 0, v_done, None)
                with pe.Fori(0, NT - 1) as t:
                    turn(0, t)
                    gemm(0, t + 1, q_done, q_evac)
                    turn(1, t)
                    gemm(1, t + 1, k_done, k_evac)
                    features(t)
                    gemm(2, t + 1, v_done, v_evac)
                    keys_values(t, False)
                turn(0, NT - 1)
                turn(1, NT - 1)
                features(NT - 1)
                keys_values(NT - 1, True)
        numerator(nc, cx, tag, half, rfT, qT, kv, attn, a_loaded, slice_loaded, ws, ab, wa, load_next)


def logits(nc, cx, st, block, W1, xnT, ident, wa, w, al, alT_dram, w_loaded):
    rows_done, rows_copied, turned, stored = (
        cx.sem("logit_" + s) for s in ("rows_done", "rows_copied", "turned", "stored"))
    J = 2 * H1
    alT = sb(nc, st, "logit_alT", [J, N])
    R = [pb(nc, st, f"logit_R{c}", [J, 512]) for c in range(CH)]
    T = pb(nc, st, "logit_T", [P, NT, J])

    @block.scalar
    def _(act):
        act.dma_start(w[:], W1.rearrange("(k p) n -> p k n", p=128)).then_inc(w_loaded, 16)
        for c in range(CH):
            act.wait_ge(rows_done, c + 1)
            act.activation(alT[:, CHO[c]:CHO[c] + CHW[c]], R[c][:, 0:CHW[c]], ACT.Copy).then_inc(rows_copied, 1)
        act.wait_ge(rows_copied, CH)
        act.dma_start(alT_dram, alT[:]).then_inc(stored, 16)
        act.wait_ge(turned, 1)
        act.activation(al[:], T[:], ACT.Copy)
        act.wait_ge(stored, 16)

    @block.tensor
    def _(pe):
        for c in range(CH):
            for k in range(KD):
                last = pe.matmul(R[c][:, 0:CHW[c]], wa[:, k, :], xnT[:, k, CHO[c]:CHO[c] + CHW[c]],
                                 start=(k == 0), stop=(k == KD - 1))
            last.then_inc(rows_done, 1)
        pe.wait_ge(rows_copied, CH)
        for t in range(NT):
            last = pe.transpose(T[:, t, :], alT[:, t * P:(t + 1) * P], ident[0:J, 0:J])
        last.then_inc(turned, 1)


def edge_table(nc, cx, st, block, src, dst, ident, keyT, sloT, spans):
    blank, loaded, iotas, key_ready, turned, span_ready, span_max, copied = (
        cx.sem("edge_" + s) for s in
        ("blank", "loaded", "iotas", "key_ready", "turned", "span_ready", "span_max", "copied"))
    dve_step = cx.sem("edge_step")
    FULL = EDGES // ER
    REST = EDGES - FULL * ER
    LAST = FULL - 2 * EGP
    di = sb(nc, st, "edge_di", [EGP, EG, ER], I32)
    si = sb(nc, st, "edge_si", [EGP, EG, ER], I32)
    df = sb(nc, st, "edge_df", [EGP, EG, ER])
    sf = sb(nc, st, "edge_sf", [EGP, EG, ER])
    hi = sb(nc, st, "edge_hi", [EGP, EG, ER])
    key = sb(nc, st, "edge_key", [EGP, EG, ER])
    slo = sb(nc, st, "edge_slo", [EGP, EG, ER])
    rng = sb(nc, st, "edge_rng", [EGP, 2, EG])
    row = sb(nc, st, "edge_row", [EGP, EG])
    row1 = sb(nc, st, "edge_row1", [EGP, 2, EG])
    win = sb(nc, st, "edge_win", [EGP, NW])
    c1 = sb(nc, st, "edge_c1", [EGP, NW])
    best = sb(nc, st, "edge_best", [EGP, 2, NW])
    allb = sb(nc, st, "edge_allb", [EGP, 2, NW])
    spi = sb(nc, st, "edge_spi", [EGP, 2, NW], I32)
    T = [pb(nc, st, f"edge_T{j}", [128, EROWS]) for j in range(2)]

    @block.sync
    def _(sp):
        sp.wait_ge(blank, 2)
        for v, t in ((dst, di), (src, si)):
            for g in range(2):
                sp.dma_start(t[:, g, :], v[g * EGP * ER:(g + 1) * EGP * ER].rearrange("(p e) -> p e", e=ER)
                             ).then_inc(loaded, 16)
            sp.dma_start(t[0:LAST, 2, :], v[2 * EGP * ER:FULL * ER].rearrange("(p e) -> p e", e=ER)
                         ).then_inc(loaded, 16)
            sp.dma_start(t[LAST:LAST + 1, 2, 0:REST], v[FULL * ER:EDGES].unsqueeze(0)).then_inc(loaded, 16)

    @block.gpsimd
    def _(pool):
        pool.memset(di[:], PADNODE).then_inc(blank, 1)
        pool.memset(si[:], 0).then_inc(blank, 1)
        pool.iota(row[:], [[EGP, EG]], base=0, channel_multiplier=1,
                  allow_small_or_imprecise_dtypes=True).then_inc(iotas, 1)
        pool.iota(win[:], [[WIN, NW]], base=0, channel_multiplier=0,
                  allow_small_or_imprecise_dtypes=True).then_inc(iotas, 1)
        pool.wait_ge(span_ready, 1)
        pool.partition_all_reduce(allb[:], best[:], EGP, bass.bass_isa.ReduceOp.max).then_inc(span_max, 1)

    @block.vector
    def _(dve):
        step = Chain(dve, dve_step)
        dve.wait_ge(loaded, 8 * 16)
        step(dve.tensor_copy(df[:], di[:]))
        step(dve.tensor_copy(sf[:], si[:]))
        step(dve.tensor_scalar(hi[:], sf[:], float(SLO), None, ALU.is_ge))
        for part in range(2, SPLIT):
            step(dve.scalar_tensor_tensor(hi[:], sf[:], float(part * SLO), hi[:], ALU.is_ge, ALU.add))
        step(dve.scalar_tensor_tensor(slo[:], hi[:], -float(SLO), sf[:], ALU.mult, ALU.add))
        dve.scalar_tensor_tensor(key[:], df[:], float(SPLIT), hi[:], ALU.mult, ALU.add).then_inc(key_ready, 1)
        step(dve.tensor_reduce(rng[:, 0, :], df[:], AX.X, ALU.min))
        step(dve.tensor_reduce(rng[:, 1, :], df[:], AX.X, ALU.max))
        dve.wait_ge(iotas, 2)
        step(dve.tensor_scalar(row1[:, 0, :], row[:], -1.0, 1000.0, ALU.mult, ALU.add))
        step(dve.tensor_scalar(row1[:, 1, :], row[:], 1.0, None, ALU.add))
        step(dve.memset(best[:], 0.0))
        for g in range(EG):
            step(dve.tensor_scalar(c1[:], win[:], float(WIN - 1), rng[:, 0, g:g + 1], ALU.add, ALU.is_ge))
            step(dve.scalar_tensor_tensor(c1[:], win[:], rng[:, 1, g:g + 1], c1[:], ALU.is_le, ALU.mult))
            for e in range(2):
                ins = dve.scalar_tensor_tensor(best[:, e, :], c1[:], row1[:, e, g:g + 1], best[:, e, :],
                                               ALU.mult, ALU.max)
                if (g, e) == (EG - 1, 1):
                    ins.then_inc(span_ready, 1)
                else:
                    step(ins)
        dve.wait_ge(span_max, 1)
        step(dve.tensor_scalar(allb[:, 0, :], allb[:, 0, :], -1.0, 1000.0, ALU.mult, ALU.add))
        step(dve.tensor_scalar(allb[:, 0, :], allb[:, 0, :], float(EROWS - RB), None, ALU.min))
        step(dve.tensor_scalar(allb[:, 1, :], allb[:, 1, :], float(RB - 1), None, ALU.add))
        step(dve.scalar_tensor_tensor(allb[:, 1, :], allb[:, 0, :], float(RB), allb[:, 1, :], ALU.add, ALU.max))
        step(dve.tensor_copy(spi[:], allb[:]))
        step(dve.tensor_scalar(spans[:], spi[0:1, :, :].rearrange("p e w -> p (e w)"), RB.bit_length() - 1, None,
                               ALU.logical_shift_right))
        for j, dest in enumerate((keyT, sloT)):
            dve.wait_ge(turned, j + 1)
            dve.tensor_copy(dest[:], T[j][:]).then_inc(copied, 1)

    @block.tensor
    def _(pe):
        pe.wait_ge(key_ready, 1)
        for j, s in enumerate((key, slo)):
            for g in range(EG):
                last = pe.transpose(T[j][:, g * EGP:(g + 1) * EGP], s[:, g, :], ident[0:EGP, 0:EGP])
            last.then_inc(turned, 1)


def count_phase(nc, cx, keyT, sloT, spans, ct_dram, xnT, w, w_loaded, h):
    assert NW == H1 * NT
    RING = 4
    consts, hot, used, counted, evac, gemm, h_evac = (
        cx.sem("count_" + s) for s in ("consts", "hot", "used", "counted", "evac", "gemm", "h_evac"))
    stores = [cx.sem(f"count_stored{b}") for b in range(2)]
    with ExitStack() as st:
        ikey = sb(nc, st, "count_ikey", [128, 128])
        islo = sb(nc, st, "count_islo", [128, SLO], F16)
        off = sb(nc, st, "count_off", [128, NW])
        zero = sb(nc, st, "count_zero", [128, 128], BF16)
        A = sb(nc, st, "count_A", [128, RING * RB, 128], BF16)
        B = sb(nc, st, "count_B", [128, RING * RB, SLO], BF16)
        out = [sb(nc, st, f"count_out{b}", [128, SLO]) for b in range(2)]
        S = [pb(nc, st, f"count_S{b}", [128, SLO]) for b in range(2)]
        G = [pb(nc, st, f"count_G{b}", [P, C1]) for b in range(2)]
        block = st.enter_context(nc.Block())

        def windows(eng, name, body, before=None, after=None):
            with eng.register(name + "_turn") as turn:
                eng.reg_mov(turn, 1)
                with eng.Fori(0, H1) as hd:
                    for t in range(NT):
                        lo = eng.value_load(spans[0:1, bass.ds(hd * NT + t, 1)], min_val=0, max_val=EROWS // RB - 1)
                        hi = eng.value_load(spans[0:1, bass.ds(hd * NT + (NW + t), 1)], min_val=1,
                                            max_val=EROWS // RB)
                        if before is not None:
                            before(hd, t)
                        with eng.Fori(lo, hi) as r:
                            n = eng.snap(turn)
                            body(r, n, eng.snap(n & (RING - 1), min_val=0, max_val=RING - 1), hd, t)
                            eng.reg_add(turn, turn, 1)
                        if after is not None:
                            after(hd, t)

        @block.gpsimd
        def _(pool):
            kw = dict(allow_small_or_imprecise_dtypes=True)
            pool.iota(ikey[:], [[1, 128]], base=0, channel_multiplier=0, **kw).then_inc(consts, 1)
            pool.iota(islo[:], [[1, SLO]], base=0, channel_multiplier=0, **kw).then_inc(consts, 1)
            pool.iota(off[:], [[WIN * SPLIT, NW]], base=0, channel_multiplier=0, **kw).then_inc(consts, 1)
            pool.memset(zero[:], 0.0).then_inc(consts, 1)
            pool.memset(h[:, :, :, C1:C1 + 1], 1.0)

        @block.vector
        def _(dve):
            dve.wait_ge(consts, 4)

            def body(r, n, s, hd, t):
                dve.wait_ge(used, n)
                dve.scalar_tensor_tensor(A[:, bass.ds(s * RB, RB), :],
                                         ikey[:].unsqueeze(1).to_broadcast([128, RB, 128]),
                                         off[:, bass.ds(hd * NT + t, 1)],
                                         keyT[:, bass.ds(r * RB, RB)].unsqueeze(2).to_broadcast([128, RB, 128]),
                                         ALU.add, ALU.is_equal)
                for b in range(RB):
                    last = dve.tensor_scalar(B[:, bass.ds(s * RB + b, 1), :], islo[:].unsqueeze(1),
                                             sloT[:, bass.ds(r * RB + b, 1)], None, ALU.is_equal)
                last.then_inc(hot, 1)

            windows(dve, "count_dve", body)

        @block.tensor
        def _(pe):
            pe.wait_ge(consts, 4)
            pe.wait_ge(w_loaded, 16)
            pe.sem_inc(used, RING)

            def before(hd, t):
                pe.wait_ge(h_evac, hd * NT + (t + 1))
                for k in range(KD):
                    last = pe.matmul(G[t % 2][:], xnT[:, k, t * P:(t + 1) * P], w[:, k, bass.ds(hd * C1, C1)],
                                     start=(k == 0), stop=(k == KD - 1))
                last.then_inc(gemm, 1)
                pe.wait_ge(evac, hd * NT + (t + 1))
                pe.matmul(S[t % 2][:], zero[:], islo[:], start=True, stop=False, skip_group_check=True)

            def body(r, n, s, hd, t):
                pe.wait_ge(hot, n)
                for b in range(RB):
                    last = pe.matmul(S[t % 2][:], A[:, bass.ds(s * RB + b, 1), :].rearrange("p o k -> p (o k)"),
                                     B[:, bass.ds(s * RB + b, 1), :].rearrange("p o k -> p (o k)"),
                                     start=False, stop=False, skip_group_check=True)
                last.then_inc(used, 1)

            def after(hd, t):
                pe.matmul(S[t % 2][:], zero[:], islo[:], start=False, stop=True, skip_group_check=True
                          ).then_inc(counted, 1)

            windows(pe, "count_pe", body, before, after)

        @block.scalar
        def _(act):
            act.sem_inc(evac, 2)
            act.sem_inc(h_evac, 2)
            with act.Fori(0, H1) as hd:
                for t in range(NT):
                    act.wait_ge(gemm, hd * NT + (t + 1))
                    act.activation(h[:, t, bass.ds(hd, 1), 0:C1], G[t % 2][:].unsqueeze(1), ACT.Copy
                                   ).then_inc(h_evac, 1)
                    act.wait_ge(counted, hd * NT + (t + 1))
                    act.wait_ge(stores[t % 2], hd * (16 * NT // 2) + 16 * (t // 2))
                    act.activation(out[t % 2][:], S[t % 2][:], ACT.Copy).then_inc(evac, 1)

        @block.sync
        def _(sp):
            with sp.Fori(0, NW // 2) as w2:
                for q in range(2):
                    sp.wait_ge(evac, w2 * 2 + (q + 3))
                    sp.dma_start(ct_dram[bass.ds(w2 * 256 + q * 128, 128), :], out[q][:]).then_inc(stores[q], 16)
            for q in range(2):
                sp.wait_ge(stores[q], 16 * (NW // 2))


def mask_phase(nc, cx, ct_dram, c_dram, mask_dram, alT_dram, ident, al, mT_dram):
    HT = NT // 2
    rows_loaded, masked, turned, ev_d, ev_a, m_ready, m_turned, m_copied, m_stored = (
        cx.sem("mask_" + s) for s in ("rows_loaded", "masked", "turned", "ev_d", "ev_a", "m_ready",
                                      "m_turned", "m_copied", "m_stored"))
    loads = [cx.sem(f"mask_loaded{b}") for b in range(2)]
    mask_stores = [cx.sem(f"mask_mstored{b}") for b in range(2)]
    c_stores = [cx.sem(f"mask_cstored{b}") for b in range(2)]
    dve_step = cx.sem("mask_step")
    with ExitStack() as st:
        ct = [sb(nc, st, f"mask_ct{b}", [P, N]) for b in range(2)]
        mk = [sb(nc, st, f"mask_mk{b}", [P, N]) for b in range(2)]
        co = [sb(nc, st, f"mask_co{b}", [P, NT, P]) for b in range(2)]
        rows = sb(nc, st, "mask_rows", [P, H1, N])
        junk = sb(nc, st, "mask_junk", [P, N])
        big = sb(nc, st, "mask_big", [P, NT, H1])
        m = sb(nc, st, "mask_m", [P, NT, H1])
        mT = sb(nc, st, "mask_mT", [H1, N])
        T = [[pb(nc, st, f"mask_T{b}{j}", [P, 4, P]) for j in range(3)] for b in range(2)]
        width = [4, 4, 2]
        block = st.enter_context(nc.Block())

        @block.sync
        def _(sp):
            for h in range(H1):
                sp.dma_start(rows[:, h, :], alT_dram[h, :].partition_broadcast(P)).then_inc(rows_loaded, 16)
            with sp.Fori(0, HT) as i:
                for b in range(2):
                    sp.wait_ge(turned, i * 2 + (b + 1))
                    sp.wait_ge(masked, i * 2 + (b + 1))
                    sp.dma_start(ct[b][:], ct_dram.rearrange("(d a) s -> d (a s)", a=SPLIT)
                                 [bass.ds(i * (2 * P) + b * P, P), 0:N]).then_inc(loads[b], 16)
            sp.wait_ge(m_copied, 3)
            sp.dma_start(mT_dram, mT[:]).then_inc(m_stored, 16)
            sp.wait_ge(m_stored, 16)

        @block.gpsimd
        def _(pool):
            for t in range(NT):
                b = t % 2
                pool.wait_ge(masked, t + 3)
                pool.dma_start(mask_dram[t, :, :], mk[b][:]).then_inc(mask_stores[b], 16)
                pool.wait_ge(ev_d, t + 3)
                pool.wait_ge(ev_a, t + 3)
                pool.dma_start(c_dram[t, :, :], co[b][:].rearrange("p t d -> p (t d)")).then_inc(c_stores[b], 16)
            for b in range(2):
                pool.wait_ge(mask_stores[b], 16 * HT)
                pool.wait_ge(c_stores[b], 16 * HT)

        @block.vector
        def _(dve):
            step = Chain(dve, dve_step)
            dve.sem_inc(masked, 2)
            dve.sem_inc(ev_d, 2)
            dve.wait_ge(rows_loaded, 64)
            for t in range(NT):
                b = t % 2
                dve.wait_ge(loads[b], 16 * (t // 2 + 1))
                diag = ct[b][:, t * P:(t + 1) * P]
                step(dve.tensor_tensor(diag, diag, ident[0:P, 0:P], ALU.add))
                dve.wait_ge(mask_stores[b], 16 * (t // 2))
                dve.tensor_scalar(mk[b][:], ct[b][:], 0.0, -BIG, ALU.is_equal, ALU.mult).then_inc(masked, 1)
                dve.wait_ge(masked, t + 3)
                for h in range(H1):
                    step(dve.tensor_tensor_reduce(out=junk[:], in0=mk[b][:], in1=rows[:, h, :], scale=1.0,
                                                  scalar=-3.0e38, op0=ALU.add, op1=ALU.max,
                                                  accum_out=big[:, t, h:h + 1]))
                dve.wait_ge(turned, t + 3)
                dve.wait_ge(c_stores[b], 16 * (t // 2))
                dve.tensor_copy(co[b][:, 0:4, :], T[b][0][:]).then_inc(ev_d, 1)
            step(dve.tensor_tensor(big[:], big[:], al[:, :, H1:2 * H1], ALU.add))
            dve.scalar_tensor_tensor(m[:], big[:], SLOPE, big[:], ALU.mult, ALU.max).then_inc(m_ready, 1)
            for j in range(3):
                dve.wait_ge(m_turned, j + 1)
                dve.tensor_copy(mT[:, 4 * j * P:(4 * j + width[j]) * P],
                                T[0][j][0:H1, 0:width[j], :].rearrange("p t d -> p (t d)")).then_inc(m_copied, 1)

        @block.scalar
        def _(act):
            act.sem_inc(ev_a, 2)
            with act.Fori(0, HT) as i:
                for b in range(2):
                    act.wait_ge(turned, i * 2 + (b + 3))
                    act.wait_ge(c_stores[b], i * 16)
                    act.activation(co[b][:, 4:8, :], T[b][1][:], ACT.Copy)
                    act.activation(co[b][:, 8:10, :], T[b][2][:, 0:2, :], ACT.Copy).then_inc(ev_a, 1)

        @block.tensor
        def _(pe):
            pe.sem_inc(turned, 2)
            with pe.Fori(0, HT) as i:
                for b in range(2):
                    pe.wait_ge(masked, i * 2 + (b + 3))
                    pe.wait_ge(ev_a, i * 2 + (b + 1))
                    pe.wait_ge(ev_d, i * 2 + (b + 1))
                    for t in range(NT):
                        last = pe.transpose(T[b][t // 4][:, t % 4, :], ct[b][:, t * P:(t + 1) * P], ident[0:P, 0:P])
                    last.then_inc(turned, 1)
            pe.wait_ge(m_ready, 1)
            pe.wait_ge(ev_a, NT + 2)
            pe.wait_ge(ev_d, NT + 2)
            for j in range(3):
                for t in range(width[j]):
                    last = pe.transpose(T[0][j][0:H1, t, :], m[:, 4 * j + t, :], ident[0:P, 0:P])
                last.then_inc(m_turned, 1)


def gat1_phase(nc, cx, b1, h, al, alT_dram, mT_dram, c_dram, h1T_dram, ident):
    (e_ready, exp_done, w_ready, agg, mn_ready, exp_mn, elu_ready, turned, t_evac, dve_step, b_loaded) = (
        cx.sem("gat1_" + s) for s in
        ("e_ready", "exp_done", "w_ready", "agg", "mn_ready", "exp_mn", "elu_ready", "turned", "t_evac", "dve_step",
         "b_loaded"))
    rows_loaded = [cx.sem(f"gat1_rows_loaded{b}") for b in range(2)]
    c_loaded = [cx.sem(f"gat1_c_loaded{b}") for b in range(2)]
    stored = [cx.sem(f"gat1_stored{b}") for b in range(2)]
    HC = C1 // 2
    HT16 = 16 * NT // 2
    with ExitStack() as st:
        brow = sb(nc, st, "gat1_brow", [P, F1])
        rows = [sb(nc, st, f"gat1_rows{b}", [P, 2, N]) for b in range(2)]
        u = sb(nc, st, "gat1_u", [P, NT, P])
        e = [sb(nc, st, f"gat1_e{b}", [P, NT, P]) for b in range(2)]
        wt = [sb(nc, st, f"gat1_wt{b}", [P, NT, P]) for b in range(2)]
        cnt = [sb(nc, st, f"gat1_cnt{b}", [P, NT, P]) for b in range(2)]
        rden = [sb(nc, st, f"gat1_rden{b}", [P, 1]) for b in range(2)]
        o = [sb(nc, st, f"gat1_o{b}", [P, C1]) for b in range(2)]
        mn = [sb(nc, st, f"gat1_mn{b}", [P, C1]) for b in range(2)]
        oT = [sb(nc, st, f"gat1_oT{b}", [128, 4, P]) for b in range(2)]
        Z = [[pb(nc, st, f"gat1_Z{b}{j}", [P, HC + j]) for j in range(2)] for b in range(2)]
        T = [pb(nc, st, f"gat1_T{b}", [128, 4, P]) for b in range(2)]
        block = st.enter_context(nc.Block())

        def heads(eng, body):
            body(0, 0, True, False)
            with eng.Fori(0, H1 // 2 - 1) as i:
                body(i * 2 + 1, 1, False, False)
                body(i * 2 + 2, 0, False, False)
            body(H1 - 1, 1, False, True)

        @block.sync
        def _(sp):
            sp.dma_start(brow[:], b1.partition_broadcast(P)).then_inc(b_loaded, 16)

            def load_rows(hd, b):
                sp.dma_start(rows[b][:, 0, :], alT_dram[bass.ds(hd + H1, 1), :].partition_broadcast(P)
                             ).then_inc(rows_loaded[b], 16)
                sp.dma_start(rows[b][:, 1, :], mT_dram[bass.ds(hd, 1), :].partition_broadcast(P)
                             ).then_inc(rows_loaded[b], 16)

            load_rows(0, 0)

            def body(hd, b, first, last):
                if not last:
                    if not first:
                        sp.wait_ge(e_ready, hd * NT)
                    load_rows(hd + 1, 1 - b)
                for t in range(NT):
                    sp.wait_ge(w_ready, hd * NT + (t + 1))
                    sp.dma_start(cnt[t % 2][:], c_dram[t, :, :].rearrange("p (t d) -> p t d", d=P)
                                 ).then_inc(c_loaded[t % 2], 16)

            heads(sp, body)

        @block.vector
        def _(dve):
            def steps(before):
                made = [0]

                def step(ins):
                    made[0] += 1
                    ins.then_inc(dve_step, 1)
                    dve.wait_ge(dve_step, before + made[0])
                return step

            STEPS = 5

            for freed in (w_ready, mn_ready):
                dve.sem_inc(freed, 2)
            dve.wait_ge(b_loaded, 16)

            def scores(hd, t, hb):
                b, g = t % 2, hd * NT + t
                step = steps(2 * g if isinstance(g, int) and g < 2 else g * STEPS - 6)
                if t == 0:
                    dve.wait_ge(rows_loaded[hb], (hd - hb) * 16 + 32)
                if not (isinstance(g, int) and g == 0):
                    dve.wait_ge(e_ready, g)
                step(dve.tensor_tensor(u[:], al[:, :, bass.ds(hd, 1)].to_broadcast([P, NT, P]),
                                       rows[hb][:, 0:1, t * P:(t + 1) * P].to_broadcast([P, NT, P]), ALU.add))
                step(dve.scalar_tensor_tensor(u[:], u[:], SLOPE, u[:], ALU.mult, ALU.max))
                dve.wait_ge(w_ready, g + 1)
                dve.tensor_tensor(e[b][:], u[:], rows[hb][:, 1:2, t * P:(t + 1) * P].to_broadcast([P, NT, P]),
                                  ALU.subtract).then_inc(e_ready, 1)

            def weights(hd, t):
                b, g = t % 2, hd * NT + t
                dve.wait_ge(exp_done, g + 1)
                dve.wait_ge(c_loaded[b], hd * HT16 + 16 * (t // 2 + 1))
                dve.wait_ge(agg, g + 1)
                dve.tensor_tensor(wt[b][:], e[b][:], cnt[b][:], ALU.mult).then_inc(w_ready, 1)

            def normalise(hd, t, left):
                b, g = t % 2, hd * NT + t
                step = steps(g * STEPS + (6, 4, 2)[left])
                dve.wait_ge(agg, g + 3)
                dve.wait_ge(turned, g + 1)
                step(dve.tensor_scalar(rden[b][:], Z[b][1][:, HC:HC + 1], 1e-16, None, ALU.add))
                step(dve.reciprocal(rden[b][:], rden[b][:]))
                dve.scalar_tensor_tensor(o[b][:, 0:HC], Z[b][0][:], rden[b][:],
                                         brow[:, bass.ds(hd * C1, HC)], ALU.mult, ALU.add)
                step(dve.scalar_tensor_tensor(o[b][:, HC:C1], Z[b][1][:, 0:HC], rden[b][:],
                                              brow[:, bass.ds(hd * C1 + HC, HC)], ALU.mult, ALU.add))
                if not (isinstance(g, int) and g == 0):
                    dve.wait_ge(elu_ready, g)
                dve.tensor_scalar(mn[b][:], o[b][:], 0.0, None, ALU.min).then_inc(mn_ready, 1)

            def elu(hd, t):
                b, g = t % 2, hd * NT + t
                dve.wait_ge(exp_mn, g + 1)
                dve.scalar_tensor_tensor(o[b][:], mn[b][:], -1.0, o[b][:], ALU.add, ALU.max).then_inc(elu_ready, 1)

            for t in range(2):
                scores(0, t, 0)
                weights(0, t)

            def body(hd, hb, first, last):
                for t in range(NT):
                    if t + 2 < NT:
                        scores(hd, t + 2, hb)
                    elif not last:
                        scores(hd + 1, t + 2 - NT, 1 - hb)
                    normalise(hd, t, max(0, t + 3 - NT) if last else 0)
                    if t + 2 < NT:
                        weights(hd, t + 2)
                    elif not last:
                        weights(hd + 1, t + 2 - NT)
                    elu(hd, t)

            heads(dve, body)

        @block.scalar
        def _(act):
            act.sem_inc(t_evac, 2)

            def exp_scores(hd, t):
                act.wait_ge(e_ready, hd * NT + (t + 1))
                act.activation(e[t % 2][:], e[t % 2][:], ACT.Exp).then_inc(exp_done, 1)

            exp_scores(0, 0)
            exp_scores(0, 1)

            def body(hd, hb, first, last):
                for t in range(NT):
                    if t + 2 < NT:
                        exp_scores(hd, t + 2)
                    elif not last:
                        exp_scores(hd + 1, t + 2 - NT)
                    b = t % 2
                    act.wait_ge(mn_ready, hd * NT + (t + 3))
                    act.activation(mn[b][:], mn[b][:], ACT.Exp).then_inc(exp_mn, 1)
                    act.wait_ge(turned, hd * NT + (t + 3))
                    if not (first and t < 2):
                        act.wait_ge(stored[b], hd * HT16 + 16 * (t // 2))
                    act.activation(oT[b][:], T[b][:], ACT.Copy).then_inc(t_evac, 1)
                    act.wait_ge(t_evac, hd * NT + (t + 3))
                    act.dma_start(h1T_dram[t, :, :].rearrange("p (f d) -> p f d", d=P)[:, bass.ds(hd * 4, 4), :],
                                  oT[b][:]).then_inc(stored[b], 16)

            heads(act, body)
            for b in range(2):
                act.wait_ge(stored[b], H1 * HT16)

        @block.tensor
        def _(pe):
            pe.sem_inc(agg, 2)
            pe.sem_inc(turned, 2)

            def aggregate(hd, t):
                b, g = t % 2, hd * NT + t
                pe.wait_ge(w_ready, g + 3)
                pe.wait_ge(mn_ready, g + 1)
                for j in range(2):
                    for s in range(NT):
                        last = pe.matmul(Z[b][j][:], wt[b][:, s, :],
                                         h[:, s, bass.ds(hd, 1), j * HC:(j + 1) * HC + j],
                                         start=(s == 0), stop=(s == NT - 1))
                last.then_inc(agg, 1)

            def turn(hd, t):
                b, g = t % 2, hd * NT + t
                pe.wait_ge(elu_ready, g + 1)
                pe.wait_ge(t_evac, g + 1)
                for f in range(4):
                    last = pe.transpose(T[b][:, f, :], o[b][:, f * 128:(f + 1) * 128], ident[0:P, 0:P])
                last.then_inc(turned, 1)

            aggregate(0, 0)

            def body(hd, hb, first, last):
                for t in range(NT):
                    if t + 1 < NT:
                        aggregate(hd, t + 1)
                    elif not last:
                        aggregate(hd + 1, 0)
                    turn(hd, t)

            heads(pe, body)


def gat2_project_phase(nc, cx, W2, a_src, a_dst, h1T_dram, ident, h2, al2, al2T_dram):
    loaded, wa_step, w2_ready, projected, ev_a, ev_d, turned, copied, stored = (
        cx.sem("gat2p_" + s) for s in
        ("loaded", "wa_step", "w2_ready", "projected", "ev_a", "ev_d", "turned", "copied", "stored"))
    in_loaded = [cx.sem(f"gat2p_in{b}") for b in range(2)]
    W = D + 2
    HW = W // 2
    with ExitStack() as st:
        w = sb(nc, st, "gat2p_w", [128, KF, W])
        ab = sb(nc, st, "gat2p_a", [128, 2, D])
        junk = sb(nc, st, "gat2p_junk", [128, 2, D])
        hT = [sb(nc, st, f"gat2p_hT{b}", [128, KF, P]) for b in range(2)]
        alT = sb(nc, st, "gat2p_alT", [2, N])
        Y = [[pb(nc, st, f"gat2p_Y{b}{j}", [P, HW]) for j in range(2)] for b in range(2)]
        T = [pb(nc, st, f"gat2p_T{j}", [2, 4, P]) for j in range(3)]
        width = [4, 4, 2]
        block = st.enter_context(nc.Block())

        @block.sync
        def _(sp):
            sp.dma_start(ab[:, 0, :], a_src[0, :].partition_broadcast(128)).then_inc(loaded, 16)
            sp.dma_start(ab[:, 1, :], a_dst[0, :].partition_broadcast(128)).then_inc(loaded, 16)
            sp.dma_start(w[:, :, 0:D], W2.rearrange("(k p) n -> p k n", p=128)).then_inc(loaded, 16)
            with sp.Fori(0, NT // 2) as i:
                for b in range(2):
                    sp.wait_ge(projected, i * 2 + (b + 1))
                    sp.dma_start(hT[b][:], h1T_dram[bass.ds(i * 2 + b, 1), :, :]
                                 .rearrange("o p (f d) -> p (o f) d", d=P)).then_inc(in_loaded[b], 16)
            sp.wait_ge(copied, 3)
            sp.dma_start(al2T_dram, alT[:]).then_inc(stored, 16)
            sp.wait_ge(stored, 16)

        @block.vector
        def _(dve):
            dve.sem_inc(ev_d, 2)
            dve.memset(h2[:, :, D:D + 1], 1.0).then_inc(w2_ready, 1)
            dve.wait_ge(loaded, 48)
            n = 0
            for k in range(KF):
                for s in range(2):
                    if n >= 2:
                        dve.wait_ge(wa_step, n - 1)
                    dve.tensor_tensor_reduce(out=junk[:, n % 2, :], in0=w[:, k, 0:D], in1=ab[:, s, :], scale=1.0,
                                             scalar=0.0, op0=ALU.mult, op1=ALU.add,
                                             accum_out=w[:, k, D + s:D + s + 1]).then_inc(wa_step, 1)
                    n += 1
            with dve.Fori(0, NT // 2) as i:
                for b in range(2):
                    dve.wait_ge(projected, i * 2 + (b + 3))
                    dve.tensor_copy(h2[:, bass.ds(i * 2 + b, 1), HW:D], Y[b][1][:, 0:HW - 2].unsqueeze(1))
                    dve.tensor_copy(al2[:, bass.ds(i * 2 + b, 1), :], Y[b][1][:, HW - 2:HW].unsqueeze(1)
                                    ).then_inc(ev_d, 1)
            for j in range(3):
                dve.wait_ge(turned, j + 1)
                dve.tensor_copy(alT[:, 4 * j * P:(4 * j + width[j]) * P],
                                T[j][:, 0:width[j], :].rearrange("p t d -> p (t d)")).then_inc(copied, 1)

        @block.scalar
        def _(act):
            act.sem_inc(ev_a, 2)
            with act.Fori(0, NT // 2) as i:
                for b in range(2):
                    act.wait_ge(projected, i * 2 + (b + 3))
                    act.activation(h2[:, bass.ds(i * 2 + b, 1), 0:HW], Y[b][0][:].unsqueeze(1), ACT.Copy
                                   ).then_inc(ev_a, 1)

        @block.tensor
        def _(pe):
            pe.sem_inc(projected, 2)
            pe.wait_ge(loaded, 48)
            pe.wait_ge(wa_step, 2 * KF)
            with pe.Fori(0, NT // 2) as i:
                for b in range(2):
                    pe.wait_ge(in_loaded[b], i * 16 + 16)
                    pe.wait_ge(ev_a, i * 2 + (b + 1))
                    pe.wait_ge(ev_d, i * 2 + (b + 1))
                    for j in range(2):
                        for k in range(KF):
                            last = pe.matmul(Y[b][j][:], hT[b][:, k, :], w[:, k, j * HW:(j + 1) * HW],
                                             start=(k == 0), stop=(k == KF - 1))
                    last.then_inc(projected, 1)
            pe.wait_ge(ev_d, NT + 2)
            for j in range(3):
                for t in range(width[j]):
                    last = pe.transpose(T[j][:, t, :], al2[:, 4 * j + t, :], ident[0:P, 0:P])
                last.then_inc(turned, 1)


def gat2_max_phase(nc, cx, mask_dram, al2, al2T_dram, m2T_dram, ident):
    row_loaded, m_ready, turned, copied, stored = (
        cx.sem("gat2m_" + s) for s in ("row_loaded", "m_ready", "turned", "copied", "stored"))
    loads = [cx.sem(f"gat2m_in{b}") for b in range(2)]
    maxed = cx.sem("gat2m_maxed")
    dve_step = cx.sem("gat2m_step")
    with ExitStack() as st:
        row = sb(nc, st, "gat2m_row", [P, N])
        mk = [sb(nc, st, f"gat2m_mk{b}", [P, N]) for b in range(2)]
        junk = [sb(nc, st, f"gat2m_junk{b}", [P, N]) for b in range(2)]
        big = sb(nc, st, "gat2m_big", [P, NT])
        m = sb(nc, st, "gat2m_m", [P, NT])
        mT = sb(nc, st, "gat2m_mT", [1, N])
        T = [pb(nc, st, f"gat2m_T{j}", [1, 4, P]) for j in range(3)]
        width = [4, 4, 2]
        block = st.enter_context(nc.Block())

        @block.sync
        def _(sp):
            sp.dma_start(row[:], al2T_dram[0, :].partition_broadcast(P)).then_inc(row_loaded, 16)
            with sp.Fori(0, NT // 2) as i:
                for b in range(2):
                    sp.wait_ge(maxed, i * 2 + (b + 1))
                    sp.dma_start(mk[b][:], mask_dram[bass.ds(i * 2 + b, 1), :, :].rearrange("o p n -> p (o n)")
                                 ).then_inc(loads[b], 16)
            sp.wait_ge(copied, 3)
            sp.dma_start(m2T_dram, mT[:]).then_inc(stored, 16)
            sp.wait_ge(stored, 16)

        @block.vector
        def _(dve):
            step = Chain(dve, dve_step)
            dve.sem_inc(maxed, 2)
            dve.wait_ge(row_loaded, 16)
            for t in range(NT):
                b = t % 2
                dve.wait_ge(loads[b], 16 * (t // 2 + 1))
                dve.wait_ge(maxed, t + 1)
                dve.tensor_tensor_reduce(out=junk[b][:], in0=mk[b][:], in1=row[:], scale=1.0, scalar=-3.0e38,
                                         op0=ALU.add, op1=ALU.max, accum_out=big[:, t:t + 1]).then_inc(maxed, 1)
            dve.wait_ge(maxed, NT + 2)
            step(dve.tensor_tensor(big[:], big[:], al2[:, :, 1], ALU.add))
            dve.scalar_tensor_tensor(m[:], big[:], SLOPE, big[:], ALU.mult, ALU.max).then_inc(m_ready, 1)
            for j in range(3):
                dve.wait_ge(turned, j + 1)
                dve.tensor_copy(mT[:, 4 * j * P:(4 * j + width[j]) * P],
                                T[j][:, 0:width[j], :].rearrange("p t d -> p (t d)")).then_inc(copied, 1)

        @block.tensor
        def _(pe):
            pe.wait_ge(m_ready, 1)
            for j in range(3):
                for t in range(width[j]):
                    last = pe.transpose(T[j][:, t, :], m[:, 4 * j + t:4 * j + t + 1], ident[0:P, 0:P])
                last.then_inc(turned, 1)


def gat2_phase(nc, cx, al2, al2T_dram, m2T_dram, c_dram, h2, x1_dram, x1):
    (rows_loaded, x_loaded, e_ready, exp_done, w_ready, agg, summed, dve_step) = (
        cx.sem("gat2_" + s) for s in
        ("rows_loaded", "x_loaded", "e_ready", "exp_done", "w_ready", "agg", "summed", "dve_step"))
    c_loaded = [cx.sem(f"gat2_c_loaded{b}") for b in range(2)]
    CW = [385, 384]
    with ExitStack() as st:
        rows = sb(nc, st, "gat2_rows", [P, 2, N])
        u = sb(nc, st, "gat2_u", [P, NT, P])
        e = [sb(nc, st, f"gat2_e{b}", [P, NT, P]) for b in range(2)]
        wt = [sb(nc, st, f"gat2_wt{b}", [P, NT, P]) for b in range(2)]
        cnt = [sb(nc, st, f"gat2_cnt{b}", [P, NT, P]) for b in range(2)]
        rden = [sb(nc, st, f"gat2_rden{b}", [P, 1]) for b in range(2)]
        Z = [[pb(nc, st, f"gat2_Z{b}{j}", [P, CW[j]]) for j in range(2)] for b in range(2)]
        block = st.enter_context(nc.Block())

        @block.sync
        def _(sp):
            sp.dma_start(rows[:, 0, :], al2T_dram[1, :].partition_broadcast(P)).then_inc(rows_loaded, 16)
            sp.dma_start(rows[:, 1, :], m2T_dram[0, :].partition_broadcast(P)).then_inc(rows_loaded, 16)
            sp.dma_start(x1[:], x1_dram.rearrange("(t p) d -> p t d", p=P)).then_inc(x_loaded, 16)
            for t in range(NT):
                sp.wait_ge(w_ready, t + 1)
                sp.dma_start(cnt[t % 2][:], c_dram[t, :, :].rearrange("p (t d) -> p t d", d=P)
                             ).then_inc(c_loaded[t % 2], 16)

        @block.vector
        def _(dve):
            step = Chain(dve, dve_step)
            dve.sem_inc(w_ready, 2)
            dve.sem_inc(summed, 2)

            def scores(t):
                b = t % 2
                dve.wait_ge(e_ready, t)
                step(dve.tensor_tensor(u[:], al2[:, :, 0:1].to_broadcast([P, NT, P]),
                                       rows[:, 0:1, t * P:(t + 1) * P].to_broadcast([P, NT, P]), ALU.add))
                step(dve.scalar_tensor_tensor(u[:], u[:], SLOPE, u[:], ALU.mult, ALU.max))
                dve.wait_ge(w_ready, t + 1)
                dve.tensor_tensor(e[b][:], u[:], rows[:, 1:2, t * P:(t + 1) * P].to_broadcast([P, NT, P]),
                                  ALU.subtract).then_inc(e_ready, 1)

            def weights(t):
                b = t % 2
                dve.wait_ge(exp_done, t + 1)
                dve.wait_ge(c_loaded[b], 16 * (t // 2 + 1))
                dve.wait_ge(agg, t + 1)
                dve.tensor_tensor(wt[b][:], e[b][:], cnt[b][:], ALU.mult).then_inc(w_ready, 1)

            def add(t):
                b = t % 2
                dve.wait_ge(agg, t + 3)
                dve.wait_ge(summed, t + 1)
                step(dve.tensor_scalar(rden[b][:], Z[b][1][:, 383:384], 1e-16, None, ALU.add))
                step(dve.reciprocal(rden[b][:], rden[b][:]))
                dve.scalar_tensor_tensor(x1[:, t, 0:385], Z[b][0][:], rden[b][:], x1[:, t, 0:385], ALU.mult, ALU.add)
                dve.scalar_tensor_tensor(x1[:, t, 385:D], Z[b][1][:, 0:383], rden[b][:], x1[:, t, 385:D],
                                         ALU.mult, ALU.add).then_inc(summed, 1)

            dve.wait_ge(rows_loaded, 32)
            dve.wait_ge(x_loaded, 16)
            scores(0)
            weights(0)
            for t in range(NT + 1):
                if t + 1 < NT:
                    scores(t + 1)
                if t >= 1:
                    add(t - 1)
                if t + 1 < NT:
                    weights(t + 1)

        @block.scalar
        def _(act):
            for t in range(NT):
                act.wait_ge(e_ready, t + 1)
                act.activation(e[t % 2][:], e[t % 2][:], ACT.Exp).then_inc(exp_done, 1)

        @block.tensor
        def _(pe):
            pe.sem_inc(agg, 2)
            for t in range(NT):
                b = t % 2
                pe.wait_ge(w_ready, t + 3)
                pe.wait_ge(summed, t + 1)
                for j in range(2):
                    for s in range(NT):
                        last = pe.matmul(Z[b][j][:], wt[b][:, s, :], h2[:, s, 385 * j:385 * j + CW[j]],
                                         start=(s == 0), stop=(s == NT - 1))
                last.then_inc(agg, 1)


def route_norm_phase(nc, cx, x1, wg, wge, bg, bge, xn2_dram, ident, lg):
    (stats_done, sqrt_done, xn_ready, turned, ev_d, ev_a, w_loaded, mm, lg_done, zeroed) = (
        cx.sem("rn_" + s) for s in
        ("stats_done", "sqrt_done", "xn_ready", "turned", "ev_d", "ev_a", "w_loaded", "mm", "lg_done", "zeroed"))
    stored = [cx.sem(f"rn_stored{b}") for b in range(2)]
    zstored = cx.sem("rn_zstored")
    dve_step = cx.sem("rn_step")
    L = NG + NE
    with ExitStack() as st:
        stats = sb(nc, st, "rn_stats", [P, NT, 2, 6])
        mv = sb(nc, st, "rn_mv", [P, NT, 2])
        std = sb(nc, st, "rn_std", [P, NT])
        veps = sb(nc, st, "rn_veps", [P, NT])
        tmp = sb(nc, st, "rn_tmp", [P, NT])
        rstd = sb(nc, st, "rn_rstd", [P, NT])
        w = sb(nc, st, "rn_w", [128, KD, L])
        brow = sb(nc, st, "rn_brow", [P, L])
        zero = sb(nc, st, "rn_zero", [SLOT, D])
        xn = [sb(nc, st, f"rn_xn{b}", [P, D]) for b in range(2)]
        xT = [sb(nc, st, f"rn_xT{b}", [128, KD, P]) for b in range(2)]
        T = [[pb(nc, st, f"rn_T{b}{j}", [128, 3, P]) for j in range(2)] for b in range(2)]
        Y = [pb(nc, st, f"rn_Y{b}", [P, L]) for b in range(2)]
        block = st.enter_context(nc.Block())

        @block.sync
        def _(sp):
            sp.dma_start(w[:, :, 0:NG], wg.rearrange("(k p) n -> p k n", p=128)).then_inc(w_loaded, 16)
            sp.dma_start(w[:, :, NG:L], wge.rearrange("(k p) n -> p k n", p=128)).then_inc(w_loaded, 16)
            sp.dma_start(brow[:, 0:NG], bg.partition_broadcast(P)).then_inc(w_loaded, 16)
            sp.dma_start(brow[:, NG:L], bge.rearrange("g e -> (g e)").partition_broadcast(P)).then_inc(w_loaded, 16)
            sp.wait_ge(zeroed, 1)
            sp.dma_start(xn2_dram[N:N + SLOT, :], zero[:]).then_inc(zstored, 16)
            with sp.Fori(0, NT // 2) as i:
                for b in range(2):
                    sp.wait_ge(xn_ready, i * 2 + (b + 1))
                    sp.dma_start(xn2_dram[bass.ds(i * (2 * P) + b * P, P), :], xn[b][:]).then_inc(stored[b], 16)
            sp.wait_ge(zstored, 16)
            for b in range(2):
                sp.wait_ge(stored[b], 16 * (NT // 2))

        @block.gpsimd
        def _(pool):
            pool.memset(zero[:], 0.0).then_inc(zeroed, 1)

        @block.vector
        def _(dve):
            step = Chain(dve, dve_step)
            for t in range(NT):
                for h in range(2):
                    last = dve.bn_stats(stats[:, t, h, :], x1[:, t, h * 384:(h + 1) * 384])
            step(last)
            for t in range(NT):
                last = dve.bn_aggr(mv[:, t, :], stats[:, t, :, :])
            step(last)
            dve.tensor_scalar(veps[:], mv[:, :, 1], EPS, None, ALU.add).then_inc(stats_done, 1)
            dve.wait_ge(sqrt_done, 1)
            refine_rstd(step, dve, rstd[:], std[:], veps[:], tmp[:])
            dve.wait_ge(w_loaded, 64)
            dve.sem_inc(ev_d, 2)
            dve.sem_inc(lg_done, 2)

            def scaled(t, b, before):
                dve.wait_ge(turned, t + 1)
                dve.wait_ge(stored[b], before * 16)
                dve.tensor_scalar(xn[b][:], x1[:, bass.ds(t, 1), :], mv[:, bass.ds(t, 1), 0],
                                  rstd[:, bass.ds(t, 1)], ALU.subtract, ALU.mult).then_inc(xn_ready, 1)

            def copy(t, b):
                dve.wait_ge(turned, t + 3)
                dve.wait_ge(mm, t + 1)
                dve.tensor_copy(xT[b][:, 0:3, :], T[b][0][:]).then_inc(ev_d, 1)

            def logits(t, b):
                dve.wait_ge(mm, t + 3)
                dve.tensor_tensor(lg[:, bass.ds(t, 1), :], Y[b][:].unsqueeze(1), brow[:].unsqueeze(1),
                                  ALU.add).then_inc(lg_done, 1)

            scaled(0, 0, 0)
            scaled(1, 1, 0)
            copy(0, 0)
            with dve.Fori(0, NT // 2 - 1) as i:
                for b in range(2):
                    scaled(i * 2 + (b + 2), b, i + 1)
                    copy(i * 2 + (b + 1), 1 - b)
                    logits(i * 2 + b, b)
            copy(NT - 1, 1)
            logits(NT - 2, 0)
            logits(NT - 1, 1)

        @block.scalar
        def _(act):
            act.sem_inc(ev_a, 2)
            act.wait_ge(stats_done, 1)
            act.activation(std[:], veps[:], ACT.Sqrt).then_inc(sqrt_done, 1)
            with act.Fori(0, NT // 2) as i:
                for b in range(2):
                    act.wait_ge(turned, i * 2 + (b + 3))
                    act.wait_ge(mm, i * 2 + (b + 1))
                    act.activation(xT[b][:, 3:6, :], T[b][1][:], ACT.Copy).then_inc(ev_a, 1)

        @block.tensor
        def _(pe):
            pe.sem_inc(turned, 2)
            pe.sem_inc(mm, 2)
            pe.wait_ge(w_loaded, 64)

            def turn(t, b):
                pe.wait_ge(xn_ready, t + 1)
                pe.wait_ge(ev_d, t + 1)
                pe.wait_ge(ev_a, t + 1)
                for k in range(KD):
                    last = pe.transpose(T[b][k // 3][:, k % 3, :], xn[b][:, k * 128:(k + 1) * 128], ident[0:P, 0:P])
                last.then_inc(turned, 1)

            def product(t, b):
                pe.wait_ge(ev_d, t + 3)
                pe.wait_ge(ev_a, t + 3)
                pe.wait_ge(lg_done, t + 1)
                for k in range(KD):
                    last = pe.matmul(Y[b][:], xT[b][:, k, :], w[:, k, :], start=(k == 0), stop=(k == KD - 1))
                last.then_inc(mm, 1)

            turn(0, 0)
            with pe.Fori(0, NT // 2 - 1) as i:
                for b in range(2):
                    turn(i * 2 + (b + 1), 1 - b)
                    product(i * 2 + b, b)
            turn(NT - 1, 1)
            product(NT - 2, 0)
            product(NT - 1, 1)


def route_phase(nc, cx, lg, x1, b2, out, ident, codes, posm, ntile, tstart):
    (consts, exp_in, exp_out, sel_ready, counted, comb_ready, turned, copied, mm, summed, b2_loaded, stored) = (
        cx.sem("rt_" + s) for s in
        ("consts", "exp_in", "exp_out", "sel_ready", "counted", "comb_ready", "turned", "copied", "mm", "summed",
         "b2_loaded", "stored"))
    pre = cx.sem("rt_pre")
    dve_step = cx.sem("rt_step")
    TG = NT * NG
    with ExitStack() as st:
        gl = sb(nc, st, "rt_gl", [P, NT, NG])
        el = sb(nc, st, "rt_el", [P, TG, EPG])
        tri = sb(nc, st, "rt_tri", [P, EPG, EPG])
        low = sb(nc, st, "rt_low", [P, P])
        ones = sb(nc, st, "rt_ones", [P, P])
        cmp = sb(nc, st, "rt_cmp", [P, TG, EPG, EPG])
        eq = sb(nc, st, "rt_eq", [P, TG, EPG, EPG])
        rank = [sb(nc, st, "rt_rank0", [P, NT, NG]), sb(nc, st, "rt_rank1", [P, TG, EPG])]
        sel = [sb(nc, st, "rt_sel0", [P, NT, NG]), sb(nc, st, "rt_sel1", [P, TG, EPG])]
        mx = [sb(nc, st, "rt_mx0", [P, NT]), sb(nc, st, "rt_mx1", [P, TG])]
        gate = [sb(nc, st, "rt_gate0", [P, NT, NG]), sb(nc, st, "rt_gate1", [P, TG, EPG])]
        comb = sb(nc, st, "rt_comb", [P, TG, EPG])
        sele = sb(nc, st, "rt_sele", [P, TG, EPG])
        rest = sb(nc, st, "rt_rest", [P, TG, EPG])
        cum = sb(nc, st, "rt_cum", [P, NT + 1, NE])
        tot = sb(nc, st, "rt_tot", [P, NT, NE])
        ci = sb(nc, st, "rt_ci", [1, NE], I32)
        cf = sb(nc, st, "rt_cf", [1, 2, NE])
        ip = sb(nc, st, "rt_ip", [P, NT, NE], BF16)
        it = sb(nc, st, "rt_it", [P, NT, NE], BF16)
        b2s = sb(nc, st, "rt_b2", [NE, D])
        cT = sb(nc, st, "rt_cT", [NE, NT, P])
        zero = sb(nc, st, "rt_zero", [SLOT, D])
        PW = pb(nc, st, "rt_PW", [P, NT * NE])
        PT = pb(nc, st, "rt_PT", [P, NT * NE])
        T = [pb(nc, st, f"rt_T{j}", [NE, 4, P]) for j in range(3)]
        Y = [pb(nc, st, f"rt_Y{j}", [P, 384]) for j in range(2)]
        width = [4, 4, 2]
        block = st.enter_context(nc.Block())

        @block.sync
        def _(sp):
            sp.dma_start(b2s[:], b2).then_inc(b2_loaded, 16)
            sp.wait_ge(consts, 8)
            sp.dma_start(out[N:N + SLOT, :], zero[:]).then_inc(stored, 16)
            sp.wait_ge(summed, 2 * NT)
            sp.dma_start(out[0:N, :].rearrange("(t p) d -> p t d", p=P), x1[:]).then_inc(stored, 16)
            sp.wait_ge(stored, 32)

        @block.gpsimd
        def _(pool):
            kw = dict(allow_small_or_imprecise_dtypes=True)
            pool.memset(tri[:], 1.0).then_inc(pre, 1)
            pool.memset(low[:], 1.0).then_inc(pre, 1)
            pool.wait_ge(pre, 2)
            pool.affine_select(out=tri[:], in_=tri[:], compare_op=ALU.is_gt, fill=0.0, base=0,
                               pattern=[[1, EPG], [-1, EPG]], channel_multiplier=0).then_inc(consts, 1)
            pool.affine_select(out=low[:], in_=low[:], compare_op=ALU.is_gt, fill=0.0, base=0,
                               pattern=[[1, P]], channel_multiplier=-1).then_inc(consts, 1)
            pool.memset(ones[:], 1.0).then_inc(consts, 1)
            pool.memset(zero[:], 0.0).then_inc(consts, 1)
            pool.iota(ip[:], [[0, NT * NE]], base=0, channel_multiplier=1, **kw).then_inc(consts, 1)
            pool.iota(it[:], [[1, NT], [0, NE]], base=0, channel_multiplier=0, **kw).then_inc(consts, 1)
            pool.memset(codes[:, :, :, 2:3], 1.0).then_inc(consts, 1)
            pool.memset(cum[:, 0, :], 0.0).then_inc(consts, 1)

        @block.vector
        def _(dve):
            step = Chain(dve, dve_step)
            step(dve.tensor_copy(gl[:], lg[:, :, 0:NG]))
            step(dve.tensor_copy(el[:].rearrange("p (t g) e -> p t (g e)", g=NG), lg[:, :, NG:NG + NE]))
            dve.wait_ge(consts, 8)
            for s, (l, a, n) in enumerate(((gl, NT, NG), (el, TG, EPG))):
                flat = lambda buf: buf[:].rearrange("p a i j -> p (a i j)")[:, 0:a * n * n].rearrange(
                    "p (a i j) -> p a i j", i=n, j=n)
                lj = l[:].unsqueeze(2).to_broadcast([P, a, n, n])
                li = l[:].unsqueeze(3).to_broadcast([P, a, n, n])
                step(dve.tensor_tensor(flat(cmp), lj, li, ALU.is_gt))
                step(dve.tensor_tensor(flat(eq), lj, li, ALU.is_equal))
                step(dve.tensor_tensor(flat(eq), flat(eq), tri[:, 0:n, 0:n].unsqueeze(1).to_broadcast([P, a, n, n]),
                                       ALU.mult))
                step(dve.tensor_tensor(flat(cmp), flat(cmp), flat(eq), ALU.add))
                step(dve.tensor_reduce(rank[s][:], flat(cmp), AX.X, ALU.add))
                step(dve.tensor_scalar(sel[s][:], rank[s][:], 2.0, None, ALU.is_lt))
                step(dve.tensor_reduce(mx[s][:], l[:], AX.X, ALU.max))
                dve.tensor_tensor(gate[s][:], l[:], mx[s][:].unsqueeze(2).to_broadcast([P, a, n]),
                                  ALU.subtract).then_inc(exp_in, 1)
                dve.wait_ge(exp_out, s + 1)
                step(dve.tensor_tensor(gate[s][:], gate[s][:], sel[s][:], ALU.mult))
                step(dve.tensor_reduce(mx[s][:], gate[s][:], AX.X, ALU.add))
                step(dve.reciprocal(mx[s][:], mx[s][:]))
                step(dve.tensor_tensor(gate[s][:], gate[s][:], mx[s][:].unsqueeze(2).to_broadcast([P, a, n]),
                                       ALU.mult))
            g4 = lambda a: a[:].rearrange("p t g -> p (t g)").unsqueeze(2).to_broadcast([P, TG, EPG])
            dve.tensor_tensor(sele[:], sel[1][:], g4(sel[0]), ALU.mult).then_inc(sel_ready, 1)
            dve.tensor_tensor(comb[:], gate[1][:], g4(gate[0]), ALU.mult).then_inc(comb_ready, 1)
            dve.wait_ge(comb_ready, 1)
            c3 = lambda j: codes[:, :, :, j]
            combf = comb[:].rearrange("p (t g) e -> p t (g e)", g=NG)
            restf = rest[:].rearrange("p (t g) e -> p t (g e)", g=NG)
            step(dve.tensor_copy(c3(3), combf))
            step(dve.tensor_tensor(restf, combf, c3(3), ALU.subtract))
            step(dve.tensor_copy(c3(4), restf))
            step(dve.tensor_tensor(c3(5), restf, c3(4), ALU.subtract))
            step(dve.tensor_copy(c3(0), ip[:]))
            step(dve.tensor_copy(c3(1), it[:]))
            dve.wait_ge(counted, 2)
            step(dve.tensor_copy(tot[:].rearrange("p t e -> p (t e)"), PT[:]))
            for t in range(NT):
                step(dve.tensor_tensor(cum[:, t + 1, :], cum[:, t, :], tot[:, t, :], ALU.add))
            step(dve.tensor_tensor(posm[:].rearrange("p t e -> p (t e)"), PW[:],
                                   cum[:, 0:NT, :].rearrange("p t e -> p (t e)"), ALU.add))
            selef = sele[:].rearrange("p (t g) e -> p t (g e)", g=NG)
            step(dve.tensor_scalar(posm[:], posm[:], 1.0, None, ALU.add))
            step(dve.tensor_tensor(posm[:], posm[:], selef, ALU.mult))
            step(dve.tensor_scalar(posm[:], posm[:], -1.0, None, ALU.add))
            step(dve.tensor_scalar(cf[:, 0, :], cum[0:1, NT, :], float(SLOT - 1), None, ALU.add))
            step(dve.tensor_copy(ci[:], cf[:, 0, :]))
            step(dve.tensor_scalar(ci[:], ci[:], SLOT.bit_length() - 1, None, ALU.logical_shift_right))
            step(dve.tensor_copy(cf[:, 0, :], ci[:]))
            step(dve.tensor_scalar(cf[:, 0, :], cf[:, 0, :], 1.0, None, ALU.max))
            step(dve.tensor_copy(ntile[:], cf[:, 0, :]))
            step(dve.tensor_tensor_scan(cf[:, 1, :], ones[0:1, 0:NE], cf[:, 0, :], 0.0, ALU.mult, ALU.add))
            step(dve.tensor_tensor(cf[:, 1, :], cf[:, 1, :], cf[:, 0, :], ALU.subtract))
            step(dve.tensor_copy(tstart[:], cf[:, 1, :]))
            for j in range(3):
                dve.wait_ge(turned, j + 1)
                dve.tensor_copy(cT[:, 4 * j:4 * j + width[j], :], T[j][:, 0:width[j], :]).then_inc(copied, 1)
            for t in range(NT):
                for j in range(2):
                    col = x1[:, t, j * 384:(j + 1) * 384]
                    dve.wait_ge(mm, 2 * t + j + 1)
                    dve.tensor_tensor(col, Y[j][:], col, ALU.add).then_inc(summed, 1)

        @block.scalar
        def _(act):
            for s in range(2):
                act.wait_ge(exp_in, s + 1)
                act.activation(gate[s][:], gate[s][:], ACT.Exp).then_inc(exp_out, 1)

        @block.tensor
        def _(pe):
            pe.wait_ge(sel_ready, 1)
            pe.wait_ge(consts, 8)
            rhs = sele[:].rearrange("p a e -> p (a e)")
            pe.matmul(PW[:], low[:], rhs, start=True, stop=True).then_inc(counted, 1)
            pe.matmul(PT[:], ones[:], rhs, start=True, stop=True).then_inc(counted, 1)
            pe.wait_ge(comb_ready, 1)
            pe.wait_ge(b2_loaded, 16)
            for j in range(3):
                for t in range(width[j]):
                    tt = 4 * j + t
                    last = pe.transpose(T[j][:, t, :], comb[:, tt * NG:(tt + 1) * NG, :].rearrange("p a e -> p (a e)"),
                                        ident[0:P, 0:P])
                last.then_inc(turned, 1)
            pe.wait_ge(copied, 3)
            for t in range(NT):
                for j in range(2):
                    if t >= 1:
                        pe.wait_ge(summed, 2 * (t - 1) + j + 1)
                    pe.matmul(Y[j][:], cT[:, t, :], b2s[:, j * 384:(j + 1) * 384], start=True, stop=True
                              ).then_inc(mm, 1)


def expert_phase(nc, cx, W1, b1, W2, xn2_dram, out, ident, codes, posm, ntile, tstart):
    NB = 4
    (consts, q_ready, ids_done, idx_ready, gathered, x_turned, xT_d, xT_a, gemm1, h_biased, h_gelu, h_turned,
     hT_ready, gemm2, y_d, y_a, added, flat, g_ready) = (
        cx.sem("ex_" + s) for s in
        ("consts", "q_ready", "ids_done", "idx_ready", "gathered", "x_turned", "xT_d", "xT_a", "gemm1", "h_biased",
         "h_gelu", "h_turned", "hT_ready", "gemm2", "y_d", "y_a", "added", "flat", "g_ready"))
    w_loaded = [cx.sem(f"ex_w_loaded{b}") for b in range(NB)]
    passed = cx.sem("ex_passed")
    dve_step = cx.sem("ex_step")
    STEPS = 8
    CONSTS = 11
    with ExitStack() as st:
        w1 = sb(nc, st, "ex_w1", [128, NB, KD, FM])
        w2 = sb(nc, st, "ex_w2", [128, NB, KM, D])
        b1r = sb(nc, st, "ex_b1", [SLOT, NB, FM])
        iot = sb(nc, st, "ex_iota", [P, SLOT])
        pad = sb(nc, st, "ex_pad", [SLOT, 1])
        rel = sb(nc, st, "ex_rel", [P, NT])
        Q = sb(nc, st, "ex_Q", [P, NT, SLOT], BF16)
        cod = sb(nc, st, "ex_cod", [SLOT, 6])
        idf = sb(nc, st, "ex_idf", [SLOT, 2])
        found, waiting, leaving = (sb(nc, st, "ex_" + s, [SLOT, 2]) for s in ("found", "waiting", "leaving"))
        idG = sb(nc, st, "ex_idG", [SLOT, 1], I32)
        idS = sb(nc, st, "ex_idS", [SLOT, 1], I32)
        gS = sb(nc, st, "ex_gS", [SLOT, 1])
        X = sb(nc, st, "ex_X", [SLOT, D])
        xT = sb(nc, st, "ex_xT", [128, KD, SLOT])
        h = sb(nc, st, "ex_h", [SLOT, FM])
        hT = sb(nc, st, "ex_hT", [128, KM, SLOT])
        y = sb(nc, st, "ex_y", [SLOT, D])
        PI = pb(nc, st, "ex_PI", [SLOT, 6])
        TX = [pb(nc, st, f"ex_TX{j}", [128, 3, SLOT]) for j in range(2)]
        PH = pb(nc, st, "ex_PH", [SLOT, FM])
        TH = pb(nc, st, "ex_TH", [128, KM, SLOT])
        PY = [pb(nc, st, f"ex_PY{j}", [SLOT, 384]) for j in range(2)]
        block = st.enter_context(nc.Block())

        def turns(eng, turn, body, enter=None):
            eng.reg_mov(turn, 1)
            with eng.Fori(0, NE // NB) as i:
                for b in range(NB):
                    if enter is not None:
                        enter(i, b)
                    count = eng.value_load(ntile[0:1, bass.ds(i * NB + b, 1)], min_val=1, max_val=NT)
                    with eng.Fori(0, count) as _:
                        body(eng.snap(turn), b)
                        eng.reg_add(turn, turn, 1)
            return eng.snap(turn)

        @block.sync
        def _(sp):
            def load_first(e, b):
                sp.dma_start(w1[:, b, :, :], W1[e, :, :].rearrange("o (k p) n -> p (o k) n", p=128)
                             ).then_inc(w_loaded[b], 16)

            def load_second(e, b):
                sp.dma_start(b1r[:, b, :], b1[e, :].partition_broadcast(SLOT)).then_inc(w_loaded[b], 16)
                sp.dma_start(w2[:, b, :, :], W2[e, :, :].rearrange("o (k p) n -> p (o k) n", p=128)
                             ).then_inc(w_loaded[b], 16)

            for b in range(NB):
                load_first(slice(b, b + 1), b)
                load_second(slice(b, b + 1), b)
            with sp.Fori(1, NE // NB) as i:
                for b in range(NB):
                    done = sp.value_load(tstart[0:1, bass.ds(i * NB + (b + 1 - NB), 1)], min_val=0, max_val=MAXT)
                    sp.wait_ge(gemm1, done + 2)
                    load_first(bass.ds(i * NB + b, 1), b)
                    sp.wait_ge(gemm2, done + 3)
                    load_second(bass.ds(i * NB + b, 1), b)

        @block.gpsimd
        def _(pool):
            kw = dict(allow_small_or_imprecise_dtypes=True)
            pool.iota(iot[:], [[1, SLOT]], base=0, channel_multiplier=0, **kw).then_inc(consts, 1)
            pool.iota(pad[:], [[0, 1]], base=N, channel_multiplier=1, **kw).then_inc(consts, 1)
            for m in (found, waiting, leaving):
                pool.iota(m[:, 0:1], [[0, 1]], base=N, channel_multiplier=1, **kw).then_inc(consts, 1)
                pool.memset(m[:, 1:2], 0.0).then_inc(consts, 1)
            pool.memset(X[:], 0.0).then_inc(consts, 1)
            pool.memset(h[:], 0.0).then_inc(consts, 1)
            pool.memset(hT[:], 0.0).then_inc(consts, 1)
            pool.wait_ge(consts, CONSTS)

            def scatter(n):
                pool.wait_ge(y_d, n)
                pool.wait_ge(y_a, n)
                pool.sem_inc(passed, 1)
                pool.indirect_dma_start(out, bass.IndirectOffsetOnAxis(ap=idS[:, 0:1], axis=0), y[:], None,
                                        compute_op=ALU.add).then_inc(added, 16)

            def body(n, b):
                scatter(n)
                pool.wait_ge(idx_ready, n)
                pool.wait_ge(x_turned, n)
                pool.sem_inc(passed, 1)
                pool.indirect_dma_start(X[:], None, xn2_dram, bass.IndirectOffsetOnAxis(ap=idG[:, 0:1], axis=0)
                                        ).then_inc(gathered, 16)

            with pool.register("ex_turn_pool") as turn:
                end = turns(pool, turn, body)
                for k in range(3):
                    scatter(end + k)
                pool.wait_ge(added, (end + 2) * 16)

        @block.vector
        def _(dve):
            def steps(n):
                state = [0]

                def step(ins):
                    state[0] += 1
                    ins.then_inc(dve_step, 1)
                    dve.wait_ge(dve_step, n * STEPS + (state[0] - STEPS))
                return step, state

            def turn_x(n):
                dve.wait_ge(x_turned, n)
                dve.wait_ge(gemm1, n)
                dve.tensor_copy(xT[:, 0:3, :], TX[0][:]).then_inc(xT_d, 1)

            def turn_h(n):
                dve.wait_ge(h_turned, n)
                dve.wait_ge(gemm2, n)
                dve.tensor_copy(hT[:], TH[:]).then_inc(hT_ready, 1)

            def find(step, n):
                dve.wait_ge(ids_done, n + 1)
                step(dve.tensor_copy(cod[:], PI[:]))
                step(dve.tensor_copy(waiting[:], found[:]))
                step(dve.scalar_tensor_tensor(idf[:, 0:1], cod[:, 1:2], float(P), cod[:, 0:1], ALU.mult, ALU.add))
                step(dve.scalar_tensor_tensor(idf[:, 1:2], cod[:, 2:3], -1.0, pad[:], ALU.add, ALU.mult))
                step(dve.scalar_tensor_tensor(found[:, 1:2], cod[:, 5:6], cod[:, 4:5], cod[:, 3:4], ALU.add, ALU.add))
                step(dve.tensor_tensor(found[:, 0:1], idf[:, 0:1], idf[:, 1:2], ALU.subtract))
                dve.wait_ge(gathered, n * 16 - 16)
                dve.tensor_copy(idG[:], found[:, 0:1]).then_inc(idx_ready, 1)

            def second(n, step=None, then=None):
                dve.wait_ge(added, n * 16 - 16)
                dve.tensor_copy(idS[:], leaving[:, 0:1])
                dve.tensor_copy(gS[:], leaving[:, 1:2]).then_inc(g_ready, 1)
                dve.wait_ge(g_ready, n)
                if then is not None:
                    step(dve.tensor_copy(leaving[:], then[:]))
                dve.wait_ge(gemm2, n)
                dve.tensor_scalar(y[:, 0:384], PY[0][:], gS[:], None, ALU.mult).then_inc(y_d, 1)

            def bias(n, b_prev):
                dve.wait_ge(gemm1, n + 1)
                dve.wait_ge(h_turned, n)
                dve.tensor_tensor(h[:].unsqueeze(1), PH[:].unsqueeze(1), b1r[:, bass.ds(b_prev, 1), :], ALU.add
                                  ).then_inc(h_biased, 1)

            dve.wait_ge(consts, CONSTS)
            with dve.register("ex_b_prev") as b_prev, dve.register("ex_turn_dve") as turn:
                dve.reg_mov(b_prev, 0)

                def enter(i, b):
                    dve.wait_ge(w_loaded[b], i * 48 + 48)
                    dve.tensor_copy(rel[:], posm[:, :, bass.ds(i * NB + b, 1)].rearrange("p t o -> p (t o)")
                                    ).then_inc(flat, 1)
                    dve.wait_ge(flat, i * NB + (b + 1))

                def body(n, b):
                    step, state = steps(n)
                    dve.wait_ge(ids_done, n)
                    dve.tensor_tensor(Q[:], rel[:].unsqueeze(2).to_broadcast([P, NT, SLOT]),
                                      iot[:].unsqueeze(1).to_broadcast([P, NT, SLOT]), ALU.is_equal
                                      ).then_inc(q_ready, 1)
                    second(n, step, waiting)
                    turn_h(n)
                    turn_x(n)
                    dve.wait_ge(q_ready, n)
                    step(dve.tensor_scalar(rel[:], rel[:], -float(SLOT), None, ALU.add))
                    find(step, n)
                    bias(n, dve.snap(b_prev))
                    assert state[0] == STEPS
                    dve.reg_mov(b_prev, b)

                end = turns(dve, turn, body, enter)
                last = dve.snap(b_prev)
                step, state = steps(end)
                second(end, step, waiting)
                turn_h(end)
                turn_x(end)
                bias(end, last)
                second(end + 1, step, found)
                turn_h(end + 1)
                second(end + 2)

        @block.scalar
        def _(act):
            def turn_x(n):
                act.wait_ge(x_turned, n)
                act.wait_ge(gemm1, n)
                act.activation(xT[:, 3:6, :], TX[1][:], ACT.Copy).then_inc(xT_a, 1)

            def second(n):
                act.wait_ge(gemm2, n)
                act.wait_ge(g_ready, n)
                act.activation(y[:, 384:768], PY[1][:], ACT.Copy, scale=gS[:]).then_inc(y_a, 1)

            def gelu(n):
                act.wait_ge(h_biased, n)
                act.activation(h[:], h[:], ACT.Gelu).then_inc(h_gelu, 1)

            act.wait_ge(consts, CONSTS)

            def body(n, b):
                second(n)
                turn_x(n)
                gelu(n)

            with act.register("ex_turn_act") as turn:
                end = turns(act, turn, body)
                body(end, None)
                second(end + 1)
                second(end + 2)

        @block.tensor
        def _(pe):
            pe.wait_ge(consts, CONSTS)

            def find(n, e):
                pe.wait_ge(q_ready, n)
                pe.wait_ge(idx_ready, n - 1)
                for t in range(NT):
                    last = pe.matmul(PI[:], Q[:, t, :], codes[:, t, bass.ds(e, 1), :].rearrange("p o c -> p (o c)"),
                                     start=(t == 0), stop=(t == NT - 1))
                last.then_inc(ids_done, 1)

            def turn_x(n):
                pe.wait_ge(gathered, n * 16 - 16)
                pe.wait_ge(xT_d, n - 1)
                pe.wait_ge(xT_a, n - 1)
                for k in range(KD):
                    last = pe.transpose(TX[k // 3][:, k % 3, :], X[:, k * 128:(k + 1) * 128], ident[:])
                last.then_inc(x_turned, 1)

            def turn_h(n):
                if n is not None:
                    pe.wait_ge(h_gelu, n)
                    pe.wait_ge(hT_ready, n)
                for k in range(KM):
                    last = pe.transpose(TH[:, k, :], h[:, k * 128:(k + 1) * 128], ident[:])
                last.then_inc(h_turned, 1)

            def second(n, b):
                if n is not None:
                    pe.wait_ge(hT_ready, n)
                    pe.wait_ge(y_d, n)
                    pe.wait_ge(y_a, n)
                for j in range(2):
                    for k in range(KM):
                        last = pe.matmul(PY[j][:], hT[:, k, :], w2[:, bass.ds(b, 1), k, j * 384:(j + 1) * 384],
                                         start=(k == 0), stop=(k == KM - 1))
                last.then_inc(gemm2, 1)

            def first(n, b):
                pe.wait_ge(xT_d, n)
                pe.wait_ge(xT_a, n)
                pe.wait_ge(h_biased, n - 1)
                for k in range(KD):
                    last = pe.matmul(PH[:], xT[:, k, :], w1[:, bass.ds(b, 1), k, :], start=(k == 0),
                                     stop=(k == KD - 1))
                last.then_inc(gemm1, 1)

            pe.sem_inc(ids_done, 1)
            pe.sem_inc(gemm1, 1)
            with pe.register("ex_b1_prev") as b1_prev, pe.register("ex_b2_prev") as b2_prev, \
                    pe.register("ex_turn_pe") as turn:
                pe.reg_mov(b1_prev, 0)
                pe.reg_mov(b2_prev, 0)
                expert = [None]
                pe.wait_ge(w_loaded[0], 48)
                second(None, 0)
                turn_h(None)

                def enter(i, b):
                    pe.wait_ge(w_loaded[b], i * 48 + 48)
                    expert[0] = i * NB + b

                def body(n, b):
                    turn_x(n)
                    find(n, expert[0])
                    first(n, pe.snap(b1_prev))
                    second(n, pe.snap(b2_prev))
                    turn_h(n)
                    pe.reg_mov(b2_prev, pe.snap(b1_prev))
                    pe.reg_mov(b1_prev, b)

                end = turns(pe, turn, body, enter)
                turn_x(end)
                first(end, pe.snap(b1_prev))
                second(end, pe.snap(b2_prev))
                turn_h(end)
                second(end + 1, pe.snap(b1_prev))


def host_layout(i):
    import numpy as np
    o = dict(i)
    for name in ("L0_mix_qkv_w", "L0_mix_proj_w", "L0_mix_rf"):
        o[name] = np.ascontiguousarray(np.asarray(i[name]).T)
    o["L0_ffn_Wge"] = np.asarray(i["L0_ffn_Wge"]).transpose(1, 0, 2).reshape(D, NE)
    return {k: np.ascontiguousarray(v) for k, v in o.items()}


def build(nc, ins, out, stages=99):
    x = ins["x"]
    dram = lambda name, *shape: nc.dram_tensor(name, shape, F32).ap()
    with ExitStack() as st:
        cx = Ctx(nc)
        x1_dram = dram("x1_dram", N, D)
        alT_dram = dram("alT_dram", 2 * H1, N)
        mT_dram = dram("mT_dram", H1, N)
        al2T_dram = dram("al2T_dram", 2, N)
        m2T_dram = dram("m2T_dram", 1, N)
        ct_dram = dram("ct_dram", NW * 128, SLO)
        c_dram = dram("c_dram", NT, P, N)
        mask_dram = dram("mask_dram", NT, P, N)
        h1T_dram = dram("h1T_dram", NT, 128, KF * P)
        ident = sb(nc, st, "ident", [128, 128])
        with ExitStack() as st1:
            xnT = sb(nc, st1, "xnT", [128, KD, N])
            wa = sb(nc, st1, "gnn_wa", [128, KD, 2 * H1])
            attn_scope = ExitStack()
            attn = sb(nc, attn_scope, "attn", [P, NT, D])
            w_proj = sb(nc, attn_scope, "proj_w", [128, KD, D])
            proj_loaded = cx.sem("proj_w_loaded")
            with ExitStack() as st2:
                w_qkv = sb(nc, st2, "mix_w", [128, KD, 3, D // 2])
                b_qkv = sb(nc, st2, "mix_brow", [P, 3, D // 2])
                mix_loaded = cx.sem("mix_w_loaded")

                def load_half(half):
                    return lambda sp: load_mix_weights(sp, half, ins["L0_mix_qkv_w"], ins["L0_mix_qkv_b"], w_qkv,
                                                       b_qkv, mix_loaded)

                def load_proj(sp):
                    sp.dma_start(w_proj[:], ins["L0_mix_proj_w"].rearrange("(k p) n -> p k n", p=128)
                                 ).then_inc(proj_loaded, 16)

                norm_phase(nc, cx, x, ident, xnT, load_half(0))
                for half in range(2):
                    mix_half_phase(nc, cx, half, ins["L0_mix_rf"], xnT, ident, w_qkv, b_qkv, mix_loaded, attn,
                                   ins["L0_gnn_W1"], ins["L0_gnn_att_src1"], ins["L0_gnn_att_dst1"], wa,
                                   load_half(1) if half == 0 else load_proj)
            proj_phase(nc, cx, attn, w_proj, proj_loaded, ins["L0_mix_proj_b"], ins["L0_gnn_b2"], x, x1_dram, ident)
            attn_scope.close()
            if stages == 3:
                return
            al = sb(nc, st1, "al", [P, NT, 2 * H1])
            h = sb(nc, st1, "h", [P, NT, H1, C1 + 1])
            with ExitStack() as st2:
                w1 = sb(nc, st2, "gnn_w1", [128, KD, F1])
                w1_loaded = cx.sem("w1_loaded")
                keyT = sb(nc, st2, "keyT", [128, EROWS])
                sloT = sb(nc, st2, "sloT", [128, EROWS])
                spans = sb(nc, st2, "spans", [1, 2 * NW], I32)
                with ExitStack() as st3:
                    block = st3.enter_context(nc.Block())
                    logits(nc, cx, st3, block, ins["L0_gnn_W1"], xnT, ident, wa, w1, al, alT_dram, w1_loaded)
                    edge_table(nc, cx, st3, block, ins["src"], ins["dst"], ident, keyT, sloT, spans)
                count_phase(nc, cx, keyT, sloT, spans, ct_dram, xnT, w1, w1_loaded, h)
            mask_phase(nc, cx, ct_dram, c_dram, mask_dram, alT_dram, ident, al, mT_dram)
            if stages == 4:
                return
            cx.clear()
            gat1_phase(nc, cx, ins["L0_gnn_b1"], h, al, alT_dram, mT_dram, c_dram, h1T_dram, ident)
        x1 = sb(nc, st, "x1", [P, NT, D])
        with ExitStack() as st1:
            h2 = sb(nc, st1, "h2", [P, NT, D + 1])
            al2 = sb(nc, st1, "al2", [P, NT, 2])
            gat2_project_phase(nc, cx, ins["L0_gnn_W2"], ins["L0_gnn_att_src2"], ins["L0_gnn_att_dst2"], h1T_dram,
                               ident, h2, al2, al2T_dram)
            gat2_max_phase(nc, cx, mask_dram, al2, al2T_dram, m2T_dram, ident)
            if stages == 5:
                return
            gat2_phase(nc, cx, al2, al2T_dram, m2T_dram, c_dram, h2, x1_dram, x1)
        if stages == 6:
            return
        xn2_dram = dram("xn2_dram", N + SLOT, D)
        codes = sb(nc, st, "codes", [P, NT, NE, 6], BF16)
        posm = sb(nc, st, "posm", [P, NT, NE])
        ntile = sb(nc, st, "ntile", [1, NE], I32)
        tstart = sb(nc, st, "tstart", [1, NE], I32)
        lg = sb(nc, st, "lg", [P, NT, NG + NE])
        route_norm_phase(nc, cx, x1, ins["L0_ffn_Wg"], ins["L0_ffn_Wge"], ins["L0_ffn_bg"], ins["L0_ffn_bge"],
                         xn2_dram, ident, lg)
        route_phase(nc, cx, lg, x1, ins["L0_ffn_b2"], out, ident, codes, posm, ntile, tstart)
        if stages == 7:
            return
        expert_phase(nc, cx, ins["L0_ffn_W1"], ins["L0_ffn_b1"], ins["L0_ffn_W2"], xn2_dram, out, ident, codes, posm,
                     ntile, tstart)


def kernel(**inputs):
    import concourse.bacc as bacc
    from concourse.bass_utils import run_bass_kernel_spmd

    nc = bacc.Bacc("TRN2", target_bir_lowering=False, num_devices=1)
    arrays = host_layout(inputs)
    ins = {k: nc.dram_tensor(f"in_{k}", a.shape, mybir.dt.from_np(a.dtype), kind="ExternalInput").ap()
           for k, a in arrays.items()}
    out = nc.dram_tensor("out_rows", (N + SLOT, D), F32, kind="ExternalOutput").ap()
    build(nc, ins, out)
    r = run_bass_kernel_spmd(nc, [{f"in_{k}": a for k, a in arrays.items()}], core_ids=[0])
    return r.results[0]["out_rows"][0:N]
```

```python
from contextlib import ExitStack

import concourse.bass as bass
from concourse import mybir

F32 = mybir.dt.float32
F16 = mybir.dt.float16
BF16 = mybir.dt.bfloat16
I32 = mybir.dt.int32
ALU = mybir.AluOpType
ACT = mybir.ActivationFunctionType
AX = mybir.AxisListType

N = 1250
NT = 10
P = N // NT
D = 768
KD = D // 128
H1 = 4
C1 = 512
F1 = H1 * C1
KF = F1 // 128
CH = 3
CHW = [416, 416, 418]
CHO = [0, 416, 832]
EDGES = 41250
ER = 128
RB = 4
EROWS = 324
EG = 3
EGP = EROWS // EG
WIN = 32
NW = 40
SPLIT = 4
SLO = 314
PADNODE = NW * WIN - 1
BIG = 1.0e30
MH = 8
MD = D // MH
RF = 256
NE = 32
NG = 4
EPG = NE // NG
NB = 4
FM = 384
KM = FM // 128
SLOT = 128
MAXT = (4 * N + NE * (SLOT - 1)) // SLOT + NE // 4
SLOPE = 0.2
EPS = 1e-5


class Chain:

    def __init__(self, eng, sem):
        self.eng, self.sem, self.base, self.i, self.per, self.j = eng, sem, 0, 0, 0, 0

    def start(self, i, per):
        self.base += self.j
        self.i, self.per, self.j = i, per, 0

    def end(self, count):
        assert self.j == self.per, (self.j, self.per)
        self.base += count * self.per
        self.i, self.per, self.j = 0, 0, 0

    def __call__(self, ins):
        self.j += 1
        ins.then_inc(self.sem, 1)
        self.eng.wait_ge(self.sem, self.i * self.per + (self.base + self.j))


class Ctx:

    def __init__(self, nc):
        self.nc, self.sems = nc, []

    def sem(self, name):
        self.sems.append(self.nc.alloc_semaphore(name=name))
        return self.sems[-1]

    def clear(self):
        self.nc.clear_and_free_semaphores(self.sems)
        self.sems = []
        with self.nc.Block():
            pass


def sb(nc, st, name, shape, dt=F32):
    return st.enter_context(nc.sbuf_tensor(name, shape, dt))


def pb(nc, st, name, shape, dt=F32):
    return st.enter_context(nc.psum_tensor(name, shape, dt))


def refine_rstd(step, dve, rstd, std, veps, tmp):
    step(dve.reciprocal(rstd, std))
    step(dve.tensor_tensor(tmp, rstd, rstd, ALU.mult))
    step(dve.tensor_tensor(tmp, tmp, veps, ALU.mult))
    step(dve.tensor_scalar(tmp, tmp, -0.5, 1.5, ALU.mult, ALU.add))
    step(dve.tensor_tensor(rstd, rstd, tmp, ALU.mult))


def norm_phase(nc, cx, x, ident, xnT, load_next):
    x_loaded = [cx.sem(f"norm_x_loaded{h}") for h in range(2)]
    stats_done, sqrt_done, xn_ready, transposed, used_dve, used_act, id_done = (
        cx.sem(f"norm_{s}") for s in
        ("stats_done", "sqrt_done", "xn_ready", "transposed", "used_dve", "used_act", "id_done"))
    dve_step = cx.sem("norm_dve_step")
    HT = NT // 2
    with ExitStack() as st:
        xa = sb(nc, st, "xa", [P, NT, D])
        stats = sb(nc, st, "stats", [P, NT, 2, 6])
        mv = sb(nc, st, "mv", [P, NT, 2])
        std = sb(nc, st, "std", [P, NT])
        veps = sb(nc, st, "veps", [P, NT])
        tmp = sb(nc, st, "tmp", [P, NT])
        rstd = sb(nc, st, "rstd", [P, NT])
        xn = [sb(nc, st, f"xn{b}", [P, D]) for b in range(2)]
        tp = [[pb(nc, st, f"tp{b}{h}", [128, 3, P]) for h in range(2)] for b in range(2)]
        block = st.enter_context(nc.Block())

        @block.sync
        def _(sp):
            for h in range(2):
                sp.dma_start(xa[:, h * HT:(h + 1) * HT, :], x.rearrange("(t p) d -> p t d", p=P)
                             [:, h * HT:(h + 1) * HT, :]).then_inc(x_loaded[h], 16)
            load_next(sp)

        @block.gpsimd
        def _(pool):
            pool.memset(ident[:], 0.0).then_inc(id_done, 1)
            pool.wait_ge(id_done, 1)
            pool.affine_select(out=ident[:], in_=ident[:], compare_op=ALU.not_equal, fill=1.0, base=0,
                               pattern=[[-1, 128]], channel_multiplier=1).then_inc(id_done, 1)

        @block.vector
        def _(dve):
            step = Chain(dve, dve_step)
            for t in range(NT):
                if t % HT == 0:
                    dve.wait_ge(x_loaded[t // HT], 16)
                for h in range(2):
                    last = dve.bn_stats(stats[:, t, h, :], xa[:, t, h * 384:(h + 1) * 384])
            step(last)
            for t in range(NT):
                last = dve.bn_aggr(mv[:, t, :], stats[:, t, :, :])
            step(last)
            dve.tensor_scalar(veps[:], mv[:, :, 1], EPS, None, ALU.add).then_inc(stats_done, 1)
            dve.wait_ge(sqrt_done, 1)
            refine_rstd(step, dve, rstd[:], std[:], veps[:], tmp[:])

            def scaled(t, b):
                dve.wait_ge(transposed, t + 1)
                dve.tensor_scalar(xn[b][:], xa[:, bass.ds(t, 1), :], mv[:, bass.ds(t, 1), 0],
                                  rstd[:, bass.ds(t, 1)], ALU.subtract, ALU.mult).then_inc(xn_ready, 1)

            def copy(t, b):
                dve.wait_ge(transposed, t + 3)
                dve.tensor_copy(xnT[:, 0:3, bass.ds(t * P, P)], tp[b][0][:]).then_inc(used_dve, 1)

            scaled(0, 0)
            with dve.Fori(0, NT // 2 - 1) as i:
                for b in range(2):
                    scaled(i * 2 + (b + 1), 1 - b)
                    copy(i * 2 + b, b)
            scaled(NT - 1, 1)
            copy(NT - 2, 0)
            copy(NT - 1, 1)

        @block.scalar
        def _(act):
            act.wait_ge(stats_done, 1)
            act.activation(std[:], veps[:], ACT.Sqrt).then_inc(sqrt_done, 1)
            with act.Fori(0, NT // 2) as i:
                for b in range(2):
                    act.wait_ge(transposed, i * 2 + (b + 3))
                    act.activation(xnT[:, 3:6, bass.ds(i * (2 * P) + b * P, P)], tp[b][1][:],
                                   ACT.Copy).then_inc(used_act, 1)

        @block.tensor
        def _(pe):
            pe.sem_inc(transposed, 2)
            pe.sem_inc(used_dve, 2)
            pe.sem_inc(used_act, 2)
            pe.wait_ge(id_done, 2)
            with pe.Fori(0, NT // 2) as i:
                for b in range(2):
                    pe.wait_ge(xn_ready, i * 2 + (b + 1))
                    pe.wait_ge(used_dve, i * 2 + (b + 1))
                    pe.wait_ge(used_act, i * 2 + (b + 1))
                    for k in range(KD):
                        last = pe.transpose(tp[b][k // 3][:, k % 3, :], xn[b][:, k * 128:(k + 1) * 128],
                                            ident[0:P, 0:P])
                    last.then_inc(transposed, 1)


def numerator(nc, cx, tag, half, rfT, qT, kv, attn, a_loaded, slice_loaded, ws, ab, wa, load_next):
    KH = KD // 2
    HH, A, HT = MH // 2, MD + 1, NT // 2
    feat, exped, num, num_used = (cx.sem(tag + s) for s in ("feat", "exped", "num", "num_used"))
    dve_step = cx.sem(tag + "num_step")
    wa_step = cx.sem(tag + "wa_step")
    with ExitStack() as st:
        junk = sb(nc, st, tag + "junk", [128, 2, C1])
        phiq = [sb(nc, st, tag + f"phiq{b}", [128, 2, N]) for b in range(2)]
        den = sb(nc, st, tag + "den", [P, 2, HT])
        F = [pb(nc, st, tag + f"F{j}", [128, 512]) for j in range(6)]
        R = [pb(nc, st, tag + f"R{j}", [P, HT, A]) for j in range(2)]
        block = st.enter_context(nc.Block())

        @block.sync
        def _(sp):
            load_next(sp)

        @block.tensor
        def _(pe):
            pe.sem_inc(num, 4)
            with pe.Fori(0, HH // 2) as i:
                for b in range(2):
                    for j in range(6):
                        m, c = j // CH, j % CH
                        pe.wait_ge(exped, i * 12 + (6 * b + j + 1))
                        pe.matmul(F[j][:, 0:CHW[c]], rfT[:, m * 128:(m + 1) * 128],
                                  qT[:, bass.ds(i * 2 + b, 1), CHO[c]:CHO[c] + CHW[c]],
                                  start=True, stop=True).then_inc(feat, 1)
                for b in range(2):
                    pe.wait_ge(exped, i * 12 + (6 * b + 12))
                    for j in range(2):
                        pe.wait_ge(num_used, i * 4 + (2 * b + j + 1))
                        for t in range(HT):
                            tt = j * HT + t
                            for m in range(2):
                                last = pe.matmul(R[j][:, t, :], phiq[b][:, m, tt * P:(tt + 1) * P],
                                                 kv[:, bass.ds(i * 2 + b, 1), m, :], start=(m == 0), stop=(m == 1),
                                                 skip_group_check=True)
                        last.then_inc(num, 1)

        @block.scalar
        def _(act):
            act.sem_inc(exped, 6)
            with act.Fori(0, HH // 2) as i:
                for b in range(2):
                    act.wait_ge(num, i * 4 + (2 * b + 2))
                    for j in range(6):
                        m, c = j // CH, j % CH
                        act.wait_ge(feat, i * 12 + (6 * b + j + 1))
                        act.activation(phiq[b][:, m, CHO[c]:CHO[c] + CHW[c]], F[j][:, 0:CHW[c]],
                                       ACT.Exp).then_inc(exped, 1)

        @block.vector
        def _(dve):
            step = Chain(dve, dve_step)
            dve.wait_ge(a_loaded, 32)
            n = 0
            for k in range(KH):
                dve.wait_ge(slice_loaded[k], 16)
                for s in range(2):
                    for h in range(H1):
                        if n >= 2:
                            dve.wait_ge(wa_step, n - 1)
                        col = s * H1 + h
                        dve.tensor_tensor_reduce(out=junk[:, n % 2, :], in0=ws[k][:, h * C1:(h + 1) * C1],
                                                 in1=ab[:, s, h * C1:(h + 1) * C1], scale=1.0, scalar=0.0,
                                                 op0=ALU.mult, op1=ALU.add,
                                                 accum_out=wa[:, half * KH + k, col:col + 1]).then_inc(wa_step, 1)
                        n += 1
            dve.sem_inc(num_used, 2)
            with dve.Fori(0, HH // 2) as i:
                step.start(i, 8)
                for b in range(2):
                    for j in range(2):
                        dve.wait_ge(num, i * 4 + (2 * b + j + 5))
                        dve.wait_ge(num_used, i * 4 + (2 * b + j + 1))
                        step(dve.tensor_scalar(den[:, j, :], R[j][:, :, MD], 1e-6, None, ALU.max))
                        step(dve.reciprocal(den[:, j, :], den[:, j, :]))
                        dve.tensor_tensor(attn[:, j * HT:(j + 1) * HT, bass.ds((i * 2 + b) * MD + half * HH * MD, MD)],
                                          R[j][:, :, 0:MD], den[:, j, :].unsqueeze(2).to_broadcast([P, HT, MD]),
                                          ALU.mult).then_inc(num_used, 1)
            step.end(HH // 2)


def proj_phase(nc, cx, attn, w, w_loaded, proj_b, gnn_b2, x, x1_dram, ident):
    (loaded, x_loaded, staged, turned, copied_a, copied_d, projected, stored, stores) = (
        cx.sem("proj_" + s) for s in ("loaded", "x_loaded", "staged", "turned", "copied_a", "copied_d", "projected",
                                      "stored", "stores"))
    biased = cx.sem("proj_biased")
    with ExitStack() as st:
        bias = sb(nc, st, "proj_bias", [P, 2, D])
        xr = sb(nc, st, "proj_x", [P, NT, D])
        at = sb(nc, st, "proj_at", [P, D])
        aT = [sb(nc, st, f"proj_aT{b}", [128, KD, P]) for b in range(2)]
        TP = [pb(nc, st, f"proj_T{j}", [128, 3, P]) for j in range(2)]
        Y = [pb(nc, st, f"proj_Y{j}", [P, 384]) for j in range(2)]
        block = st.enter_context(nc.Block())

        @block.sync
        def _(sp):
            sp.dma_start(bias[:, 0, :], proj_b.partition_broadcast(P)).then_inc(loaded, 16)
            sp.dma_start(bias[:, 1, :], gnn_b2.partition_broadcast(P)).then_inc(loaded, 16)
            sp.dma_start(xr[:], x.rearrange("(t p) d -> p t d", p=P)).then_inc(x_loaded, 16)
            with sp.Fori(0, NT) as t:
                sp.wait_ge(stored, t * 2 + 4)
                sp.dma_start(x1_dram[bass.ds(t * P, P), :], xr[:, bass.ds(t, 1), :].rearrange("p o d -> p (o d)")
                             ).then_inc(stores, 16)
            sp.wait_ge(stores, 16 * NT)

        @block.gpsimd
        def _(pool):
            with pool.Fori(0, NT) as t:
                pool.wait_ge(turned, t + 1)
                pool.tensor_copy(at[:], attn[:, bass.ds(t, 1), :]).then_inc(staged, 1)

        @block.tensor
        def _(pe):
            pe.sem_inc(turned, 1)
            pe.sem_inc(projected, 4)

            def turn(t):
                pe.wait_ge(staged, t + 1)
                pe.wait_ge(copied_a, t + 1)
                pe.wait_ge(copied_d, t + 1)
                for k in range(KD):
                    last = pe.transpose(TP[k // 3][:, k % 3, :], at[:, k * 128:(k + 1) * 128], ident[0:P, 0:P])
                last.then_inc(turned, 1)

            def project(t, b):
                pe.wait_ge(copied_a, t + 2)
                pe.wait_ge(copied_d, t + 2)
                for j in range(2):
                    pe.wait_ge(stored, 2 * t + (j + 1))
                    for k in range(KD):
                        last = pe.matmul(Y[j][:], aT[b][:, k, :], w[:, k, j * 384:(j + 1) * 384],
                                         start=(k == 0), stop=(k == KD - 1))
                    last.then_inc(projected, 1)

            pe.wait_ge(w_loaded, 16)
            turn(0)
            with pe.Fori(0, NT // 2 - 1) as i:
                for b in range(2):
                    turn(i * 2 + (b + 1))
                    project(i * 2 + b, b)
            turn(NT - 1)
            project(NT - 2, 0)
            project(NT - 1, 1)

        @block.scalar
        def _(act):
            act.sem_inc(copied_a, 1)
            with act.Fori(0, NT // 2) as i:
                for b in range(2):
                    act.wait_ge(turned, i * 2 + (b + 2))
                    act.wait_ge(projected, i * 4 + (2 * b + 2))
                    act.activation(aT[b][:, 0:3, :], TP[0][:], ACT.Copy).then_inc(copied_a, 1)

        @block.vector
        def _(dve):
            dve.sem_inc(copied_d, 1)
            dve.sem_inc(stored, 2)

            def turn(t, b):
                dve.wait_ge(turned, t + 2)
                dve.wait_ge(projected, 2 * t + 2)
                dve.tensor_copy(aT[b][:, 3:6, :], TP[1][:]).then_inc(copied_d, 1)

            def add(t):
                row = xr[:, bass.ds(t, 1), :]
                dve.tensor_tensor(row, row, bias[:, 0:1, :], ALU.add).then_inc(biased, 1)
                dve.wait_ge(biased, t + 2)
                for j in range(2):
                    dve.wait_ge(projected, 2 * t + (j + 5))
                    col = xr[:, bass.ds(t, 1), j * 384:(j + 1) * 384]
                    dve.tensor_tensor(col, Y[j][:].unsqueeze(1), col, ALU.add).then_inc(stored, 1)

            turn(0, 0)
            turn(1, 1)
            dve.wait_ge(loaded, 32)
            dve.tensor_tensor(bias[:, 0, :], bias[:, 0, :], bias[:, 1, :], ALU.add).then_inc(biased, 1)
            dve.wait_ge(x_loaded, 16)
            dve.wait_ge(biased, 1)
            with dve.Fori(0, NT // 2 - 1) as i:
                for b in range(2):
                    add(i * 2 + b)
                    turn(i * 2 + (b + 2), b)
            add(NT - 2)
            add(NT - 1)


def load_mix_weights(sp, half, wqkvT, qkv_b, w, brow, w_loaded):
    HW = D // 2
    for c in range(3):
        cols = slice(c * D + half * HW, c * D + (half + 1) * HW)
        sp.dma_start(w[:, :, c, :], wqkvT[:, cols].rearrange("(k p) n -> p k n", p=128)).then_inc(w_loaded, 16)
        sp.dma_start(brow[:, c, :], qkv_b[cols].partition_broadcast(P)).then_inc(w_loaded, 16)


def mix_half_phase(nc, cx, half, rfT_dram, xnT, ident, w, brow, w_loaded, attn, gnn_w1, a_src, a_dst, wa, load_next):
    HH = MH // 2
    HW = HH * MD
    A = MD + 1
    SCALE = MD ** -0.5
    tag = f"mix{half}_"
    (rf_loaded, staged, q_done, k_done, v_done, q_evac, k_evac, v_evac, qsq, ksq, q_ready, k_ready, q_turned,
     k_turned, qT_done, kT_done, phi_a, phi_b, exp_a, exp_b, kv_step, kv_copied, consts) = (
        cx.sem(tag + s) for s in
        ("rf_loaded", "staged", "q_done", "k_done", "v_done", "q_evac", "k_evac", "v_evac", "qsq", "ksq", "q_ready",
         "k_ready", "q_turned", "k_turned", "qT_done", "kT_done", "phi_a", "phi_b", "exp_a", "exp_b", "kv_step",
         "kv_copied", "consts"))
    dve_step = cx.sem(tag + "dve_step")
    a_loaded = cx.sem(tag + "a_loaded")
    slice_loaded = [cx.sem(tag + f"slice_loaded{k}") for k in range(KD // 2)]
    with ExitStack() as st:
        rfT = sb(nc, st, tag + "rfT", [A, RF])
        qT = sb(nc, st, tag + "qT", [A, HH, N])
        kv = sb(nc, st, tag + "kv", [128, HH, 2, A])
        ws = [sb(nc, st, tag + f"w1_slice{k}", [128, F1]) for k in range(KD // 2)]
        ab = sb(nc, st, tag + "a", [128, 2, F1])
        with ExitStack() as st1:
            xs = [sb(nc, st1, tag + f"xs{b}", [128, KD, P]) for b in range(2)]
            qs = sb(nc, st1, tag + "qs", [P, 2, HH, A])
            sq = sb(nc, st1, tag + "sq", [P, 2, HH, MD])
            nrm = sb(nc, st1, tag + "nrm", [P, 2, HH])
            vs = sb(nc, st1, tag + "vs", [P, HH, A])
            kT = sb(nc, st1, tag + "kT", [A, HH, P])
            phik = sb(nc, st1, tag + "phik", [P, HH, RF])
            zero = sb(nc, st1, tag + "zero", [P, 128])
            G = [pb(nc, st1, tag + f"G{j}", [P, HW]) for j in range(3)]
            TQ = pb(nc, st1, tag + "TQ", [A, HH, P])
            PH = [pb(nc, st1, tag + f"PH{j}", [P, 2, RF]) for j in range(2)]
            KV = [pb(nc, st1, tag + f"KV{j}", [128, 2, 2, A]) for j in range(2)]
            block = st1.enter_context(nc.Block())

            @block.sync
            def _(sp):
                sp.dma_start(rfT[0:MD, :], rfT_dram).then_inc(rf_loaded, 16)
                sp.dma_start(ab[:, 0, :], a_src.rearrange("h c -> (h c)").partition_broadcast(128)
                             ).then_inc(a_loaded, 16)
                sp.dma_start(ab[:, 1, :], a_dst.rearrange("h c -> (h c)").partition_broadcast(128)
                             ).then_inc(a_loaded, 16)
                for k in range(KD // 2):
                    row = (half * (KD // 2) + k) * 128
                    sp.dma_start(ws[k][:], gnn_w1[row:row + 128, :]).then_inc(slice_loaded[k], 16)

            @block.gpsimd
            def _(pool):
                pool.memset(zero[:], 0.0).then_inc(consts, 1)
                pool.memset(vs[:], 1.0).then_inc(consts, 1)
                for b in range(2):
                    pool.tensor_copy(xs[b][:], xnT[:, :, b * P:(b + 1) * P]).then_inc(staged, 1)
                with pool.Fori(1, NT // 2) as i:
                    for b in range(2):
                        pool.wait_ge(v_done, i * 2 + (b - 1))
                        pool.tensor_copy(xs[b][:], xnT[:, :, bass.ds(i * (2 * P) + b * P, P)]).then_inc(staged, 1)

            @block.vector
            def _(dve):
                step = Chain(dve, dve_step)
                dve.sem_inc(q_ready, 1)
                dve.sem_inc(k_ready, 1)
                dve.wait_ge(w_loaded, 16 * 6 * (half + 1))
                dve.wait_ge(rf_loaded, 16)
                step(dve.memset(rfT[MD:A, :], 1.0))
                step(dve.tensor_scalar(brow[:, 0:2, :], brow[:, 0:2, :], SCALE, None, ALU.mult))
                dve.wait_ge(consts, 2)
                with dve.Fori(0, NT) as t:
                    step.start(t, 2)
                    for c, (done, turned, evac, squared, ready) in enumerate(
                            ((q_done, q_turned, q_evac, qsq, q_ready), (k_done, k_turned, k_evac, ksq, k_ready))):
                        dve.wait_ge(done, t + 1)
                        dve.wait_ge(turned, t + 1)
                        dve.scalar_tensor_tensor(qs[:, c, :, 0:MD], G[c][:].rearrange("p (h d) -> p h d", d=MD), SCALE,
                                                 brow[:, c, :].rearrange("p (h d) -> p h d", d=MD),
                                                 ALU.mult, ALU.add).then_inc(evac, 1)
                        dve.wait_ge(squared, t + 1)
                        step(dve.tensor_reduce(nrm[:, c, :], sq[:, c, :, :], AX.X, ALU.add))
                        dve.tensor_scalar(qs[:, c, :, MD:A], nrm[:, c, :].unsqueeze(2), -0.5, None,
                                          ALU.mult).then_inc(ready, 1)
                    dve.wait_ge(v_done, t + 1)
                    dve.wait_ge(kv_step, t + 1)
                    dve.tensor_tensor(vs[:, :, 0:MD], G[2][:].rearrange("p (h d) -> p h d", d=MD),
                                      brow[:, 2, :].rearrange("p (h d) -> p h d", d=MD), ALU.add).then_inc(v_evac, 1)
                step.end(NT)
                dve.wait_ge(kv_step, NT + 1)
                for j in range(2):
                    dve.tensor_copy(kv[:, 2 * j:2 * j + 2, :, :], KV[j][:]).then_inc(kv_copied, 1)

            @block.scalar
            def _(act):
                for freed in (kT_done, exp_a, exp_b):
                    act.sem_inc(freed, 1)
                with act.Fori(0, NT) as t:
                    for c, (evac, squared, ready) in enumerate(((q_evac, qsq, q_ready), (k_evac, ksq, k_ready))):
                        act.wait_ge(evac, t + 1)
                        act.wait_ge(ready, t + 1)
                        act.activation(sq[:, c, :, :], qs[:, c, :, 0:MD], ACT.Square).then_inc(squared, 1)
                        if c == 0:
                            act.wait_ge(q_turned, t + 2)
                            act.activation(qT[:, :, bass.ds(t * P, P)], TQ[:], ACT.Copy).then_inc(qT_done, 1)
                    act.wait_ge(k_turned, t + 2)
                    act.wait_ge(phi_b, t + 1)
                    act.activation(kT[:], TQ[:], ACT.Copy).then_inc(kT_done, 1)
                    act.wait_ge(kv_step, t + 1)
                    act.wait_ge(phi_a, t + 1)
                    act.activation(phik[:, 0:2, :], PH[0][:], ACT.Exp).then_inc(exp_a, 1)
                    act.wait_ge(phi_b, t + 2)
                    act.activation(phik[:, 2:4, :], PH[1][:], ACT.Exp).then_inc(exp_b, 1)

            @block.tensor
            def _(pe):
                pe.sem_inc(q_turned, 1)
                pe.sem_inc(k_turned, 1)
                pe.sem_inc(kv_step, 1)
                pe.sem_inc(phi_b, 1)

                def gemm(c, t, b, done, evac):
                    if c == 0:
                        pe.wait_ge(staged, t + 1)
                    if evac is not None:
                        pe.wait_ge(evac, t)
                    for k in range(KD):
                        last = pe.matmul(G[c][:], xs[b][:, k, :], w[:, k, c, :], start=(k == 0), stop=(k == KD - 1))
                    last.then_inc(done, 1)

                def turn(c, t):
                    pe.wait_ge(k_ready if c else q_ready, t + 2)
                    if c == 0:
                        pe.wait_ge(kT_done, t + 1)
                    else:
                        pe.wait_ge(qT_done, t + 1)
                    for h in range(HH):
                        last = pe.transpose(TQ[:, h, :], qs[:, c, h, :], ident[0:P, 0:P])
                    last.then_inc(k_turned if c else q_turned, 1)

                def features(t):
                    pe.wait_ge(kT_done, t + 2)
                    for j, (done, used) in enumerate(((phi_a, exp_a), (phi_b, exp_b))):
                        pe.wait_ge(used, t + 1)
                        for h in range(2):
                            last = pe.matmul(PH[j][:, h, :], kT[:, 2 * j + h, :], rfT[:], start=True, stop=True,
                                             skip_group_check=True)
                        last.then_inc(done, 1)

                def keys_values(t, stop):
                    pe.wait_ge(exp_b, t + 2)
                    pe.wait_ge(exp_a, t + 2)
                    pe.wait_ge(v_evac, t + 1)
                    for h in range(HH):
                        for m in range(2):
                            last = pe.matmul(KV[h // 2][:, h % 2, m, :], phik[:, h, m * 128:(m + 1) * 128],
                                             vs[:, h, :], start=False, stop=stop, skip_group_check=True)
                    last.then_inc(kv_step, 1)

                pe.wait_ge(consts, 2)
                pe.wait_ge(w_loaded, 16 * 6 * (half + 1))
                pe.wait_ge(rf_loaded, 16)
                for j in range(2):
                    pe.matmul(KV[j][:].rearrange("p h m a -> p (h m a)"), zero[:],
                              vs[:].rearrange("p h a -> p (h a)"), start=True, stop=False, skip_group_check=True)
                gemm(0, 0, 0, q_done, None)
                gemm(1, 0, 0, k_done, None)
                gemm(2, 0, 0, v_done, None)

                def tile(t, b):
                    turn(0, t)
                    gemm(0, t + 1, b, q_done, q_evac)
                    turn(1, t)
                    gemm(1, t + 1, b, k_done, k_evac)
                    features(t)
                    gemm(2, t + 1, b, v_done, v_evac)
                    keys_values(t, False)

                with pe.Fori(0, NT // 2 - 1) as i:
                    for b in range(2):
                        tile(i * 2 + b, 1 - b)
                tile(NT - 2, 1)
                turn(0, NT - 1)
                turn(1, NT - 1)
                features(NT - 1)
                keys_values(NT - 1, True)
        numerator(nc, cx, tag, half, rfT, qT, kv, attn, a_loaded, slice_loaded, ws, ab, wa, load_next)


def logits(nc, cx, st, block, W1, xnT, ident, wa, w, al, alT_dram, w_loaded):
    rows_done, rows_copied, turned, stored = (
        cx.sem("logit_" + s) for s in ("rows_done", "rows_copied", "turned", "stored"))
    J = 2 * H1
    alT = sb(nc, st, "logit_alT", [J, N])
    R = [pb(nc, st, f"logit_R{c}", [J, 512]) for c in range(CH)]
    T = pb(nc, st, "logit_T", [P, NT, J])

    @block.scalar
    def _(act):
        act.dma_start(w[:, :, 0:C1], W1.rearrange("(k p) n -> p k n", p=128)[:, :, 0:C1]).then_inc(w_loaded[0], 16)
        for c in range(CH):
            act.wait_ge(rows_done, c + 1)
            act.activation(alT[:, CHO[c]:CHO[c] + CHW[c]], R[c][:, 0:CHW[c]], ACT.Copy).then_inc(rows_copied, 1)
        act.wait_ge(rows_copied, CH)
        act.dma_start(alT_dram, alT[:]).then_inc(stored, 16)
        act.wait_ge(turned, 1)
        act.activation(al[:], T[:], ACT.Copy)
        act.wait_ge(stored, 16)

    @block.tensor
    def _(pe):
        for c in range(CH):
            for k in range(KD):
                last = pe.matmul(R[c][:, 0:CHW[c]], wa[:, k, :], xnT[:, k, CHO[c]:CHO[c] + CHW[c]],
                                 start=(k == 0), stop=(k == KD - 1))
            last.then_inc(rows_done, 1)
        pe.wait_ge(rows_copied, CH)
        for t in range(NT):
            last = pe.transpose(T[:, t, :], alT[:, t * P:(t + 1) * P], ident[0:J, 0:J])
        last.then_inc(turned, 1)


def edge_table(nc, cx, st, block, src, dst, ident, keyT, sloT, spans):
    blank, loaded, iotas, key_ready, turned, span_ready, span_max, copied = (
        cx.sem("edge_" + s) for s in
        ("blank", "loaded", "iotas", "key_ready", "turned", "span_ready", "span_max", "copied"))
    dve_step = cx.sem("edge_step")
    FULL = EDGES // ER
    REST = EDGES - FULL * ER
    LAST = FULL - 2 * EGP
    di = sb(nc, st, "edge_di", [EGP, EG, ER], I32)
    si = sb(nc, st, "edge_si", [EGP, EG, ER], I32)
    df = sb(nc, st, "edge_df", [EGP, EG, ER])
    sf = sb(nc, st, "edge_sf", [EGP, EG, ER])
    hi = sb(nc, st, "edge_hi", [EGP, EG, ER])
    key = sb(nc, st, "edge_key", [EGP, EG, ER])
    slo = sb(nc, st, "edge_slo", [EGP, EG, ER])
    rng = sb(nc, st, "edge_rng", [EGP, 2, EG])
    row = sb(nc, st, "edge_row", [EGP, EG])
    row1 = sb(nc, st, "edge_row1", [EGP, 2, EG])
    win = sb(nc, st, "edge_win", [EGP, NW])
    c1 = sb(nc, st, "edge_c1", [EGP, NW])
    best = sb(nc, st, "edge_best", [EGP, 2, NW])
    allb = sb(nc, st, "edge_allb", [EGP, 2, NW])
    spi = sb(nc, st, "edge_spi", [EGP, 2, NW], I32)
    T = [pb(nc, st, f"edge_T{j}", [128, EROWS]) for j in range(2)]

    @block.sync
    def _(sp):
        sp.wait_ge(blank, 2)
        for v, t in ((dst, di), (src, si)):
            for g in range(2):
                sp.dma_start(t[:, g, :], v[g * EGP * ER:(g + 1) * EGP * ER].rearrange("(p e) -> p e", e=ER)
                             ).then_inc(loaded, 16)
            sp.dma_start(t[0:LAST, 2, :], v[2 * EGP * ER:FULL * ER].rearrange("(p e) -> p e", e=ER)
                         ).then_inc(loaded, 16)
            sp.dma_start(t[LAST:LAST + 1, 2, 0:REST], v[FULL * ER:EDGES].unsqueeze(0)).then_inc(loaded, 16)

    @block.gpsimd
    def _(pool):
        pool.memset(di[:], PADNODE).then_inc(blank, 1)
        pool.memset(si[:], 0).then_inc(blank, 1)
        pool.iota(row[:], [[EGP, EG]], base=0, channel_multiplier=1,
                  allow_small_or_imprecise_dtypes=True).then_inc(iotas, 1)
        pool.iota(win[:], [[WIN, NW]], base=0, channel_multiplier=0,
                  allow_small_or_imprecise_dtypes=True).then_inc(iotas, 1)
        pool.wait_ge(span_ready, 1)
        pool.partition_all_reduce(allb[:], best[:], EGP, bass.bass_isa.ReduceOp.max).then_inc(span_max, 1)

    @block.vector
    def _(dve):
        step = Chain(dve, dve_step)
        dve.wait_ge(loaded, 8 * 16)
        step(dve.tensor_copy(df[:], di[:]))
        step(dve.tensor_copy(sf[:], si[:]))
        step(dve.tensor_scalar(hi[:], sf[:], float(SLO), None, ALU.is_ge))
        for part in range(2, SPLIT):
            step(dve.scalar_tensor_tensor(hi[:], sf[:], float(part * SLO), hi[:], ALU.is_ge, ALU.add))
        step(dve.scalar_tensor_tensor(slo[:], hi[:], -float(SLO), sf[:], ALU.mult, ALU.add))
        dve.scalar_tensor_tensor(key[:], df[:], float(SPLIT), hi[:], ALU.mult, ALU.add).then_inc(key_ready, 1)
        step(dve.tensor_reduce(rng[:, 0, :], df[:], AX.X, ALU.min))
        step(dve.tensor_reduce(rng[:, 1, :], df[:], AX.X, ALU.max))
        dve.wait_ge(iotas, 2)
        step(dve.tensor_scalar(row1[:, 0, :], row[:], -1.0, 1000.0, ALU.mult, ALU.add))
        step(dve.tensor_scalar(row1[:, 1, :], row[:], 1.0, None, ALU.add))
        step(dve.memset(best[:], 0.0))
        for g in range(EG):
            step(dve.tensor_scalar(c1[:], win[:], float(WIN - 1), rng[:, 0, g:g + 1], ALU.add, ALU.is_ge))
            step(dve.scalar_tensor_tensor(c1[:], win[:], rng[:, 1, g:g + 1], c1[:], ALU.is_le, ALU.mult))
            for e in range(2):
                ins = dve.scalar_tensor_tensor(best[:, e, :], c1[:], row1[:, e, g:g + 1], best[:, e, :],
                                               ALU.mult, ALU.max)
                if (g, e) == (EG - 1, 1):
                    ins.then_inc(span_ready, 1)
                else:
                    step(ins)
        dve.wait_ge(span_max, 1)
        step(dve.tensor_scalar(allb[:, 0, :], allb[:, 0, :], -1.0, 1000.0, ALU.mult, ALU.add))
        step(dve.tensor_scalar(allb[:, 0, :], allb[:, 0, :], float(EROWS - RB), None, ALU.min))
        step(dve.tensor_scalar(allb[:, 1, :], allb[:, 1, :], float(RB - 1), None, ALU.add))
        step(dve.scalar_tensor_tensor(allb[:, 1, :], allb[:, 0, :], float(RB), allb[:, 1, :], ALU.add, ALU.max))
        step(dve.tensor_copy(spi[:], allb[:]))
        step(dve.tensor_scalar(spans[:], spi[0:1, :, :].rearrange("p e w -> p (e w)"), RB.bit_length() - 1, None,
                               ALU.logical_shift_right))
        for j, dest in enumerate((keyT, sloT)):
            dve.wait_ge(turned, j + 1)
            dve.tensor_copy(dest[:], T[j][:]).then_inc(copied, 1)

    @block.tensor
    def _(pe):
        pe.wait_ge(key_ready, 1)
        for j, s in enumerate((key, slo)):
            for g in range(EG):
                last = pe.transpose(T[j][:, g * EGP:(g + 1) * EGP], s[:, g, :], ident[0:EGP, 0:EGP])
            last.then_inc(turned, 1)


def count_phase(nc, cx, keyT, sloT, spans, ct_dram, xnT, W1, w, w_loaded, h):
    assert NW == H1 * NT
    RING = 4
    consts, hot, used, counted, evac, gemm, h_evac = (
        cx.sem("count_" + s) for s in ("consts", "hot", "used", "counted", "evac", "gemm", "h_evac"))
    stores = [cx.sem(f"count_stored{b}") for b in range(2)]
    with ExitStack() as st:
        ikey = sb(nc, st, "count_ikey", [128, 128])
        islo = sb(nc, st, "count_islo", [128, SLO], F16)
        off = sb(nc, st, "count_off", [128, NW])
        zero = sb(nc, st, "count_zero", [128, 128], BF16)
        A = sb(nc, st, "count_A", [128, RING * RB, 128], BF16)
        B = sb(nc, st, "count_B", [128, RING * RB, SLO], BF16)
        out = [sb(nc, st, f"count_out{b}", [128, SLO]) for b in range(2)]
        S = [pb(nc, st, f"count_S{b}", [128, SLO]) for b in range(2)]
        G = [pb(nc, st, f"count_G{b}", [P, C1]) for b in range(2)]
        block = st.enter_context(nc.Block())

        def windows(eng, name, body, before=None, after=None, between=None):
            with eng.register(name + "_turn") as turn:
                eng.reg_mov(turn, 1)

                def head(hd):
                    for t in range(NT):
                        lo = eng.value_load(spans[0:1, bass.ds(hd * NT + t, 1)], min_val=0, max_val=EROWS // RB - 1)
                        hi = eng.value_load(spans[0:1, bass.ds(hd * NT + (NW + t), 1)], min_val=1,
                                            max_val=EROWS // RB)
                        if before is not None:
                            before(hd, t)
                        with eng.Fori(lo, hi) as r:
                            n = eng.snap(turn)
                            body(r, n, eng.snap(n & (RING - 1), min_val=0, max_val=RING - 1), hd, t)
                            eng.reg_add(turn, turn, 1)
                        if after is not None:
                            after(hd, t)

                head(0)
                if between is not None:
                    between()
                with eng.Fori(1, H1) as hd:
                    head(hd)

        @block.gpsimd
        def _(pool):
            kw = dict(allow_small_or_imprecise_dtypes=True)
            pool.iota(ikey[:], [[1, 128]], base=0, channel_multiplier=0, **kw).then_inc(consts, 1)
            pool.iota(islo[:], [[1, SLO]], base=0, channel_multiplier=0, **kw).then_inc(consts, 1)
            pool.iota(off[:], [[WIN * SPLIT, NW]], base=0, channel_multiplier=0, **kw).then_inc(consts, 1)
            pool.memset(zero[:], 0.0).then_inc(consts, 1)
            pool.memset(h[:, :, :, C1:C1 + 1], 1.0)

        @block.vector
        def _(dve):
            dve.wait_ge(consts, 4)

            def body(r, n, s, hd, t):
                dve.wait_ge(used, n)
                dve.scalar_tensor_tensor(A[:, bass.ds(s * RB, RB), :],
                                         ikey[:].unsqueeze(1).to_broadcast([128, RB, 128]),
                                         off[:, bass.ds(hd * NT + t, 1)],
                                         keyT[:, bass.ds(r * RB, RB)].unsqueeze(2).to_broadcast([128, RB, 128]),
                                         ALU.add, ALU.is_equal)
                for b in range(RB):
                    last = dve.tensor_scalar(B[:, bass.ds(s * RB + b, 1), :], islo[:].unsqueeze(1),
                                             sloT[:, bass.ds(r * RB + b, 1)], None, ALU.is_equal)
                last.then_inc(hot, 1)

            windows(dve, "count_dve", body)

        @block.tensor
        def _(pe):
            pe.wait_ge(consts, 4)
            pe.wait_ge(w_loaded[0], 16)
            pe.sem_inc(used, RING)

            def before(hd, t):
                pe.wait_ge(h_evac, hd * NT + (t + 1))
                for k in range(KD):
                    last = pe.matmul(G[t % 2][:], xnT[:, k, t * P:(t + 1) * P], w[:, k, bass.ds(hd * C1, C1)],
                                     start=(k == 0), stop=(k == KD - 1))
                last.then_inc(gemm, 1)
                pe.wait_ge(evac, hd * NT + (t + 1))
                pe.matmul(S[t % 2][:], zero[:], islo[:], start=True, stop=False, skip_group_check=True)

            def body(r, n, s, hd, t):
                pe.wait_ge(hot, n)
                for b in range(RB):
                    last = pe.matmul(S[t % 2][:], A[:, bass.ds(s * RB + b, 1), :].rearrange("p o k -> p (o k)"),
                                     B[:, bass.ds(s * RB + b, 1), :].rearrange("p o k -> p (o k)"),
                                     start=False, stop=False, skip_group_check=True)
                last.then_inc(used, 1)

            def after(hd, t):
                pe.matmul(S[t % 2][:], zero[:], islo[:], start=False, stop=True, skip_group_check=True
                          ).then_inc(counted, 1)

            windows(pe, "count_pe", body, before, after, lambda: pe.wait_ge(w_loaded[1], 16))

        @block.scalar
        def _(act):
            act.sem_inc(evac, 2)
            act.sem_inc(h_evac, 2)

            def head(hd, first):
                for t in range(NT):
                    act.wait_ge(gemm, hd * NT + (t + 1))
                    act.activation(h[:, t, bass.ds(hd, 1), 0:C1], G[t % 2][:].unsqueeze(1), ACT.Copy
                                   ).then_inc(h_evac, 1)
                    act.wait_ge(counted, hd * NT + (t + 1))
                    if not (first and t < 2):
                        act.wait_ge(stores[t % 2], hd * (16 * NT // 2) + 16 * (t // 2))
                    act.activation(out[t % 2][:], S[t % 2][:], ACT.Copy).then_inc(evac, 1)

            head(0, True)
            with act.Fori(1, H1) as hd:
                head(hd, False)

        @block.sync
        def _(sp):
            sp.dma_start(w[:, :, C1:F1], W1.rearrange("(k p) n -> p k n", p=128)[:, :, C1:F1]
                         ).then_inc(w_loaded[1], 16)
            with sp.Fori(0, NW // 2) as w2:
                for q in range(2):
                    sp.wait_ge(evac, w2 * 2 + (q + 3))
                    sp.dma_start(ct_dram[bass.ds(w2 * 256 + q * 128, 128), :], out[q][:]).then_inc(stores[q], 16)
            for q in range(2):
                sp.wait_ge(stores[q], 16 * (NW // 2))


def mask_phase(nc, cx, ct_dram, c_dram, mask_dram, alT_dram, ident, al, mT_dram):
    rows_loaded, looped, masked, maxed, turned, copied, m_ready, m_turned, m_copied, m_stored, consts = (
        cx.sem("mask_" + s) for s in ("rows_loaded", "looped", "masked", "maxed", "turned", "copied", "m_ready",
                                      "m_turned", "m_copied", "m_stored", "consts"))
    loads = [cx.sem(f"mask_loaded{b}") for b in range(2)]
    mask_stores = [cx.sem(f"mask_mstored{b}") for b in range(2)]
    c_stores = [cx.sem(f"mask_cstored{b}") for b in range(2)]
    dve_step = cx.sem("mask_step")
    with ExitStack() as st:
        ct = [sb(nc, st, f"mask_ct{b}", [P, N]) for b in range(2)]
        mk = [sb(nc, st, f"mask_mk{b}", [P, N]) for b in range(2)]
        co = [sb(nc, st, f"mask_co{b}", [P, NT, P]) for b in range(2)]
        rows = sb(nc, st, "mask_rows", [P, H1, N])
        junk = sb(nc, st, "mask_junk", [P, N])
        large = sb(nc, st, "mask_large", [P, 1])
        big = sb(nc, st, "mask_big", [P, NT, H1])
        m = sb(nc, st, "mask_m", [P, NT, H1])
        mT = sb(nc, st, "mask_mT", [H1, N])
        T = [[pb(nc, st, f"mask_T{b}{j}", [P, 4, P]) for j in range(3)] for b in range(2)]
        width = [4, 4, 2]
        block = st.enter_context(nc.Block())

        @block.sync
        def _(sp):
            for t in range(NT):
                b = t % 2
                if t >= 2:
                    sp.wait_ge(turned, t - 1)
                    sp.wait_ge(masked, t - 1)
                sp.dma_start(ct[b][:], ct_dram.rearrange("(d a) s -> d (a s)", a=SPLIT)[t * P:(t + 1) * P, 0:N]
                             ).then_inc(loads[b], 16)
                if t == 0:
                    for h in range(H1):
                        sp.dma_start(rows[:, h, :], alT_dram[h, :].partition_broadcast(P)).then_inc(rows_loaded, 16)
            sp.wait_ge(m_copied, 3)
            sp.dma_start(mT_dram, mT[:]).then_inc(m_stored, 16)
            sp.wait_ge(m_stored, 16)

        @block.gpsimd
        def _(pool):
            pool.memset(large[:], BIG).then_inc(consts, 1)
            for t in range(NT):
                b = t % 2
                pool.wait_ge(masked, t + 1)
                pool.dma_start(mask_dram[t, :, :], mk[b][:]).then_inc(mask_stores[b], 16)
                pool.wait_ge(copied, t + 1)
                pool.dma_start(c_dram[t, :, :], co[b][:].rearrange("p t d -> p (t d)")).then_inc(c_stores[b], 16)
            for b in range(2):
                pool.wait_ge(mask_stores[b], 16 * (NT // 2))
                pool.wait_ge(c_stores[b], 16 * (NT // 2))

        @block.vector
        def _(dve):
            step = Chain(dve, dve_step)

            def loop(t):
                b = t % 2
                dve.wait_ge(loads[b], 16 * (t // 2 + 1))
                diag = ct[b][:, t * P:(t + 1) * P]
                dve.tensor_tensor(diag, diag, ident[0:P, 0:P], ALU.add).then_inc(looped, 1)

            loop(0)
            dve.wait_ge(rows_loaded, 64)
            for t in range(NT):
                b = t % 2
                if t + 1 < NT:
                    loop(t + 1)
                dve.wait_ge(masked, t + 1)
                for h in range(H1):
                    n = H1 * t + h
                    if n >= 1:
                        dve.wait_ge(maxed, n)
                    dve.tensor_tensor_reduce(out=junk[:], in0=rows[:, h, :], in1=mk[b][:], scale=1.0,
                                             scalar=-3.0e38, op0=ALU.subtract, op1=ALU.max,
                                             accum_out=big[:, t, h:h + 1]).then_inc(maxed, 1)
            dve.wait_ge(maxed, H1 * NT)
            step(dve.tensor_tensor(big[:], big[:], al[:, :, H1:2 * H1], ALU.add))
            dve.scalar_tensor_tensor(m[:], big[:], SLOPE, big[:], ALU.mult, ALU.max).then_inc(m_ready, 1)
            for j in range(3):
                dve.wait_ge(m_turned, j + 1)
                dve.tensor_copy(mT[:, 4 * j * P:(4 * j + width[j]) * P],
                                T[0][j][0:H1, 0:width[j], :].rearrange("p t d -> p (t d)")).then_inc(m_copied, 1)

        @block.scalar
        def _(act):
            act.wait_ge(consts, 1)
            for t in range(NT):
                b = t % 2
                act.wait_ge(looped, t + 1)
                if t >= 2:
                    act.wait_ge(maxed, H1 * (t - 1))
                    act.wait_ge(mask_stores[b], 16 * (t // 2))
                act.activation(mk[b][:], ct[b][:], ACT.Relu, scale=-BIG, bias=large[:]).then_inc(masked, 1)
                act.wait_ge(turned, t + 1)
                if t >= 2:
                    act.wait_ge(c_stores[b], 16 * (t // 2))
                for j in range(3):
                    last = act.activation(co[b][:, 4 * j:4 * j + width[j], :], T[b][j][:, 0:width[j], :], ACT.Copy)
                last.then_inc(copied, 1)

        @block.tensor
        def _(pe):
            for t in range(NT):
                b = t % 2
                pe.wait_ge(looped, t + 1)
                if t >= 2:
                    pe.wait_ge(copied, t - 1)
                for s in range(NT):
                    last = pe.transpose(T[b][s // 4][:, s % 4, :], ct[b][:, s * P:(s + 1) * P], ident[0:P, 0:P])
                last.then_inc(turned, 1)
            pe.wait_ge(copied, NT)
            pe.wait_ge(m_ready, 1)
            for j in range(3):
                for t in range(width[j]):
                    last = pe.transpose(T[0][j][0:H1, t, :], m[:, 4 * j + t, :], ident[0:P, 0:P])
                last.then_inc(m_turned, 1)


def gat1_phase(nc, cx, b1, h, al, alT_dram, mT_dram, c_dram, h1T_dram, ident):
    (e_ready, exp_done, w_ready, agg, mn_ready, exp_mn, elu_ready, turned, t_evac, dve_step, b_loaded) = (
        cx.sem("gat1_" + s) for s in
        ("e_ready", "exp_done", "w_ready", "agg", "mn_ready", "exp_mn", "elu_ready", "turned", "t_evac", "dve_step",
         "b_loaded"))
    rows_loaded = [cx.sem(f"gat1_rows_loaded{b}") for b in range(2)]
    c_loaded = [cx.sem(f"gat1_c_loaded{b}") for b in range(2)]
    stored = [cx.sem(f"gat1_stored{b}") for b in range(2)]
    HC = C1 // 2
    HT16 = 16 * NT // 2
    with ExitStack() as st:
        brow = sb(nc, st, "gat1_brow", [P, F1])
        rows = [sb(nc, st, f"gat1_rows{b}", [P, 2, N]) for b in range(2)]
        u = sb(nc, st, "gat1_u", [P, NT, P])
        e = [sb(nc, st, f"gat1_e{b}", [P, NT, P]) for b in range(2)]
        wt = [sb(nc, st, f"gat1_wt{b}", [P, NT, P]) for b in range(2)]
        cnt = [sb(nc, st, f"gat1_cnt{b}", [P, NT, P]) for b in range(2)]
        rden = [sb(nc, st, f"gat1_rden{b}", [P, 1]) for b in range(2)]
        o = [sb(nc, st, f"gat1_o{b}", [P, C1]) for b in range(2)]
        mn = [sb(nc, st, f"gat1_mn{b}", [P, C1]) for b in range(2)]
        oT = [sb(nc, st, f"gat1_oT{b}", [128, 4, P]) for b in range(2)]
        Z = [[pb(nc, st, f"gat1_Z{b}{j}", [P, HC + j]) for j in range(2)] for b in range(2)]
        T = [pb(nc, st, f"gat1_T{b}", [128, 4, P]) for b in range(2)]
        block = st.enter_context(nc.Block())

        def heads(eng, body):
            body(0, 0, True, False)
            with eng.Fori(0, H1 // 2 - 1) as i:
                body(i * 2 + 1, 1, False, False)
                body(i * 2 + 2, 0, False, False)
            body(H1 - 1, 1, False, True)

        @block.sync
        def _(sp):
            sp.dma_start(brow[:], b1.partition_broadcast(P)).then_inc(b_loaded, 16)

            def load_rows(hd, b):
                sp.dma_start(rows[b][:, 0, :], alT_dram[bass.ds(hd + H1, 1), :].partition_broadcast(P)
                             ).then_inc(rows_loaded[b], 16)
                sp.dma_start(rows[b][:, 1, :], mT_dram[bass.ds(hd, 1), :].partition_broadcast(P)
                             ).then_inc(rows_loaded[b], 16)

            load_rows(0, 0)

            def body(hd, b, first, last):
                if not last:
                    if not first:
                        sp.wait_ge(e_ready, hd * NT)
                    load_rows(hd + 1, 1 - b)
                for t in range(NT):
                    sp.wait_ge(w_ready, hd * NT + (t + 1))
                    sp.dma_start(cnt[t % 2][:], c_dram[t, :, :].rearrange("p (t d) -> p t d", d=P)
                                 ).then_inc(c_loaded[t % 2], 16)

            heads(sp, body)

        @block.vector
        def _(dve):
            def steps(before):
                made = [0]

                def step(ins):
                    made[0] += 1
                    ins.then_inc(dve_step, 1)
                    dve.wait_ge(dve_step, before + made[0])
                return step

            STEPS = 5

            for freed in (w_ready, mn_ready):
                dve.sem_inc(freed, 2)
            dve.wait_ge(b_loaded, 16)

            def scores(hd, t, hb):
                b, g = t % 2, hd * NT + t
                step = steps(2 * g if isinstance(g, int) and g < 2 else g * STEPS - 6)
                if t == 0:
                    dve.wait_ge(rows_loaded[hb], (hd - hb) * 16 + 32)
                if not (isinstance(g, int) and g == 0):
                    dve.wait_ge(e_ready, g)
                step(dve.tensor_tensor(u[:], al[:, :, bass.ds(hd, 1)].to_broadcast([P, NT, P]),
                                       rows[hb][:, 0:1, t * P:(t + 1) * P].to_broadcast([P, NT, P]), ALU.add))
                step(dve.scalar_tensor_tensor(u[:], u[:], SLOPE, u[:], ALU.mult, ALU.max))
                dve.wait_ge(w_ready, g + 1)
                dve.tensor_tensor(e[b][:], u[:], rows[hb][:, 1:2, t * P:(t + 1) * P].to_broadcast([P, NT, P]),
                                  ALU.subtract).then_inc(e_ready, 1)

            def weights(hd, t):
                b, g = t % 2, hd * NT + t
                dve.wait_ge(exp_done, g + 1)
                dve.wait_ge(c_loaded[b], hd * HT16 + 16 * (t // 2 + 1))
                dve.wait_ge(agg, g + 1)
                dve.tensor_tensor(wt[b][:], e[b][:], cnt[b][:], ALU.mult).then_inc(w_ready, 1)

            def normalise(hd, t, left):
                b, g = t % 2, hd * NT + t
                step = steps(g * STEPS + (6, 4, 2)[left])
                dve.wait_ge(agg, g + 3)
                dve.wait_ge(turned, g + 1)
                step(dve.tensor_scalar(rden[b][:], Z[b][1][:, HC:HC + 1], 1e-16, None, ALU.add))
                step(dve.reciprocal(rden[b][:], rden[b][:]))
                dve.scalar_tensor_tensor(o[b][:, 0:HC], Z[b][0][:], rden[b][:],
                                         brow[:, bass.ds(hd * C1, HC)], ALU.mult, ALU.add)
                step(dve.scalar_tensor_tensor(o[b][:, HC:C1], Z[b][1][:, 0:HC], rden[b][:],
                                              brow[:, bass.ds(hd * C1 + HC, HC)], ALU.mult, ALU.add))
                if not (isinstance(g, int) and g == 0):
                    dve.wait_ge(elu_ready, g)
                dve.tensor_scalar(mn[b][:], o[b][:], 0.0, None, ALU.min).then_inc(mn_ready, 1)

            def elu(hd, t):
                b, g = t % 2, hd * NT + t
                dve.wait_ge(exp_mn, g + 1)
                dve.scalar_tensor_tensor(o[b][:], mn[b][:], -1.0, o[b][:], ALU.add, ALU.max).then_inc(elu_ready, 1)

            for t in range(2):
                scores(0, t, 0)
                weights(0, t)

            def body(hd, hb, first, last):
                for t in range(NT):
                    if t + 2 < NT:
                        scores(hd, t + 2, hb)
                    elif not last:
                        scores(hd + 1, t + 2 - NT, 1 - hb)
                    normalise(hd, t, max(0, t + 3 - NT) if last else 0)
                    if t + 2 < NT:
                        weights(hd, t + 2)
                    elif not last:
                        weights(hd + 1, t + 2 - NT)
                    elu(hd, t)

            heads(dve, body)

        @block.scalar
        def _(act):
            act.sem_inc(t_evac, 2)

            def exp_scores(hd, t):
                act.wait_ge(e_ready, hd * NT + (t + 1))
                act.activation(e[t % 2][:], e[t % 2][:], ACT.Exp).then_inc(exp_done, 1)

            exp_scores(0, 0)
            exp_scores(0, 1)

            def body(hd, hb, first, last):
                for t in range(NT):
                    if t + 2 < NT:
                        exp_scores(hd, t + 2)
                    elif not last:
                        exp_scores(hd + 1, t + 2 - NT)
                    b = t % 2
                    act.wait_ge(mn_ready, hd * NT + (t + 3))
                    act.activation(mn[b][:], mn[b][:], ACT.Exp).then_inc(exp_mn, 1)
                    act.wait_ge(turned, hd * NT + (t + 3))
                    if not (first and t < 2):
                        act.wait_ge(stored[b], hd * HT16 + 16 * (t // 2))
                    act.activation(oT[b][:], T[b][:], ACT.Copy).then_inc(t_evac, 1)
                    act.wait_ge(t_evac, hd * NT + (t + 3))
                    act.dma_start(h1T_dram[t, :, :].rearrange("p (f d) -> p f d", d=P)[:, bass.ds(hd * 4, 4), :],
                                  oT[b][:]).then_inc(stored[b], 16)

            heads(act, body)
            for b in range(2):
                act.wait_ge(stored[b], H1 * HT16)

        @block.tensor
        def _(pe):
            pe.sem_inc(agg, 2)
            pe.sem_inc(turned, 2)

            def aggregate(hd, t):
                b, g = t % 2, hd * NT + t
                pe.wait_ge(w_ready, g + 3)
                pe.wait_ge(mn_ready, g + 1)
                for j in range(2):
                    for s in range(NT):
                        last = pe.matmul(Z[b][j][:], wt[b][:, s, :],
                                         h[:, s, bass.ds(hd, 1), j * HC:(j + 1) * HC + j],
                                         start=(s == 0), stop=(s == NT - 1))
                last.then_inc(agg, 1)

            def turn(hd, t):
                b, g = t % 2, hd * NT + t
                pe.wait_ge(elu_ready, g + 1)
                pe.wait_ge(t_evac, g + 1)
                for f in range(4):
                    last = pe.transpose(T[b][:, f, :], o[b][:, f * 128:(f + 1) * 128], ident[0:P, 0:P])
                last.then_inc(turned, 1)

            aggregate(0, 0)

            def body(hd, hb, first, last):
                for t in range(NT):
                    if t + 1 < NT:
                        aggregate(hd, t + 1)
                    elif not last:
                        aggregate(hd + 1, 0)
                    turn(hd, t)

            heads(pe, body)


def gat2_project_phase(nc, cx, W2, a_src, a_dst, h1T_dram, mask_dram, ident, h2, al2, al2T_dram, m2T_dram,
                       x1_dram, x1, x_loaded, rows_t, rows_loaded):
    KC = 4
    a_loaded, projected, ev_a, ev_d, al_step, turned, copied, stored = (
        cx.sem("gat2p_" + s) for s in
        ("a_loaded", "projected", "ev_a", "ev_d", "al_step", "turned", "copied", "stored"))
    row_loaded, mask_loaded, maxed, m_ready, m_turned, m_copied, m_stored = (
        cx.sem("gat2m_" + s) for s in
        ("row_loaded", "mask_loaded", "maxed", "m_ready", "m_turned", "m_copied", "m_stored"))
    dve_step = cx.sem("gat2m_step")
    w_loaded = [cx.sem(f"gat2p_w{c}") for c in range(KF // KC)]
    in_loaded = [cx.sem(f"gat2p_in{b}") for b in range(2)]
    HW = D // 2
    with ExitStack() as st:
        w = sb(nc, st, "gat2p_w", [128, KF, D])
        ab = sb(nc, st, "gat2p_a", [P, 2, D])
        junk = sb(nc, st, "gat2p_junk", [P, 2, D])
        hT = [sb(nc, st, f"gat2p_hT{b}", [128, KF, P]) for b in range(2)]
        alT = sb(nc, st, "gat2p_alT", [2, N])
        mask = sb(nc, st, "gat2p_mask", [P, NT, N])
        row = sb(nc, st, "gat2p_row", [P, N])
        big = sb(nc, st, "gat2p_big", [P, NT])
        m = sb(nc, st, "gat2p_m", [P, NT])
        mT = sb(nc, st, "gat2p_mT", [1, N])
        Y = [[pb(nc, st, f"gat2p_Y{b}{j}", [P, HW]) for j in range(2)] for b in range(2)]
        T = [pb(nc, st, f"gat2p_T{j}", [2, 4, P]) for j in range(3)]
        width = [4, 4, 2]
        block = st.enter_context(nc.Block())

        @block.sync
        def _(sp):
            def load_h(i, b):
                sp.dma_start(hT[b][:], h1T_dram[bass.ds(i * 2 + b, 1), :, :]
                             .rearrange("o p (f d) -> p (o f) d", d=P)).then_inc(in_loaded[b], 16)

            load_h(0, 0)
            for c in range(KF // KC):
                sp.dma_start(w[:, c * KC:(c + 1) * KC, :],
                             W2[c * KC * 128:(c + 1) * KC * 128, :].rearrange("(k p) n -> p k n", p=128)
                             ).then_inc(w_loaded[c], 16)
            load_h(0, 1)
            sp.dma_start(ab[:, 0, :], a_src[0, :].partition_broadcast(P)).then_inc(a_loaded, 16)
            sp.dma_start(ab[:, 1, :], a_dst[0, :].partition_broadcast(P)).then_inc(a_loaded, 16)
            with sp.Fori(1, NT // 2) as i:
                for b in range(2):
                    sp.wait_ge(projected, i * 2 + (b + 1))
                    load_h(i, b)
            sp.dma_start(x1[:], x1_dram.rearrange("(t p) d -> p t d", p=P)).then_inc(x_loaded, 16)
            sp.dma_start(mask[:], mask_dram.rearrange("t p n -> p t n")).then_inc(mask_loaded, 16)
            sp.wait_ge(copied, 3)
            sp.dma_start(al2T_dram, alT[:]).then_inc(stored, 16)
            sp.wait_ge(stored, 16)
            sp.dma_start(row[:], al2T_dram[0, :].partition_broadcast(P)).then_inc(row_loaded, 16)
            sp.dma_start(rows_t[:], al2T_dram[1, :].partition_broadcast(P)).then_inc(rows_loaded, 16)
            sp.wait_ge(m_copied, 3)
            sp.dma_start(m2T_dram, mT[:]).then_inc(m_stored, 16)
            sp.wait_ge(m_stored, 16)

        @block.vector
        def _(dve):
            step = Chain(dve, dve_step)
            dve.sem_inc(ev_d, 2)
            dve.memset(h2[:, :, D:D + 1], 1.0)
            dve.wait_ge(a_loaded, 32)
            for t in range(NT):
                b = t % 2
                dve.wait_ge(projected, t + 3)
                dve.tensor_copy(h2[:, t, HW:D], Y[b][1][:]).then_inc(ev_d, 1)
                dve.wait_ge(ev_d, t + 3)
                dve.wait_ge(ev_a, t + 3)
                for s in range(2):
                    n = 2 * t + s
                    if n >= 2:
                        dve.wait_ge(al_step, n - 1)
                    dve.tensor_tensor_reduce(out=junk[:, s, :], in0=h2[:, t, 0:D], in1=ab[0:P, s, :], scale=1.0,
                                             scalar=0.0, op0=ALU.mult, op1=ALU.add,
                                             accum_out=al2[:, t, s:s + 1]).then_inc(al_step, 1)
            for j in range(3):
                dve.wait_ge(turned, j + 1)
                dve.tensor_copy(alT[:, 4 * j * P:(4 * j + width[j]) * P],
                                T[j][:, 0:width[j], :].rearrange("p t d -> p (t d)")).then_inc(copied, 1)
            mjunk = junk[:].rearrange("p s d -> p (s d)")[:, 0:N]
            dve.wait_ge(al_step, 2 * NT)
            dve.wait_ge(row_loaded, 16)
            dve.wait_ge(mask_loaded, 16)
            for t in range(NT):
                if t >= 1:
                    dve.wait_ge(maxed, t)
                dve.tensor_tensor_reduce(out=mjunk, in0=row[:], in1=mask[:, t, :], scale=1.0, scalar=-3.0e38,
                                         op0=ALU.subtract, op1=ALU.max, accum_out=big[:, t:t + 1]).then_inc(maxed, 1)
            dve.wait_ge(maxed, NT)
            step(dve.tensor_tensor(big[:], big[:], al2[:, :, 1], ALU.add))
            dve.scalar_tensor_tensor(m[:], big[:], SLOPE, big[:], ALU.mult, ALU.max).then_inc(m_ready, 1)
            for j in range(3):
                dve.wait_ge(m_turned, j + 1)
                dve.tensor_copy(mT[:, 4 * j * P:(4 * j + width[j]) * P],
                                T[j][0:1, 0:width[j], :].rearrange("p t d -> p (t d)")).then_inc(m_copied, 1)

        @block.scalar
        def _(act):
            act.sem_inc(ev_a, 2)
            with act.Fori(0, NT // 2) as i:
                for b in range(2):
                    act.wait_ge(projected, i * 2 + (b + 3))
                    act.activation(h2[:, bass.ds(i * 2 + b, 1), 0:HW], Y[b][0][:].unsqueeze(1), ACT.Copy
                                   ).then_inc(ev_a, 1)

        @block.tensor
        def _(pe):
            pe.sem_inc(projected, 2)

            def project(i, b, chunks):
                pe.wait_ge(in_loaded[b], i * 16 + 16)
                pe.wait_ge(ev_a, i * 2 + (b + 1))
                pe.wait_ge(ev_d, i * 2 + (b + 1))
                for c in range(KF // KC):
                    if chunks:
                        pe.wait_ge(w_loaded[c], 16)
                    for j in range(2):
                        for k in range(c * KC, (c + 1) * KC):
                            last = pe.matmul(Y[b][j][:], hT[b][:, k, :], w[:, k, j * HW:(j + 1) * HW],
                                             start=(k == 0), stop=(k == KF - 1))
                last.then_inc(projected, 1)

            project(0, 0, True)
            project(0, 1, False)
            with pe.Fori(1, NT // 2) as i:
                for b in range(2):
                    project(i, b, False)
            pe.wait_ge(al_step, 2 * NT)
            for j in range(3):
                for t in range(width[j]):
                    last = pe.transpose(T[j][:, t, :], al2[:, 4 * j + t, :], ident[0:P, 0:P])
                last.then_inc(turned, 1)
            pe.wait_ge(m_ready, 1)
            for j in range(3):
                for t in range(width[j]):
                    last = pe.transpose(T[j][0:1, t, :], m[:, 4 * j + t:4 * j + t + 1], ident[0:P, 0:P])
                last.then_inc(m_turned, 1)


def gat2_phase(nc, cx, al2, m2T_dram, c_dram, h2, x1, x_loaded, rows_t, rows_loaded, stats):
    (m_loaded, e_ready, exp_done, w_ready, agg, summed, dve_step) = (
        cx.sem("gat2_" + s) for s in
        ("m_loaded", "e_ready", "exp_done", "w_ready", "agg", "summed", "dve_step"))
    c_loaded = [cx.sem(f"gat2_c_loaded{b}") for b in range(2)]
    CW = [385, 384]
    with ExitStack() as st:
        rows_m = sb(nc, st, "gat2_rows_m", [P, N])
        u = sb(nc, st, "gat2_u", [P, NT, P])
        e = [sb(nc, st, f"gat2_e{b}", [P, NT, P]) for b in range(2)]
        wt = [sb(nc, st, f"gat2_wt{b}", [P, NT, P]) for b in range(2)]
        cnt = [sb(nc, st, f"gat2_cnt{b}", [P, NT, P]) for b in range(2)]
        rden = [sb(nc, st, f"gat2_rden{b}", [P, 1]) for b in range(2)]
        Z = [[pb(nc, st, f"gat2_Z{b}{j}", [P, CW[j]]) for j in range(2)] for b in range(2)]
        block = st.enter_context(nc.Block())

        @block.sync
        def _(sp):
            sp.dma_start(rows_m[:], m2T_dram[0, :].partition_broadcast(P)).then_inc(m_loaded, 16)
            for t in range(NT):
                sp.wait_ge(w_ready, t + 1)
                sp.dma_start(cnt[t % 2][:], c_dram[t, :, :].rearrange("p (t d) -> p t d", d=P)
                             ).then_inc(c_loaded[t % 2], 16)

        @block.vector
        def _(dve):
            step = Chain(dve, dve_step)
            dve.sem_inc(w_ready, 2)
            dve.sem_inc(summed, 2)

            def scores(t):
                b = t % 2
                if t >= 1:
                    dve.wait_ge(e_ready, t)
                step(dve.tensor_tensor(u[:], al2[:, :, 0:1].to_broadcast([P, NT, P]),
                                       rows_t[:, t * P:(t + 1) * P].unsqueeze(1).to_broadcast([P, NT, P]), ALU.add))
                step(dve.scalar_tensor_tensor(u[:], u[:], SLOPE, u[:], ALU.mult, ALU.max))
                if t == 0:
                    dve.wait_ge(m_loaded, 16)
                dve.wait_ge(w_ready, t + 1)
                dve.tensor_tensor(e[b][:], u[:], rows_m[:, t * P:(t + 1) * P].unsqueeze(1).to_broadcast([P, NT, P]),
                                  ALU.subtract).then_inc(e_ready, 1)

            def weights(t):
                b = t % 2
                dve.wait_ge(exp_done, t + 1)
                dve.wait_ge(c_loaded[b], 16 * (t // 2 + 1))
                dve.wait_ge(agg, t + 1)
                dve.tensor_tensor(wt[b][:], e[b][:], cnt[b][:], ALU.mult).then_inc(w_ready, 1)

            def add(t):
                b = t % 2
                dve.wait_ge(agg, t + 3)
                dve.wait_ge(summed, t + 1)
                step(dve.tensor_scalar(rden[b][:], Z[b][1][:, 383:384], 1e-16, None, ALU.add))
                step(dve.reciprocal(rden[b][:], rden[b][:]))
                dve.scalar_tensor_tensor(x1[:, t, 0:385], Z[b][0][:], rden[b][:], x1[:, t, 0:385], ALU.mult, ALU.add)
                dve.scalar_tensor_tensor(x1[:, t, 385:D], Z[b][1][:, 0:383], rden[b][:], x1[:, t, 385:D],
                                         ALU.mult, ALU.add).then_inc(summed, 1)
                dve.wait_ge(summed, t + 3)
                for g in range(2):
                    dve.bn_stats(stats[:, t, g, :], x1[:, t, g * 384:(g + 1) * 384])

            dve.wait_ge(rows_loaded, 16)
            scores(0)
            weights(0)
            dve.wait_ge(x_loaded, 16)
            for t in range(NT + 1):
                if t + 1 < NT:
                    scores(t + 1)
                if t >= 1:
                    add(t - 1)
                if t + 1 < NT:
                    weights(t + 1)

        @block.scalar
        def _(act):
            for t in range(NT):
                act.wait_ge(e_ready, t + 1)
                act.activation(e[t % 2][:], e[t % 2][:], ACT.Exp).then_inc(exp_done, 1)

        @block.tensor
        def _(pe):
            pe.sem_inc(agg, 2)
            for t in range(NT):
                b = t % 2
                pe.wait_ge(w_ready, t + 3)
                pe.wait_ge(summed, t + 1)
                for j in range(2):
                    for s in range(NT):
                        last = pe.matmul(Z[b][j][:], wt[b][:, s, :], h2[:, s, 385 * j:385 * j + CW[j]],
                                         start=(s == 0), stop=(s == NT - 1))
                last.then_inc(agg, 1)


def route_norm_phase(nc, cx, load_next, x1, stats, wg, wge, bg, bge, xn2_dram, ident, lg):
    (stats_done, sqrt_done, xn_ready, turned, ev_d, ev_a, w_loaded, mm, lg_done, zeroed) = (
        cx.sem("rn_" + s) for s in
        ("stats_done", "sqrt_done", "xn_ready", "turned", "ev_d", "ev_a", "w_loaded", "mm", "lg_done", "zeroed"))
    stored = [cx.sem(f"rn_stored{b}") for b in range(2)]
    zstored = cx.sem("rn_zstored")
    dve_step = cx.sem("rn_step")
    L = NG + NE
    with ExitStack() as st:
        mv = sb(nc, st, "rn_mv", [P, NT, 2])
        std = sb(nc, st, "rn_std", [P, NT])
        veps = sb(nc, st, "rn_veps", [P, NT])
        tmp = sb(nc, st, "rn_tmp", [P, NT])
        rstd = sb(nc, st, "rn_rstd", [P, NT])
        w = sb(nc, st, "rn_w", [128, KD, L])
        brow = sb(nc, st, "rn_brow", [P, L])
        zero = sb(nc, st, "rn_zero", [SLOT, D])
        xn = [sb(nc, st, f"rn_xn{b}", [P, D]) for b in range(2)]
        xT = [sb(nc, st, f"rn_xT{b}", [128, KD, P]) for b in range(2)]
        T = [[pb(nc, st, f"rn_T{b}{j}", [128, 3, P]) for j in range(2)] for b in range(2)]
        Y = [pb(nc, st, f"rn_Y{b}", [P, L]) for b in range(2)]
        block = st.enter_context(nc.Block())

        @block.sync
        def _(sp):
            sp.dma_start(w[:, :, 0:NG], wg.rearrange("(k p) n -> p k n", p=128)).then_inc(w_loaded, 16)
            sp.dma_start(w[:, :, NG:L], wge.rearrange("(k p) n -> p k n", p=128)).then_inc(w_loaded, 16)
            sp.dma_start(brow[:, 0:NG], bg.partition_broadcast(P)).then_inc(w_loaded, 16)
            sp.dma_start(brow[:, NG:L], bge.rearrange("g e -> (g e)").partition_broadcast(P)).then_inc(w_loaded, 16)
            sp.wait_ge(zeroed, 1)
            sp.dma_start(xn2_dram[N:N + SLOT, :], zero[:]).then_inc(zstored, 16)
            with sp.Fori(0, NT // 2) as i:
                for b in range(2):
                    sp.wait_ge(xn_ready, i * 2 + (b + 1))
                    sp.dma_start(xn2_dram[bass.ds(i * (2 * P) + b * P, P), :], xn[b][:]).then_inc(stored[b], 16)
            sp.wait_ge(zstored, 16)
            load_next(sp)
            for b in range(2):
                sp.wait_ge(stored[b], 16 * (NT // 2))

        @block.gpsimd
        def _(pool):
            pool.memset(zero[:], 0.0).then_inc(zeroed, 1)

        @block.vector
        def _(dve):
            step = Chain(dve, dve_step)
            for t in range(NT):
                last = dve.bn_aggr(mv[:, t, :], stats[:, t, :, :])
            step(last)
            dve.tensor_scalar(veps[:], mv[:, :, 1], EPS, None, ALU.add).then_inc(stats_done, 1)
            dve.wait_ge(sqrt_done, 1)
            refine_rstd(step, dve, rstd[:], std[:], veps[:], tmp[:])
            dve.wait_ge(w_loaded, 64)
            dve.sem_inc(ev_d, 2)
            dve.sem_inc(lg_done, 2)

            def scaled(t, b, before):
                dve.wait_ge(turned, t + 1)
                dve.wait_ge(stored[b], before * 16)
                dve.tensor_scalar(xn[b][:], x1[:, bass.ds(t, 1), :], mv[:, bass.ds(t, 1), 0],
                                  rstd[:, bass.ds(t, 1)], ALU.subtract, ALU.mult).then_inc(xn_ready, 1)

            def copy(t, b):
                dve.wait_ge(turned, t + 3)
                dve.wait_ge(mm, t + 1)
                dve.tensor_copy(xT[b][:, 0:3, :], T[b][0][:]).then_inc(ev_d, 1)

            def logits(t, b):
                dve.wait_ge(mm, t + 3)
                dve.tensor_tensor(lg[:, bass.ds(t, 1), :], Y[b][:].unsqueeze(1), brow[:].unsqueeze(1),
                                  ALU.add).then_inc(lg_done, 1)

            scaled(0, 0, 0)
            scaled(1, 1, 0)
            copy(0, 0)
            with dve.Fori(0, NT // 2 - 1) as i:
                for b in range(2):
                    scaled(i * 2 + (b + 2), b, i + 1)
                    copy(i * 2 + (b + 1), 1 - b)
                    logits(i * 2 + b, b)
            copy(NT - 1, 1)
            logits(NT - 2, 0)
            logits(NT - 1, 1)

        @block.scalar
        def _(act):
            act.sem_inc(ev_a, 2)
            act.wait_ge(stats_done, 1)
            act.activation(std[:], veps[:], ACT.Sqrt).then_inc(sqrt_done, 1)
            with act.Fori(0, NT // 2) as i:
                for b in range(2):
                    act.wait_ge(turned, i * 2 + (b + 3))
                    act.wait_ge(mm, i * 2 + (b + 1))
                    act.activation(xT[b][:, 3:6, :], T[b][1][:], ACT.Copy).then_inc(ev_a, 1)

        @block.tensor
        def _(pe):
            pe.sem_inc(turned, 2)
            pe.sem_inc(mm, 2)
            pe.wait_ge(w_loaded, 64)

            def turn(t, b):
                pe.wait_ge(xn_ready, t + 1)
                pe.wait_ge(ev_d, t + 1)
                pe.wait_ge(ev_a, t + 1)
                for k in range(KD):
                    last = pe.transpose(T[b][k // 3][:, k % 3, :], xn[b][:, k * 128:(k + 1) * 128], ident[0:P, 0:P])
                last.then_inc(turned, 1)

            def product(t, b):
                pe.wait_ge(ev_d, t + 3)
                pe.wait_ge(ev_a, t + 3)
                pe.wait_ge(lg_done, t + 1)
                for k in range(KD):
                    last = pe.matmul(Y[b][:], xT[b][:, k, :], w[:, k, :], start=(k == 0), stop=(k == KD - 1))
                last.then_inc(mm, 1)

            turn(0, 0)
            with pe.Fori(0, NT // 2 - 1) as i:
                for b in range(2):
                    turn(i * 2 + (b + 1), 1 - b)
                    product(i * 2 + b, b)
            turn(NT - 1, 1)
            product(NT - 2, 0)
            product(NT - 1, 1)


def route_phase(nc, cx, lg, x1, b2, out, ident, codes, posm, ntile, tstart):
    (consts, exp_in, exp_out, sel_ready, counted, comb_ready, turned, copied, mm, summed, b2_loaded, stored) = (
        cx.sem("rt_" + s) for s in
        ("consts", "exp_in", "exp_out", "sel_ready", "counted", "comb_ready", "turned", "copied", "mm", "summed",
         "b2_loaded", "stored"))
    pre, cmp_zero = cx.sem("rt_pre"), cx.sem("rt_cmp_zero")
    dve_step = cx.sem("rt_step")
    TG = NT * NG
    with ExitStack() as st:
        gl = sb(nc, st, "rt_gl", [P, NT, NG])
        el = sb(nc, st, "rt_el", [P, TG, EPG])
        low = sb(nc, st, "rt_low", [P, P])
        ones = sb(nc, st, "rt_ones", [P, P])
        cmp = [sb(nc, st, "rt_cmp0", [P, NT, NG, NG]), sb(nc, st, "rt_cmp1", [P, TG, EPG, EPG])]
        rank = [sb(nc, st, "rt_rank0", [P, NT, NG]), sb(nc, st, "rt_rank1", [P, TG, EPG])]
        sel = [sb(nc, st, "rt_sel0", [P, NT, NG]), sb(nc, st, "rt_sel1", [P, TG, EPG])]
        mx = [sb(nc, st, "rt_mx0", [P, NT]), sb(nc, st, "rt_mx1", [P, TG])]
        gate = [sb(nc, st, "rt_gate0", [P, NT, NG]), sb(nc, st, "rt_gate1", [P, TG, EPG])]
        comb = sb(nc, st, "rt_comb", [P, TG, EPG])
        sele = sb(nc, st, "rt_sele", [P, TG, EPG])
        rest = sb(nc, st, "rt_rest", [P, TG, EPG])
        cum = sb(nc, st, "rt_cum", [P, NT + 1, NE])
        tot = sb(nc, st, "rt_tot", [P, NT, NE])
        ci = sb(nc, st, "rt_ci", [1, NE], I32)
        cf = sb(nc, st, "rt_cf", [1, 2, NE])
        ip = sb(nc, st, "rt_ip", [P, NT, NE], BF16)
        it = sb(nc, st, "rt_it", [P, NT, NE], BF16)
        b2s = sb(nc, st, "rt_b2", [NE, D])
        cT = sb(nc, st, "rt_cT", [NE, NT, P])
        zero = sb(nc, st, "rt_zero", [SLOT, D])
        PW = pb(nc, st, "rt_PW", [P, NT * NE])
        PT = pb(nc, st, "rt_PT", [P, NT * NE])
        T = [pb(nc, st, f"rt_T{j}", [NE, 4, P]) for j in range(3)]
        Y = [pb(nc, st, f"rt_Y{j}", [P, 384]) for j in range(2)]
        width = [4, 4, 2]
        block = st.enter_context(nc.Block())

        @block.sync
        def _(sp):
            sp.dma_start(b2s[:], b2).then_inc(b2_loaded, 16)
            sp.wait_ge(consts, 7)
            sp.dma_start(out[N:N + SLOT, :], zero[:]).then_inc(stored, 16)
            for t in range(NT):
                sp.wait_ge(summed, 2 * t + 2)
                sp.dma_start(out[t * P:(t + 1) * P, :], x1[:, t, :]).then_inc(stored, 16)
            sp.wait_ge(stored, 16 * (NT + 1))

        @block.gpsimd
        def _(pool):
            kw = dict(allow_small_or_imprecise_dtypes=True)
            pool.memset(cmp[0][:], 0.0).then_inc(cmp_zero, 1)
            pool.memset(cmp[1][:], 0.0).then_inc(cmp_zero, 1)
            pool.memset(low[:], 1.0).then_inc(pre, 1)
            pool.wait_ge(pre, 1)
            pool.affine_select(out=low[:], in_=low[:], compare_op=ALU.is_gt, fill=0.0, base=0,
                               pattern=[[1, P]], channel_multiplier=-1).then_inc(consts, 1)
            pool.memset(ones[:], 1.0).then_inc(consts, 1)
            pool.memset(zero[:], 0.0).then_inc(consts, 1)
            pool.iota(ip[:], [[0, NT * NE]], base=0, channel_multiplier=1, **kw).then_inc(consts, 1)
            pool.iota(it[:], [[1, NT], [0, NE]], base=0, channel_multiplier=0, **kw).then_inc(consts, 1)
            pool.memset(codes[:, :, :, 2:3], 1.0).then_inc(consts, 1)
            pool.memset(cum[:, 0, :], 0.0).then_inc(consts, 1)

        @block.vector
        def _(dve):
            step = Chain(dve, dve_step)
            step(dve.tensor_copy(gl[:], lg[:, :, 0:NG]))
            step(dve.tensor_copy(el[:].rearrange("p (t g) e -> p t (g e)", g=NG), lg[:, :, NG:NG + NE]))
            dve.wait_ge(cmp_zero, 2)
            for s, (l, a, n) in enumerate(((gl, NT, NG), (el, TG, EPG))):
                for i in range(n):
                    mine = lambda w: l[:, :, i:i + 1].to_broadcast([P, a, w])
                    if i > 0:
                        last = dve.tensor_tensor(cmp[s][:, :, i, 0:i], l[:, :, 0:i], mine(i), ALU.is_ge)
                    if i < n - 1:
                        last = dve.tensor_tensor(cmp[s][:, :, i, i + 1:n], l[:, :, i + 1:n], mine(n - 1 - i),
                                                 ALU.is_gt)
                step(last)
                step(dve.tensor_reduce(rank[s][:], cmp[s][:], AX.X, ALU.add))
                step(dve.tensor_scalar(sel[s][:], rank[s][:], 2.0, None, ALU.is_lt))
                step(dve.tensor_reduce(mx[s][:], l[:], AX.X, ALU.max))
                dve.tensor_tensor(gate[s][:], l[:], mx[s][:].unsqueeze(2).to_broadcast([P, a, n]),
                                  ALU.subtract).then_inc(exp_in, 1)
                dve.wait_ge(exp_out, s + 1)
                step(dve.tensor_tensor(gate[s][:], gate[s][:], sel[s][:], ALU.mult))
                step(dve.tensor_reduce(mx[s][:], gate[s][:], AX.X, ALU.add))
                step(dve.reciprocal(mx[s][:], mx[s][:]))
                step(dve.tensor_tensor(gate[s][:], gate[s][:], mx[s][:].unsqueeze(2).to_broadcast([P, a, n]),
                                       ALU.mult))
            g4 = lambda a: a[:].rearrange("p t g -> p (t g)").unsqueeze(2).to_broadcast([P, TG, EPG])
            dve.tensor_tensor(sele[:], sel[1][:], g4(sel[0]), ALU.mult).then_inc(sel_ready, 1)
            dve.tensor_tensor(comb[:], gate[1][:], g4(gate[0]), ALU.mult).then_inc(comb_ready, 1)
            dve.wait_ge(comb_ready, 1)
            c3 = lambda j: codes[:, :, :, j]
            combf = comb[:].rearrange("p (t g) e -> p t (g e)", g=NG)
            restf = rest[:].rearrange("p (t g) e -> p t (g e)", g=NG)
            dve.wait_ge(consts, 7)
            step(dve.tensor_copy(c3(3), combf))
            step(dve.tensor_tensor(restf, combf, c3(3), ALU.subtract))
            step(dve.tensor_copy(c3(4), restf))
            step(dve.tensor_tensor(c3(5), restf, c3(4), ALU.subtract))
            step(dve.tensor_copy(c3(0), ip[:]))
            step(dve.tensor_copy(c3(1), it[:]))
            for j in range(3):
                dve.wait_ge(turned, j + 1)
                dve.tensor_copy(cT[:, 4 * j:4 * j + width[j], :], T[j][:, 0:width[j], :]).then_inc(copied, 1)
            dve.wait_ge(counted, 2)
            step(dve.tensor_copy(tot[:].rearrange("p t e -> p (t e)"), PT[:]))
            for t in range(NT):
                step(dve.tensor_tensor(cum[:, t + 1, :], cum[:, t, :], tot[:, t, :], ALU.add))
            step(dve.tensor_tensor(posm[:].rearrange("p t e -> p (t e)"), PW[:],
                                   cum[:, 0:NT, :].rearrange("p t e -> p (t e)"), ALU.add))
            selef = sele[:].rearrange("p (t g) e -> p t (g e)", g=NG)
            step(dve.tensor_scalar(posm[:], posm[:], 1.0, None, ALU.add))
            step(dve.tensor_tensor(posm[:], posm[:], selef, ALU.mult))
            step(dve.tensor_scalar(posm[:], posm[:], -1.0, None, ALU.add))
            step(dve.tensor_scalar(cf[:, 0, :], cum[0:1, NT, :], float(SLOT - 1), None, ALU.add))
            step(dve.tensor_copy(ci[:], cf[:, 0, :]))
            step(dve.tensor_scalar(ci[:], ci[:], SLOT.bit_length() - 1, None, ALU.logical_shift_right))
            step(dve.tensor_copy(cf[:, 0, :], ci[:]))
            step(dve.tensor_scalar(cf[:, 0, :], cf[:, 0, :], 1.0, None, ALU.max))
            step(dve.tensor_copy(ntile[:], cf[:, 0, :]))
            step(dve.tensor_tensor_scan(cf[:, 1, :], ones[0:1, 0:NE], cf[:, 0, :], 0.0, ALU.mult, ALU.add))
            step(dve.tensor_tensor(cf[:, 1, :], cf[:, 1, :], cf[:, 0, :], ALU.subtract))
            step(dve.tensor_copy(tstart[:], cf[:, 1, :]))
            for t in range(NT):
                for j in range(2):
                    col = x1[:, t, j * 384:(j + 1) * 384]
                    dve.wait_ge(mm, 2 * t + j + 1)
                    dve.tensor_tensor(col, Y[j][:], col, ALU.add).then_inc(summed, 1)

        @block.scalar
        def _(act):
            for s in range(2):
                act.wait_ge(exp_in, s + 1)
                act.activation(gate[s][:], gate[s][:], ACT.Exp).then_inc(exp_out, 1)

        @block.tensor
        def _(pe):
            pe.wait_ge(sel_ready, 1)
            pe.wait_ge(consts, 7)
            rhs = sele[:].rearrange("p a e -> p (a e)")
            pe.matmul(PW[:], low[:], rhs, start=True, stop=True).then_inc(counted, 1)
            pe.matmul(PT[:], ones[:], rhs, start=True, stop=True).then_inc(counted, 1)
            pe.wait_ge(comb_ready, 1)
            pe.wait_ge(b2_loaded, 16)
            for j in range(3):
                for t in range(width[j]):
                    tt = 4 * j + t
                    last = pe.transpose(T[j][:, t, :], comb[:, tt * NG:(tt + 1) * NG, :].rearrange("p a e -> p (a e)"),
                                        ident[0:P, 0:P])
                last.then_inc(turned, 1)
            pe.wait_ge(copied, 3)
            for t in range(NT):
                for j in range(2):
                    if t >= 1:
                        pe.wait_ge(summed, 2 * (t - 1) + j + 1)
                    pe.matmul(Y[j][:], cT[:, t, :], b2s[:, j * 384:(j + 1) * 384], start=True, stop=True
                              ).then_inc(mm, 1)


def load_expert_first(eng, W1, weights, w_loaded, e, b):
    eng.dma_start(weights[0][:, b, :, :], W1[e, :, :].rearrange("o (k p) n -> p (o k) n", p=128)
                  ).then_inc(w_loaded[b], 16)


def load_expert_second(eng, b1, W2, weights, w_loaded, e, b):
    _, w2, b1r = weights
    eng.dma_start(b1r[:, b, :], b1[e, :].partition_broadcast(SLOT)).then_inc(w_loaded[b], 16)
    eng.dma_start(w2[:, b, :, :], W2[e, :, :].rearrange("o (k p) n -> p (o k) n", p=128)).then_inc(w_loaded[b], 16)


def expert_phase(nc, cx, W1, b1, W2, weights, w_loaded, xn2_dram, out, ident, codes, posm, ntile, tstart):
    (consts, q_ready, ids_done, idx_ready, gathered, x_turned, xT_d, xT_a, gemm1, h_biased, h_gelu, h_turned,
     hT_ready, gemm2, y_d, y_a, added, flat, g_ready, x_half) = (
        cx.sem("ex_" + s) for s in
        ("consts", "q_ready", "ids_done", "idx_ready", "gathered", "x_turned", "xT_d", "xT_a", "gemm1", "h_biased",
         "h_gelu", "h_turned", "hT_ready", "gemm2", "y_d", "y_a", "added", "flat", "g_ready", "x_half"))
    passed, half_passed = cx.sem("ex_passed"), cx.sem("ex_half_passed")
    dve_step = cx.sem("ex_step")
    w1, w2, b1r = weights
    STEPS = 8
    CONSTS = 13
    with ExitStack() as st:
        iot = sb(nc, st, "ex_iota", [P, SLOT])
        pad = sb(nc, st, "ex_pad", [SLOT, 1])
        rel = sb(nc, st, "ex_rel", [P, NT])
        Q = sb(nc, st, "ex_Q", [P, NT, SLOT], BF16)
        cod = sb(nc, st, "ex_cod", [SLOT, 6])
        idf = sb(nc, st, "ex_idf", [SLOT, 2])
        found, waiting, leaving = (sb(nc, st, "ex_" + s, [SLOT, 2]) for s in ("found", "waiting", "leaving"))
        idG = sb(nc, st, "ex_idG", [SLOT, 1], I32)
        idS = sb(nc, st, "ex_idS", [SLOT, 1], I32)
        gS = sb(nc, st, "ex_gS", [SLOT, 1])
        X = sb(nc, st, "ex_X", [SLOT, D])
        xT = sb(nc, st, "ex_xT", [128, KD, SLOT])
        h = sb(nc, st, "ex_h", [SLOT, FM])
        hT = sb(nc, st, "ex_hT", [128, KM, SLOT])
        y = sb(nc, st, "ex_y", [SLOT, D])
        PI = pb(nc, st, "ex_PI", [SLOT, 6])
        TX = [pb(nc, st, f"ex_TX{j}", [128, 3, SLOT]) for j in range(2)]
        PH = pb(nc, st, "ex_PH", [SLOT, FM])
        TH = pb(nc, st, "ex_TH", [128, KM, SLOT])
        PY = [pb(nc, st, f"ex_PY{j}", [SLOT, 384]) for j in range(2)]
        block = st.enter_context(nc.Block())

        def turns(eng, turn, body, enter=None):
            eng.reg_mov(turn, 1)
            with eng.Fori(0, NE // NB) as i:
                for b in range(NB):
                    if enter is not None:
                        enter(i, b)
                    count = eng.value_load(ntile[0:1, bass.ds(i * NB + b, 1)], min_val=1, max_val=NT)
                    with eng.Fori(0, count) as _:
                        body(eng.snap(turn), b)
                        eng.reg_add(turn, turn, 1)
            return eng.snap(turn)

        @block.sync
        def _(sp):
            with sp.Fori(1, NE // NB) as i:
                for b in range(NB):
                    done = sp.value_load(tstart[0:1, bass.ds(i * NB + (b + 1 - NB), 1)], min_val=0, max_val=MAXT)
                    sp.wait_ge(gemm1, done + 2)
                    load_expert_first(sp, W1, weights, w_loaded, bass.ds(i * NB + b, 1), b)
                    sp.wait_ge(gemm2, done + 3)
                    load_expert_second(sp, b1, W2, weights, w_loaded, bass.ds(i * NB + b, 1), b)

        @block.gpsimd
        def _(pool):
            kw = dict(allow_small_or_imprecise_dtypes=True)
            pool.iota(iot[:], [[1, SLOT]], base=0, channel_multiplier=0, **kw).then_inc(consts, 1)
            pool.iota(pad[:], [[0, 1]], base=N, channel_multiplier=1, **kw).then_inc(consts, 1)
            for m in (found, waiting, leaving):
                pool.iota(m[:, 0:1], [[0, 1]], base=N, channel_multiplier=1, **kw).then_inc(consts, 1)
                pool.memset(m[:, 1:2], 0.0).then_inc(consts, 1)
            for ids in (idG, idS):
                pool.iota(ids[:], [[0, 1]], base=N, channel_multiplier=1).then_inc(consts, 1)
            pool.memset(y[:], 0.0).then_inc(consts, 1)
            pool.memset(h[:], 0.0).then_inc(consts, 1)
            pool.memset(hT[:], 0.0).then_inc(consts, 1)
            pool.wait_ge(consts, CONSTS)

            def gather():
                pool.indirect_dma_start(X[:], None, xn2_dram, bass.IndirectOffsetOnAxis(ap=idG[:, 0:1], axis=0)
                                        ).then_inc(gathered, 16)

            def scatter(n):
                if n is not None:
                    pool.wait_ge(y_d, n)
                    pool.wait_ge(y_a, n)
                    pool.sem_inc(passed, 1)
                pool.indirect_dma_start(out, bass.IndirectOffsetOnAxis(ap=idS[:, 0:1], axis=0), y[:], None,
                                        compute_op=ALU.add).then_inc(added, 16)

            def body(n, b):
                scatter(n)
                pool.wait_ge(idx_ready, n + 1)
                pool.wait_ge(x_turned, n)
                pool.sem_inc(passed, 1)
                gather()

            gather()
            scatter(None)
            with pool.register("ex_turn_pool") as turn:
                end = turns(pool, turn, body)
                for k in range(3):
                    scatter(end + k)
                pool.wait_ge(added, (end + 3) * 16)

        @block.vector
        def _(dve):
            def steps(n):
                state = [0]

                def step(ins):
                    state[0] += 1
                    ins.then_inc(dve_step, 1)
                    dve.wait_ge(dve_step, n * STEPS + (state[0] - STEPS))
                return step, state

            def turn_x(n):
                dve.wait_ge(x_half, n)
                dve.wait_ge(gemm1, n)
                dve.tensor_copy(xT[:, 0:3, :], TX[0][:]).then_inc(xT_d, 1)

            def find(step, n):
                dve.wait_ge(ids_done, n + 1)
                step(dve.tensor_copy(cod[:], PI[:]))
                step(dve.tensor_copy(waiting[:], found[:]))
                step(dve.scalar_tensor_tensor(idf[:, 0:1], cod[:, 1:2], float(P), cod[:, 0:1], ALU.mult, ALU.add))
                step(dve.scalar_tensor_tensor(idf[:, 1:2], cod[:, 2:3], -1.0, pad[:], ALU.add, ALU.mult))
                step(dve.scalar_tensor_tensor(found[:, 1:2], cod[:, 5:6], cod[:, 4:5], cod[:, 3:4], ALU.add, ALU.add))
                step(dve.tensor_tensor(found[:, 0:1], idf[:, 0:1], idf[:, 1:2], ALU.subtract))
                dve.wait_ge(gathered, n * 16)
                dve.tensor_copy(idG[:], found[:, 0:1]).then_inc(idx_ready, 1)

            def second(n, step=None, then=None):
                dve.wait_ge(added, n * 16)
                dve.tensor_copy(idS[:], leaving[:, 0:1])
                dve.tensor_copy(gS[:], leaving[:, 1:2]).then_inc(g_ready, 1)
                dve.wait_ge(g_ready, n)
                if then is not None:
                    step(dve.tensor_copy(leaving[:], then[:]))
                dve.wait_ge(gemm2, n)
                dve.tensor_scalar(y[:, 0:384], PY[0][:], gS[:], None, ALU.mult).then_inc(y_d, 1)

            def bias(n, b_prev):
                dve.wait_ge(gemm1, n + 1)
                dve.wait_ge(h_turned, n)
                dve.tensor_tensor(h[:].unsqueeze(1), PH[:].unsqueeze(1), b1r[:, bass.ds(b_prev, 1), :], ALU.add
                                  ).then_inc(h_biased, 1)

            dve.wait_ge(consts, CONSTS)
            for made in (idx_ready, xT_d, h_biased):
                dve.sem_inc(made, 1)
            with dve.register("ex_b_prev") as b_prev, dve.register("ex_turn_dve") as turn:
                dve.reg_mov(b_prev, 0)

                def enter(i, b):
                    dve.wait_ge(w_loaded[b], i * 48 + 48)
                    dve.tensor_copy(rel[:], posm[:, :, bass.ds(i * NB + b, 1)].rearrange("p t o -> p (t o)")
                                    ).then_inc(flat, 1)
                    dve.wait_ge(flat, i * NB + (b + 1))

                def body(n, b):
                    step, state = steps(n)
                    dve.wait_ge(ids_done, n)
                    dve.tensor_tensor(Q[:], rel[:].unsqueeze(2).to_broadcast([P, NT, SLOT]),
                                      iot[:].unsqueeze(1).to_broadcast([P, NT, SLOT]), ALU.is_equal
                                      ).then_inc(q_ready, 1)
                    second(n, step, waiting)
                    turn_x(n)
                    dve.wait_ge(q_ready, n)
                    step(dve.tensor_scalar(rel[:], rel[:], -float(SLOT), None, ALU.add))
                    find(step, n)
                    bias(n, dve.snap(b_prev))
                    assert state[0] == STEPS
                    dve.reg_mov(b_prev, b)

                end = turns(dve, turn, body, enter)
                last = dve.snap(b_prev)
                step, state = steps(end)
                second(end, step, waiting)
                turn_x(end)
                bias(end, last)
                second(end + 1, step, found)
                second(end + 2)

        @block.scalar
        def _(act):
            def turn_x(n):
                act.wait_ge(x_turned, n)
                act.wait_ge(gemm1, n)
                act.activation(xT[:, 3:6, :], TX[1][:], ACT.Copy).then_inc(xT_a, 1)

            def second(n):
                act.wait_ge(gemm2, n)
                act.wait_ge(g_ready, n)
                act.activation(y[:, 384:768], PY[1][:], ACT.Copy, scale=gS[:]).then_inc(y_a, 1)

            def turn_h(n):
                act.wait_ge(h_turned, n)
                act.wait_ge(gemm2, n)
                act.activation(hT[:], TH[:], ACT.Copy).then_inc(hT_ready, 1)

            def gelu(n):
                act.wait_ge(h_biased, n + 1)
                act.activation(h[:], h[:], ACT.Gelu).then_inc(h_gelu, 1)

            act.wait_ge(consts, CONSTS)
            for made in (xT_a, h_gelu, hT_ready):
                act.sem_inc(made, 1)

            def body(n, b):
                second(n)
                turn_x(n)
                turn_h(n)
                gelu(n)

            with act.register("ex_turn_act") as turn:
                end = turns(act, turn, body)
                body(end, None)
                second(end + 1)
                turn_h(end + 1)
                second(end + 2)

        @block.tensor
        def _(pe):
            pe.wait_ge(consts, CONSTS)

            def find(n, e):
                pe.wait_ge(q_ready, n)
                pe.wait_ge(idx_ready, n)
                for t in range(NT):
                    last = pe.matmul(PI[:], Q[:, t, :], codes[:, t, bass.ds(e, 1), :].rearrange("p o c -> p (o c)"),
                                     start=(t == 0), stop=(t == NT - 1))
                last.then_inc(ids_done, 1)

            def turn_x(n):
                pe.wait_ge(gathered, n * 16)
                pe.wait_ge(xT_d, n)
                pe.wait_ge(xT_a, n)
                for half, turned in enumerate((x_half, x_turned)):
                    for k in range(3):
                        col = (3 * half + k) * 128
                        last = pe.transpose(TX[half][:, k, :], X[:, col:col + 128], ident[:])
                    last.then_inc(turned, 1)

            def turn_h(n):
                pe.wait_ge(h_gelu, n)
                pe.wait_ge(hT_ready, n)
                for k in range(KM):
                    last = pe.transpose(TH[:, k, :], h[:, k * 128:(k + 1) * 128], ident[:])
                last.then_inc(h_turned, 1)

            def second(n, b):
                if n is not None:
                    pe.wait_ge(hT_ready, n + 1)
                    pe.wait_ge(y_d, n)
                    pe.wait_ge(y_a, n)
                for j in range(2):
                    for k in range(KM):
                        last = pe.matmul(PY[j][:], hT[:, k, :], w2[:, bass.ds(b, 1), k, j * 384:(j + 1) * 384],
                                         start=(k == 0), stop=(k == KM - 1))
                last.then_inc(gemm2, 1)

            def first(n, b):
                pe.wait_ge(xT_d, n + 1)
                pe.wait_ge(h_biased, n)
                for k in range(KD):
                    if k == 3:
                        pe.wait_ge(xT_a, n + 1)
                        pe.sem_inc(half_passed, 1)
                    last = pe.matmul(PH[:], xT[:, k, :], w1[:, bass.ds(b, 1), k, :], start=(k == 0),
                                     stop=(k == KD - 1))
                last.then_inc(gemm1, 1)

            pe.sem_inc(ids_done, 1)
            pe.sem_inc(gemm1, 1)
            with pe.register("ex_b1_prev") as b1_prev, pe.register("ex_b2_prev") as b2_prev, \
                    pe.register("ex_turn_pe") as turn:
                pe.reg_mov(b1_prev, 0)
                pe.reg_mov(b2_prev, 0)
                expert = [None]
                pe.wait_ge(w_loaded[0], 48)
                second(None, 0)

                def enter(i, b):
                    pe.wait_ge(w_loaded[b], i * 48 + 48)
                    expert[0] = i * NB + b

                def body(n, b):
                    turn_x(n)
                    turn_h(n)
                    find(n, expert[0])
                    first(n, pe.snap(b1_prev))
                    second(n, pe.snap(b2_prev))
                    pe.reg_mov(b2_prev, pe.snap(b1_prev))
                    pe.reg_mov(b1_prev, b)

                end = turns(pe, turn, body, enter)
                turn_x(end)
                turn_h(end)
                first(end, pe.snap(b1_prev))
                second(end, pe.snap(b2_prev))
                turn_h(end + 1)
                second(end + 1, pe.snap(b1_prev))


def host_layout(i):
    import numpy as np
    o = dict(i)
    for name in ("L0_mix_qkv_w", "L0_mix_proj_w", "L0_mix_rf"):
        o[name] = np.ascontiguousarray(np.asarray(i[name]).T)
    o["L0_ffn_Wge"] = np.asarray(i["L0_ffn_Wge"]).transpose(1, 0, 2).reshape(D, NE)
    return {k: np.ascontiguousarray(v) for k, v in o.items()}


def build(nc, ins, out):
    x = ins["x"]
    dram = lambda name, *shape: nc.dram_tensor(name, shape, F32).ap()
    with ExitStack() as st:
        cx = Ctx(nc)
        x1_dram = dram("x1_dram", N, D)
        alT_dram = dram("alT_dram", 2 * H1, N)
        mT_dram = dram("mT_dram", H1, N)
        al2T_dram = dram("al2T_dram", 2, N)
        m2T_dram = dram("m2T_dram", 1, N)
        ct_dram = dram("ct_dram", NW * 128, SLO)
        c_dram = dram("c_dram", NT, P, N)
        mask_dram = dram("mask_dram", NT, P, N)
        h1T_dram = dram("h1T_dram", NT, 128, KF * P)
        ident = sb(nc, st, "ident", [128, 128])
        with ExitStack() as st1:
            xnT = sb(nc, st1, "xnT", [128, KD, N])
            wa = sb(nc, st1, "gnn_wa", [128, KD, 2 * H1])
            attn_scope = ExitStack()
            attn = sb(nc, attn_scope, "attn", [P, NT, D])
            w_proj = sb(nc, attn_scope, "proj_w", [128, KD, D])
            proj_loaded = cx.sem("proj_w_loaded")
            with ExitStack() as st2:
                w_qkv = sb(nc, st2, "mix_w", [128, KD, 3, D // 2])
                b_qkv = sb(nc, st2, "mix_brow", [P, 3, D // 2])
                mix_loaded = cx.sem("mix_w_loaded")

                def load_half(half):
                    return lambda sp: load_mix_weights(sp, half, ins["L0_mix_qkv_w"], ins["L0_mix_qkv_b"], w_qkv,
                                                       b_qkv, mix_loaded)

                def load_proj(sp):
                    sp.dma_start(w_proj[:], ins["L0_mix_proj_w"].rearrange("(k p) n -> p k n", p=128)
                                 ).then_inc(proj_loaded, 16)

                norm_phase(nc, cx, x, ident, xnT, load_half(0))
                for half in range(2):
                    mix_half_phase(nc, cx, half, ins["L0_mix_rf"], xnT, ident, w_qkv, b_qkv, mix_loaded, attn,
                                   ins["L0_gnn_W1"], ins["L0_gnn_att_src1"], ins["L0_gnn_att_dst1"], wa,
                                   load_half(1) if half == 0 else load_proj)
            proj_phase(nc, cx, attn, w_proj, proj_loaded, ins["L0_mix_proj_b"], ins["L0_gnn_b2"], x, x1_dram, ident)
            attn_scope.close()
            al = sb(nc, st1, "al", [P, NT, 2 * H1])
            h = sb(nc, st1, "h", [P, NT, H1, C1 + 1])
            with ExitStack() as st2:
                w1 = sb(nc, st2, "gnn_w1", [128, KD, F1])
                w1_loaded = [cx.sem(f"w1_loaded{j}") for j in range(2)]
                keyT = sb(nc, st2, "keyT", [128, EROWS])
                sloT = sb(nc, st2, "sloT", [128, EROWS])
                spans = sb(nc, st2, "spans", [1, 2 * NW], I32)
                with ExitStack() as st3:
                    block = st3.enter_context(nc.Block())
                    logits(nc, cx, st3, block, ins["L0_gnn_W1"], xnT, ident, wa, w1, al, alT_dram, w1_loaded)
                    edge_table(nc, cx, st3, block, ins["src"], ins["dst"], ident, keyT, sloT, spans)
                count_phase(nc, cx, keyT, sloT, spans, ct_dram, xnT, ins["L0_gnn_W1"], w1, w1_loaded, h)
            mask_phase(nc, cx, ct_dram, c_dram, mask_dram, alT_dram, ident, al, mT_dram)
            cx.clear()
            gat1_phase(nc, cx, ins["L0_gnn_b1"], h, al, alT_dram, mT_dram, c_dram, h1T_dram, ident)
        x1 = sb(nc, st, "x1", [P, NT, D])
        x1_loaded = cx.sem("x1_loaded")
        stats = sb(nc, st, "x1_stats", [P, NT, 2, 6])
        with ExitStack() as st1:
            h2 = sb(nc, st1, "h2", [P, NT, D + 1])
            al2 = sb(nc, st1, "al2", [P, NT, 2])
            rows_t = sb(nc, st1, "gat2_rows_t", [P, N])
            rows_loaded = cx.sem("gat2_rows_loaded")
            gat2_project_phase(nc, cx, ins["L0_gnn_W2"], ins["L0_gnn_att_src2"], ins["L0_gnn_att_dst2"], h1T_dram,
                               mask_dram, ident, h2, al2, al2T_dram, m2T_dram, x1_dram, x1, x1_loaded, rows_t,
                               rows_loaded)
            gat2_phase(nc, cx, al2, m2T_dram, c_dram, h2, x1, x1_loaded, rows_t, rows_loaded, stats)
        xn2_dram = dram("xn2_dram", N + SLOT, D)
        codes = sb(nc, st, "codes", [P, NT, NE, 6], BF16)
        posm = sb(nc, st, "posm", [P, NT, NE])
        ntile = sb(nc, st, "ntile", [1, NE], I32)
        tstart = sb(nc, st, "tstart", [1, NE], I32)
        lg = sb(nc, st, "lg", [P, NT, NG + NE])
        weights = (sb(nc, st, "ex_w1", [128, NB, KD, FM]), sb(nc, st, "ex_w2", [128, NB, KM, D]),
                   sb(nc, st, "ex_b1", [SLOT, NB, FM]))
        ex_loaded = [cx.sem(f"ex_w_loaded{b}") for b in range(NB)]

        def load_experts(eng):
            for b in range(NB):
                load_expert_first(eng, ins["L0_ffn_W1"], weights, ex_loaded, slice(b, b + 1), b)
                load_expert_second(eng, ins["L0_ffn_b1"], ins["L0_ffn_W2"], weights, ex_loaded, slice(b, b + 1), b)

        route_norm_phase(nc, cx, load_experts, x1, stats, ins["L0_ffn_Wg"], ins["L0_ffn_Wge"], ins["L0_ffn_bg"],
                         ins["L0_ffn_bge"], xn2_dram, ident, lg)
        route_phase(nc, cx, lg, x1, ins["L0_ffn_b2"], out, ident, codes, posm, ntile, tstart)
        expert_phase(nc, cx, ins["L0_ffn_W1"], ins["L0_ffn_b1"], ins["L0_ffn_W2"], weights,
                     ex_loaded, xn2_dram, out, ident, codes, posm,
                     ntile, tstart)


def kernel(**inputs):
    import concourse.bacc as bacc
    from concourse.bass_utils import run_bass_kernel_spmd

    nc = bacc.Bacc("TRN2", target_bir_lowering=False, num_devices=1)
    arrays = host_layout(inputs)
    ins = {k: nc.dram_tensor(f"in_{k}", a.shape, mybir.dt.from_np(a.dtype), kind="ExternalInput").ap()
           for k, a in arrays.items()}
    out = nc.dram_tensor("out_rows", (N + SLOT, D), F32, kind="ExternalOutput").ap()
    build(nc, ins, out)
    r = run_bass_kernel_spmd(nc, [{f"in_{k}": a for k, a in arrays.items()}], core_ids=[0])
    return r.results[0]["out_rows"][0:N]
```
